# Optimizing a Trainium2 kernel written in Bass

```python
import numpy as np
import jax
import jax.numpy as jnp

def _softmax(x, axis=-1):
    return jax.nn.softmax(x, axis=axis)

def _gelu(x):
    return jax.nn.gelu(x, approximate=True)

def _silu(x):
    return jax.nn.silu(x)

def _sigmoid(x):
    return jax.nn.sigmoid(x)

def _layernorm(x, axis=-1, eps=1e-05):
    m = jnp.mean(x, axis=axis, keepdims=True)
    v = jnp.var(x, axis=axis, keepdims=True)
    return (x - m) / jnp.sqrt(v + eps)

def _scatter_add(tgt, idx, src, axis=0):
    return tgt.at[idx].add(src)

def _segment_sum(src, seg, n):
    return jax.ops.segment_sum(src, seg, n)
kernel_name = 'mk_vit_tower_d1_tok_img1024_r4_a5fa00'

def setup_inputs(seed: int=0):
    np.random.seed(seed)
    _w = jnp.asarray

    def _rec_inputs():
        import jax
        import jax.numpy as jnp
        _rk = jax.random.key(seed)
        x = -0.00016672 + 0.999947 * jax.random.normal(jax.random.fold_in(_rk, 1), (32, 3, 96, 96), jnp.float32)
        return x
    x = _rec_inputs()

    def _L0_tok_setup():
        import jax, jax.numpy as jnp
        import numpy as np
        IMAGE_SIZE = 96
        PATCH = 16
        N_EMBD = 256
        C = 3
        N_PATCHES = (IMAGE_SIZE // PATCH) ** 2
        PATCH_DIM = C * PATCH * PATCH
        key = jax.random.key(seed)
        kx, kw, kb, kp = jax.random.split(key, 4)
        B = 64
        x = jax.random.normal(kx, (B, C, IMAGE_SIZE, IMAGE_SIZE), dtype=jnp.float32)
        bound = 1.0 / np.sqrt(PATCH_DIM)
        W = jax.random.uniform(kw, (N_EMBD, PATCH_DIM), minval=-bound, maxval=bound, dtype=jnp.float32)
        b = jax.random.uniform(kb, (N_EMBD,), minval=-bound, maxval=bound, dtype=jnp.float32)
        pos_embd = jax.random.normal(kp, (1, N_PATCHES, N_EMBD), dtype=jnp.float32) * 0.02
        return {'x': x, 'W': W, 'b': b, 'pos_embd': pos_embd}
    _L0_tok_all = _L0_tok_setup()
    _L0_tok_in = {k: v for k, v in _L0_tok_all.items() if k in ('W', 'b', 'pos_embd')}
    del _L0_tok_all

    def _L0_attn_setup():
        import math
        import jax, jax.numpy as jnp
        import numpy as np
        N_HEADS = 16
        N_KV_HEADS = 4
        HEAD_DIM = 64
        DIM = 256
        WINDOW = 16
        EPS = 0.01

        def _alibi_slopes(n_heads):
            closest = 2 ** math.floor(math.log2(n_heads))
            base = 2.0 ** (-2.0 ** (-(math.log2(closest) - 3)))
            slopes = base ** np.arange(1, closest + 1, dtype=np.float32)
            if closest < n_heads:
                eb = 2.0 ** (-2.0 ** (-(math.log2(2 * closest) - 3)))
                extra = eb ** np.arange(1, 2 * (n_heads - closest) + 1, 2, dtype=np.float32)
                slopes = np.concatenate([slopes, extra])
            return jnp.asarray(slopes[:n_heads])

        def _rmsnorm(x, w):
            xf = x.astype(jnp.float32)
            norm = jax.lax.rsqrt(jnp.mean(xf * xf, axis=-1, keepdims=True) + EPS)
            return (xf * norm).astype(x.dtype) * w
        key = jax.random.key(seed)
        ks = jax.random.split(key, 6)
        B, L = (2, 512)
        s = 1.0 / math.sqrt(DIM)
        return {'x': jax.random.normal(ks[0], (B, L, DIM), jnp.float32), 'wq': jax.random.normal(ks[1], (N_HEADS * HEAD_DIM, DIM), jnp.float32) * s, 'wk': jax.random.normal(ks[2], (N_KV_HEADS * HEAD_DIM, DIM), jnp.float32) * s, 'wv': jax.random.normal(ks[3], (N_KV_HEADS * HEAD_DIM, DIM), jnp.float32) * s, 'wo': jax.random.normal(ks[4], (DIM, N_HEADS * HEAD_DIM), jnp.float32) * s, 'q_norm_w': jnp.ones((HEAD_DIM,), jnp.float32), 'k_norm_w': jnp.ones((HEAD_DIM,), jnp.float32)}
    _L0_attn_all = _L0_attn_setup()
    _L0_attn_in = {k: v for k, v in _L0_attn_all.items() if k in ('wq', 'wk', 'wv', 'wo', 'q_norm_w', 'k_norm_w')}
    del _L0_attn_all

    def _L0_ffn_setup():
        import jax, jax.numpy as jnp
        import numpy as np
        H = 8
        KD = 128
        TOPK = 8
        NUM_KEYS = 64
        N_EXPERTS = NUM_KEYS * NUM_KEYS
        N_DIM = 256
        BN_EPS = 1e-05

        def gelu_new(x):
            c = jnp.sqrt(jnp.asarray(2.0 / jnp.pi, x.dtype))
            return 0.5 * x * (1.0 + jnp.tanh(c * (x + 0.044715 * x * x * x)))
        key = jax.random.key(seed)
        ks = jax.random.split(key, 5)
        b, s = (2, 256)
        x = jax.random.normal(ks[0], (b, s, N_DIM), dtype=jnp.float32)
        w_q = jax.random.normal(ks[1], (N_DIM, 2 * H * KD), dtype=jnp.float32) * 0.02
        bn_gamma = jnp.ones((2 * H * KD,), dtype=jnp.float32)
        bn_beta = jnp.zeros((2 * H * KD,), dtype=jnp.float32)
        keys = jax.random.normal(ks[2], (H, NUM_KEYS, 2, KD), dtype=jnp.float32) * 0.02
        down_embed = jax.random.normal(ks[3], (N_EXPERTS, N_DIM), dtype=jnp.float32) * 0.02
        up_embed = jax.random.normal(ks[4], (N_EXPERTS, N_DIM), dtype=jnp.float32) * 0.02
        return {'x': x, 'w_q': w_q, 'bn_gamma': bn_gamma, 'bn_beta': bn_beta, 'keys': keys, 'down_embed': down_embed, 'up_embed': up_embed}
    _L0_ffn_all = _L0_ffn_setup()
    _L0_ffn_in = {k: v for k, v in _L0_ffn_all.items() if k in ('w_q', 'bn_gamma', 'bn_beta', 'keys', 'down_embed', 'up_embed')}
    del _L0_ffn_all
    return {'x': x, 'L0_tok_W': _L0_tok_in['W'], 'L0_tok_b': _L0_tok_in['b'], 'L0_tok_pos_embd': _L0_tok_in['pos_embd'], 'L0_attn_wq': _L0_attn_in['wq'], 'L0_attn_wk': _L0_attn_in['wk'], 'L0_attn_wv': _L0_attn_in['wv'], 'L0_attn_wo': _L0_attn_in['wo'], 'L0_attn_q_norm_w': _L0_attn_in['q_norm_w'], 'L0_attn_k_norm_w': _L0_attn_in['k_norm_w'], 'L0_ffn_w_q': _L0_ffn_in['w_q'], 'L0_ffn_bn_gamma': _L0_ffn_in['bn_gamma'], 'L0_ffn_bn_beta': _L0_ffn_in['bn_beta'], 'L0_ffn_keys': _L0_ffn_in['keys'], 'L0_ffn_down_embed': _L0_ffn_in['down_embed'], 'L0_ffn_up_embed': _L0_ffn_in['up_embed']}

def reference(x, L0_tok_W, L0_tok_b, L0_tok_pos_embd, L0_attn_wq, L0_attn_wk, L0_attn_wv, L0_attn_wo, L0_attn_q_norm_w, L0_attn_k_norm_w, L0_ffn_w_q, L0_ffn_bn_gamma, L0_ffn_bn_beta, L0_ffn_keys, L0_ffn_down_embed, L0_ffn_up_embed):
    import jax
    import jax.numpy as jnp

    def _L0_tok_ref(x, W, b, pos_embd):
        import jax, jax.numpy as jnp
        import numpy as np
        IMAGE_SIZE = 96
        PATCH = 16
        N_EMBD = 256
        C = 3
        N_PATCHES = (IMAGE_SIZE // PATCH) ** 2
        PATCH_DIM = C * PATCH * PATCH
        B, Cc, H, Wd = x.shape
        p = PATCH
        Hp, Wp = (H // p, Wd // p)
        patches = x.reshape(B, Cc, Hp, p, Wp, p)
        patches = patches.transpose(0, 2, 4, 1, 3, 5)
        patches = patches.reshape(B, Hp * Wp, Cc * p * p)
        out = jnp.einsum('bnd,ed->bne', patches, W) + b + pos_embd
        return out

    def _L0_attn_ref(x, wq, wk, wv, wo, q_norm_w, k_norm_w):
        import math
        import jax, jax.numpy as jnp
        import numpy as np
        N_HEADS = 16
        N_KV_HEADS = 4
        HEAD_DIM = 64
        DIM = 256
        WINDOW = 16
        EPS = 0.01

        def _alibi_slopes(n_heads):
            closest = 2 ** math.floor(math.log2(n_heads))
            base = 2.0 ** (-2.0 ** (-(math.log2(closest) - 3)))
            slopes = base ** np.arange(1, closest + 1, dtype=np.float32)
            if closest < n_heads:
                eb = 2.0 ** (-2.0 ** (-(math.log2(2 * closest) - 3)))
                extra = eb ** np.arange(1, 2 * (n_heads - closest) + 1, 2, dtype=np.float32)
                slopes = np.concatenate([slopes, extra])
            return jnp.asarray(slopes[:n_heads])

        def _rmsnorm(x, w):
            xf = x.astype(jnp.float32)
            norm = jax.lax.rsqrt(jnp.mean(xf * xf, axis=-1, keepdims=True) + EPS)
            return (xf * norm).astype(x.dtype) * w
        B, L, _ = x.shape
        n_rep = N_HEADS // N_KV_HEADS
        q = (x @ wq.T).reshape(B, L, N_HEADS, HEAD_DIM)
        k = (x @ wk.T).reshape(B, L, N_KV_HEADS, HEAD_DIM)
        v = (x @ wv.T).reshape(B, L, N_KV_HEADS, HEAD_DIM)
        q = _rmsnorm(q, q_norm_w)
        k = _rmsnorm(k, k_norm_w)
        k = jnp.broadcast_to(k[:, :, None], (B, L, n_rep, N_KV_HEADS, HEAD_DIM)).reshape(B, L, N_HEADS, HEAD_DIM)
        v = jnp.broadcast_to(v[:, :, None], (B, L, n_rep, N_KV_HEADS, HEAD_DIM)).reshape(B, L, N_HEADS, HEAD_DIM)
        pos = jnp.arange(L)
        rel = pos[None, :] - pos[:, None]
        slopes = _alibi_slopes(N_HEADS)
        bias = slopes[:, None, None] * rel[None].astype(jnp.float32)
        masked = (rel > 0) | (rel < -WINDOW)
        bias = jnp.where(masked[None], -jnp.inf, bias)
        scale = 1.0 / math.sqrt(HEAD_DIM)
        attn = jnp.einsum('bqhd,bkhd->bhqk', q, k) * scale + bias[None]
        attn = jax.nn.softmax(attn, axis=-1)
        out = jnp.einsum('bhqk,bkhd->bqhd', attn, v).reshape(B, L, N_HEADS * HEAD_DIM)
        return out @ wo.T

    def _L0_ffn_ref(x, w_q, bn_gamma, bn_beta, keys, down_embed, up_embed):
        import jax, jax.numpy as jnp
        import numpy as np
        H = 8
        KD = 128
        TOPK = 8
        NUM_KEYS = 64
        N_EXPERTS = NUM_KEYS * NUM_KEYS
        N_DIM = 256
        BN_EPS = 1e-05

        def gelu_new(x):
            c = jnp.sqrt(jnp.asarray(2.0 / jnp.pi, x.dtype))
            return 0.5 * x * (1.0 + jnp.tanh(c * (x + 0.044715 * x * x * x)))
        b, n, d = x.shape
        q = jnp.einsum('bnd,de->bne', x, w_q)
        mean = jnp.mean(q, axis=(0, 1))
        var = jnp.var(q, axis=(0, 1))
        q = (q - mean) * jax.lax.rsqrt(var + BN_EPS) * bn_gamma + bn_beta
        q = q.reshape(b, n, 2, H, KD).transpose(2, 0, 1, 3, 4)
        sim = jnp.einsum('pbnhd,hkpd->pbnhk', q, keys)
        sx, ix = jax.lax.top_k(sim[0], TOPK)
        sy, iy = jax.lax.top_k(sim[1], TOPK)
        all_scores = (sx[..., :, None] + sy[..., None, :]).reshape(b, n, H, TOPK * TOPK)
        all_indices = (ix[..., :, None] * NUM_KEYS + iy[..., None, :]).reshape(b, n, H, TOPK * TOPK)
        scores, pk = jax.lax.top_k(all_scores, TOPK)
        indices = jnp.take_along_axis(all_indices, pk, axis=-1)
        wd = down_embed[indices]
        wu = up_embed[indices]
        h = jnp.einsum('bnd,bnhkd->bnhk', x, wd)
        h = gelu_new(h)
        h = jax.nn.softmax(scores, axis=-1) * h
        out = jnp.einsum('bnhk,bnhkd->bnd', h, wu)
        return out
    h = _L0_tok_ref(x, L0_tok_W, L0_tok_b, L0_tok_pos_embd)
    h = h + _L0_attn_ref(_layernorm(h, axis=-1), L0_attn_wq, L0_attn_wk, L0_attn_wv, L0_attn_wo, L0_attn_q_norm_w, L0_attn_k_norm_w)
    h = h + _L0_ffn_ref(_layernorm(h, axis=-1), L0_ffn_w_q, L0_ffn_bn_gamma, L0_ffn_bn_beta, L0_ffn_keys, L0_ffn_down_embed, L0_ffn_up_embed)
    return h

_drawn_inputs = setup_inputs


def setup_inputs(seed=0):
    import zlib

    import numpy as np

    out = dict(_drawn_inputs(seed))
    spreads = {'L0_attn_q_norm_w': (1.0, 0.2),
     'L0_attn_k_norm_w': (1.0, 0.2),
     'L0_ffn_bn_gamma': (1.0, 0.6),
     'L0_ffn_bn_beta': (0.0, 0.8)}
    factors = {'L0_ffn_w_q': 8.0, 'L0_ffn_keys': 8.0, 'L0_ffn_down_embed': 8.0, 'L0_ffn_up_embed': 8.0}
    for name, (base, spread) in spreads.items():
        noise = np.random.default_rng([zlib.crc32(name.encode()), seed]).standard_normal(out[name].shape)
        drawn = base * np.exp(spread * noise) if base else spread * noise
        out[name] = jnp.asarray(drawn.astype(out[name].dtype))
    for name, factor in factors.items():
        out[name] = (out[name] * factor).astype(out[name].dtype)
    return out
```

```python
import concourse.bass as bass
from concourse import mybir
from contextlib import ExitStack

IMAGES = 32
PATCHES = 36
TOK = IMAGES * PATCHES
DIM = 256
FC = DIM // 128
PATCH_DIM = 768
KC = PATCH_DIM // 128
HEADS, KV_HEADS, HD = 16, 4, 64
REP = HEADS // KV_HEADS
QC = HEADS * HD // 128
GIMG = 3
GT = GIMG * PATCHES
NG = -(-IMAGES // GIMG)
PAD_TOK = NG * GT
FH, KD, KEYS, TOPK = 8, 128, 64, 8
NC2 = 2 * FH
EXPERTS = KEYS * KEYS
EC = EXPERTS // 128
NT = TOK // 128
BLK = 384
NB = TOK // BLK
TG = 16
NTG = 128 // TG
HG = 4
NHG = EC // HG
RMS_EPS = 0.01
LN_EPS = 1e-5
GATE_SCALE = 4096.0


def vit_block(nc, x_t, tok_w, tok_b, pos, ident_in, bias_in, wq_in, wkv_in, wo_in, qw_in, kw_in,
              ffn_wq, gamma_in, beta_in, keys_in, down_in, up_in, out):
    fp32 = mybir.dt.float32
    fp16 = mybir.dt.float16
    u32 = mybir.dt.uint32
    i32 = mybir.dt.int32
    ALU = mybir.AluOpType
    ACT = mybir.ActivationFunctionType
    AX = mybir.AxisListType
    ds = bass.ds

    ctx = ExitStack()
    with ctx:
        def sb(name, shape, dt, scope=ctx):
            return scope.enter_context(nc.sbuf_tensor(name, shape, dt))

        def sem(name):
            return ctx.enter_context(nc.semaphore(name))

        def spread(ap, axis, n):
            v = ap.unsqueeze(axis)
            shape = list(v.shape)
            shape[axis] = n
            return v.broadcast_to(shape)

        hT = sb("hT", [128, FC, PAD_TOK], fp32)
        xnT = sb("xnT", [128, FC, TOK], fp32)
        downT = sb("downT", [128, FC, EXPERTS], fp32)
        up = sb("up", [128, EC, DIM], fp32)
        ident = sb("ident", [128, 128], fp32)
        mean_w = sb("mean_w", [128, 128], fp32)
        gamma = sb("gamma", [128, NC2], fp32)
        beta = sb("beta", [128, NC2], fp32)
        half_neg = sb("half_neg", [128, HEADS + KV_HEADS + 1], fp32)
        eps_ln = sb("eps_ln", [128, 1], fp32)

        p1 = ExitStack()
        xT = sb("xT", [128, KC, TOK], fp32, p1)
        tokw = sb("tokw", [128, KC, DIM], fp32, p1)
        posb = sb("posb", [128, FC, PATCHES], fp32, p1)
        tokb = sb("tokb", [128, FC], fp32, p1)
        wq = sb("wq", [128, FC, HEADS * HD], fp32, p1)
        wkv = sb("wkv", [128, FC, 2 * KV_HEADS * HD], fp32, p1)
        wo = sb("wo", [128, QC, DIM], fp32, p1)
        qw = sb("qw", [128, 1], fp32, p1)
        kw = sb("kw", [128, 1], fp32, p1)
        kscale = sb("kscale", [128, 1], fp32, p1)
        bias = sb("bias", [GT, KV_HEADS, REP, GT], fp32, p1)
        d1 = sb("d1", [128, FC, GT], fp32, p1)
        sq1 = sb("sq1", [128, FC, GT], fp32, p1)
        sqq = sb("sqq", [GT, HEADS + KV_HEADS, HD], fp32, p1)
        msum = sb("msum", [GT, HEADS + KV_HEADS], fp32, p1)
        rmsv = sb("rmsv", [GT, HEADS + KV_HEADS + 1], fp32, p1)
        vare = sb("vare", [GT, 1], fp32, p1)
        rinv = sb("rinv", [GT, HEADS + KV_HEADS + 1], fp32, p1)
        qkn = sb("qkn", [GT, HEADS + KV_HEADS, HD], fp32, p1)
        qT = sb("qT", [128, QC, GT], fp32, p1)
        kT = sb("kT", [128, KV_HEADS // 2, GT], fp32, p1)
        vall = sb("vall", [GT, NG, KV_HEADS * HD], fp32, p1)
        vcur = sb("vcur", [GT, KV_HEADS * HD], fp32, p1)
        sm = sb("sm", [GT, KV_HEADS, REP, GT], fp32, p1)
        nmax = sb("nmax", [GT, KV_HEADS, REP], fp32, p1)
        psums = sb("psums", [GT, HEADS], fp32, p1)
        pinv = sb("pinv", [GT, HEADS], fp32, p1)
        pn = sb("pn", [GT, HEADS, GT], fp32, p1)
        pT = sb("pT", [GT, KV_HEADS, REP, GT], fp32, p1)
        oT = sb("oT", [128, QC, GT], fp32, p1)
        p1.close()

        p2 = ctx
        stats = sb("stats", [128, NB, 6], fp32, p2)
        mv = sb("mv", [128, 2], fp32, p2)
        bnv = sb("bnv", [128, 1], fp32, p2)
        rstd = sb("rstd", [128, 1], fp32, p2)
        bna = sb("bna", [128, 2], fp32, p2)
        bnb = sb("bnb", [128, 2], fp32, p2)
        bnm = sb("bnm", [128, 1], fp32, p2)
        top_s = sb("top_s", [128, NT, NC2, TOPK], fp32, p2)
        top_i = sb("top_i", [128, NT, NC2, TOPK], fp32, p2)
        best_s = sb("best_s", [128, 2, NT, TOPK], fp32, p2)
        best_i = sb("best_i", [128, 2, NT, TOPK], u32, p2)
        comb = sb("comb", [128, FH, TOPK, TOPK], fp32, p2)
        best = sb("best", [128, FH, TOPK], fp32, p2)
        pick = sb("pick", [128, FH, TOPK], u32, p2)
        pick_a = sb("pick_a", [128, FH, TOPK], i32, p2)
        pick_b = sb("pick_b", [128, FH, TOPK], i32, p2)
        iota8 = sb("iota8", [128, TOPK], fp32, p2)
        mask_a = sb("mask_a", [128, FH, TOPK, TOPK], fp32, p2)
        mask_b = sb("mask_b", [128, FH, TOPK, TOPK], fp32, p2)
        key_i = sb("key_i", [128, FH, TOPK], fp32, p2)
        key_j = sb("key_j", [128, FH, TOPK], fp32, p2)
        expert = sb("expert", [128, FH * TOPK], i32, p2)
        e_lo = sb("e_lo", [128, FH * TOPK], i32, p2)
        e_hi = sb("e_hi", [128, FH * TOPK], i32, p2)
        lo2 = sb("lo2", [128, 2, FH * TOPK], fp32, p2)
        hi2 = sb("hi2", [128, 2, FH * TOPK], fp32, p2)
        dif = sb("dif", [128, FH, TOPK], fp32, p2)
        ex = sb("ex", [128, FH, TOPK], fp32, p2)
        zs = sb("zs", [128, FH], fp32, p2)
        zi = sb("zi", [128, FH], fp32, p2)
        gate2 = sb("gate2", [128, 2, FH * TOPK], fp32, p2)
        gate16 = sb("gate16", [128, FH * TOPK], fp16, p2)
        picksT = sb("picksT", [128, 3, 128], fp16, p2)
        loT = sb("loT", [128, 3, 128], fp16, p2)
        iota32 = sb("iota32", [128, EC, 128], fp16, p2)
        p3 = ExitStack()
        sq2 = sb("sq2", [128, FC, BLK], fp32, p3)
        root = sb("root", [128, 2, BLK], fp32, p3)
        wqc = sb("wqc", [128, 2, FC, KD], fp32, p3)
        keysT = sb("keysT", [128, NC2, KEYS], fp32, p3)
        qb = sb("qb", [128, 2, TOK], fp32, p3)
        sims = sb("sims", [128, 2, NT, KEYS], fp32, p3)
        p3.close()
        onehot_lo = sb("onehot_lo", [128, 128, 128], fp16, p2)
        gated_hi = sb("gated_hi", [128, EC, 128], fp16, p2)
        act_h = sb("act_h", [128, 2, EC, 128], fp32, p2)
        upout = sb("upout", [128, FC, 128], fp32, p2)
        outs = sb("outs", [128, 2, FC, 128], fp32, p2)

        ps = ctx.enter_context(nc.psum_tensor("ps", [128, 8, 512], fp32))

        ld_x = [sem(f"ld_x{k}") for k in range(KC)]
        ld_tokw, ld_pos, ld_tokb, ld_ident, ld_bias = (sem(n) for n in ("ld_tokw", "ld_pos", "ld_tokb", "ld_ident", "ld_bias"))
        ld_wq, ld_wkv, ld_wo, ld_qw, ld_kw = (sem(n) for n in ("ld_wq", "ld_wkv", "ld_wo", "ld_qw", "ld_kw"))
        ld_gamma, ld_beta, ld_keys, ld_down, ld_up = (sem(n) for n in ("ld_gamma", "ld_beta", "ld_keys", "ld_down", "ld_up"))
        ld_wqc = [sem(f"ld_wqc{s}") for s in range(2)]
        const_ready, iota_ready = sem("const_ready"), sem("iota_ready")
        embedded, posb_ready, h_ready = sem("embedded"), sem("posb_ready"), sem("h_ready")
        kscale_ready = sem("kscale_ready")
        mean_ready, d_ready, sq_ready, var_ready = sem("mean_ready"), sem("d_ready"), sem("sq_ready"), sem("var_ready")
        q0_ready, q1_ready, kv_ready = sem("q0_ready"), sem("q1_ready"), sem("kv_ready")
        sqq_ready, msum_ready, vare_ready = sem("sqq_ready"), sem("msum_ready"), sem("vare_ready")
        rmsv_ready, rinv_ready, v_ready, qkn_ready = sem("rmsv_ready"), sem("rinv_ready"), sem("v_ready"), sem("qkn_ready")
        qkt_ready, qkt_copied = sem("qkt_ready"), sem("qkt_copied")
        score_ready = [sem(f"score_ready{g}") for g in range(KV_HEADS)]
        biased = [sem(f"biased{g}") for g in range(KV_HEADS)]
        max_ready = [sem(f"max_ready{g}") for g in range(KV_HEADS)]
        exp_ready, pinv_ready, pn_ready, vcur_ready = sem("exp_ready"), sem("pinv_ready"), sem("pn_ready"), sem("vcur_ready")
        pt_ready, pt_copied_act, pt_copied_dve = sem("pt_ready"), sem("pt_copied_act"), sem("pt_copied_dve")
        o_ready, o_copied_act, o_copied_dve = sem("o_ready"), sem("o_copied_act"), sem("o_copied_dve")
        wo_ready, h2_ready = sem("wo_ready"), sem("h2_ready")
        mean2_ready, d2_ready, sq2_ready, var2_ready = sem("mean2_ready"), sem("d2_ready"), sem("sq2_ready"), sem("var2_ready")
        root_ready, rroot_ready, xn_ready = sem("root_ready"), sem("rroot_ready"), sem("xn_ready")
        fq_ready, stats_ready, mv_ready, bnv_ready, rstd_ready = (sem(n) for n in ("fq_ready", "stats_ready", "mv_ready", "bnv_ready", "rstd_ready"))
        bna_ready, bnm_ready, bnb_ready, qb_ready = (sem(n) for n in ("bna_ready", "bnm_ready", "bnb_ready", "qb_ready"))
        sim_ready, sim_copied, tops_ready, topi_ready = (sem(n) for n in ("sim_ready", "sim_copied", "tops_ready", "topi_ready"))
        top_kept = sem("top_kept")
        comb_ready, best_ready, pick_ready, dif_ready, ex_ready = (sem(n) for n in ("comb_ready", "best_ready", "pick_ready", "dif_ready", "ex_ready"))
        zs_ready, zi_ready, gate_ready, gate16_ready, gate2_ready = (sem(n) for n in ("zs_ready", "zi_ready", "gate_ready", "gate16_ready", "gate2_ready"))
        pickab_ready, mask_ready, masked_ready, key_ready = (sem(n) for n in ("pickab_ready", "mask_ready", "masked_ready", "key_ready"))
        expert_ready, elohi_ready, lohi2_ready = (sem(n) for n in ("expert_ready", "elohi_ready", "lohi2_ready"))
        picks_tr, picks_copied, lot_ready, lo_hot, hi_hot, gated = (sem(n) for n in ("picks_tr", "picks_copied", "lot_ready", "lo_hot", "hi_hot", "gated"))
        down_ready, gelu_ready, gate_mm, acts_ready = (sem(n) for n in ("down_ready", "gelu_ready", "gate_mm", "acts_ready"))
        up_ready, up_copied, sum_ready = sem("up_ready"), sem("up_copied"), sem("sum_ready")
        stored = [sem(f"stored{s}") for s in range(2)]

        block = ctx.enter_context(nc.Block())

        blocks1 = [(0, 432), (432, 432), (864, 288)]

        @block.sync
        def _(sp):
            sp.dma_start(tokw[:], tok_w).then_inc(ld_tokw, 16)
            for k in range(KC):
                sp.dma_start(xT[:, k, :], x_t[k]).then_inc(ld_x[k], 16)
            sp.dma_start(bias[:], bias_in).then_inc(ld_bias, 16)
            sp.dma_start(wo[:], wo_in).then_inc(ld_wo, 16)
            sp.dma_start(downT[:], down_in).then_inc(ld_down, 16)
            sp.dma_start(up[:], up_in).then_inc(ld_up, 16)
            sp.dma_start(gamma[:], gamma_in).then_inc(ld_gamma, 16)
            sp.dma_start(beta[:], beta_in).then_inc(ld_beta, 16)
            sp.wait_ge(h2_ready, NG)
            sp.dma_start(wqc[:, 0], ffn_wq[0]).then_inc(ld_wqc[0], 16)
            sp.dma_start(wqc[:, 1], ffn_wq[1]).then_inc(ld_wqc[1], 16)
            sp.dma_start(keysT[:], keys_in).then_inc(ld_keys, 16)
            with sp.Fori(1, NC2 // 2) as j:
                for s in range(2):
                    sp.wait_ge(fq_ready, 2 * j + s - 1)
                    sp.dma_start(wqc[:, s], ffn_wq[ds(2 * j + s, 1)].rearrange("o p f n -> p (o f) n")).then_inc(ld_wqc[s], 16)
            for t in range(NT):
                sp.wait_ge(sum_ready, t + 1)
                sp.dma_start(out[:, :, t * 128:(t + 1) * 128], outs[:, t % 2]).then_inc(stored[t % 2], 16)
            sp.wait_ge(stored[0], 16 * ((NT + 1) // 2))
            sp.wait_ge(stored[1], 16 * (NT // 2))

        @block.tensor
        def _(pe):
            mm = nc.tensor.matmul

            def mean_of_group(g, first=False):
                if not first:
                    pe.wait_ge(d_ready, g)
                    pe.wait_ge(vare_ready, g)
                for f in range(FC):
                    last = mm(ps[:, 0, 0:GT], mean_w[:], hT[:, f, ds(g * GT, GT)], start=f == 0, stop=f == FC - 1)
                last.then_inc(mean_ready, 1)

            def project_group(g, first=False):
                pe.wait_ge(sq_ready, g + 1)
                for f in range(FC):
                    last = mm(ps[0:GT, 0, 256:257], sq1[:, f, :], mean_w[:, 0:1], start=f == 0, stop=f == FC - 1)
                last.then_inc(var_ready, 1)
                if not first:
                    pe.wait_ge(qkt_copied, g)
                for bank, w, c0, done in ((1, wq, 0, q0_ready), (2, wq, 512, q1_ready), (3, wkv, 0, kv_ready)):
                    for f in range(FC):
                        last = mm(ps[0:GT, bank, :], d1[:, f, :], w[:, f, c0:c0 + 512], start=f == 0, stop=f == FC - 1)
                    last.then_inc(done, 1)

            def transpose_qk(g):
                pe.wait_ge(qkn_ready, g + 1)
                pe.wait_ge(v_ready, g + 1)
                flat = qkn[:].rearrange("p h d -> p (h d)")
                for c in range(QC + KV_HEADS // 2):
                    last = nc.tensor.transpose(ps[:, 1 + c // 4, (c % 4) * GT:(c % 4 + 1) * GT],
                                               flat[:, c * 128:(c + 1) * 128], ident[0:GT, 0:GT])
                last.then_inc(qkt_ready, 1)

            def score_group(g, free):
                pe.wait_ge(qkt_copied, g + 1)
                if free is not None:
                    pe.wait_ge(h2_ready, free)
                for kv in range(KV_HEADS):
                    r0 = 64 * (kv % 2)
                    for i in range(REP):
                        h = kv + KV_HEADS * i
                        last = mm(ps[0:GT, 4 + kv, i * GT:(i + 1) * GT], qT[r0:r0 + 64, h // 2, :],
                                  kT[r0:r0 + 64, kv // 2, :], start=True, stop=True)
                    last.then_inc(score_ready[kv], 1)

            def attend_group(g, next_scores=True):
                pe.wait_ge(pn_ready, g + 1)
                if next_scores:
                    pe.wait_ge(biased[KV_HEADS - 1], g + 2)
                else:
                    pe.wait_ge(h2_ready, g)
                for kv in range(KV_HEADS):
                    for i in range(REP):
                        last = nc.tensor.transpose(ps[0:GT, 4 + kv, i * GT:(i + 1) * GT], pn[:, REP * kv + i, :],
                                                   ident[0:GT, 0:GT])
                last.then_inc(pt_ready, 1)
                pe.wait_ge(vcur_ready, g + 1)
                pe.wait_ge(pt_copied_act, g + 1)
                pe.wait_ge(pt_copied_dve, g + 1)
                for kv in range(KV_HEADS):
                    r0 = 64 * (kv % 2)
                    last = mm(ps[r0:r0 + 64, 4 + kv // 2, 0:REP * GT], vcur[:, kv * HD:(kv + 1) * HD],
                              pT[:, kv].rearrange("p i q -> p (i q)"), start=True, stop=True)
                last.then_inc(o_ready, 1)
                pe.wait_ge(o_copied_act, g + 1)
                pe.wait_ge(o_copied_dve, g + 1)
                for f in range(FC):
                    for c in range(QC):
                        last = mm(ps[:, 6, f * GT:(f + 1) * GT], wo[:, c, f * 128:(f + 1) * 128], oT[:, c, :],
                                  start=c == 0, stop=c == QC - 1)
                last.then_inc(wo_ready, 1)

            pe.wait_ge(ld_tokw, 16)
            for k in range(KC):
                pe.wait_ge(ld_x[k], 16)
                for b, (t0, n) in enumerate(blocks1):
                    for f in range(FC):
                        last = mm(ps[:, 2 * b + f, 0:n], tokw[:, k, f * 128:(f + 1) * 128], xT[:, k, t0:t0 + n],
                                  start=k == 0, stop=k == KC - 1)
                        if k == KC - 1:
                            last.then_inc(embedded, 1)

            pe.wait_ge(const_ready, 1)
            pe.wait_ge(h_ready, FC * len(blocks1))
            pe.wait_ge(ld_ident, 16)
            pe.wait_ge(ld_wq, 16)
            pe.wait_ge(ld_wkv, 16)
            mean_of_group(0, first=True)
            project_group(0, first=True)
            mean_of_group(1)
            transpose_qk(0)
            score_group(0, None)
            project_group(1)
            mean_of_group(2)
            transpose_qk(1)
            pe.wait_ge(biased[KV_HEADS - 1], 1)
            score_group(1, None)
            pe.wait_ge(ld_wo, 16)
            with pe.Fori(1, NG - 2) as i:
                project_group(i + 1)
                attend_group(i - 1)
                mean_of_group(i + 2)
                transpose_qk(i + 1)
                score_group(i + 1, i)
            project_group(NG - 1)
            attend_group(NG - 3)
            transpose_qk(NG - 1)
            score_group(NG - 1, NG - 2)
            attend_group(NG - 2)
            attend_group(NG - 1, next_scores=False)

            for b in range(NB):
                pe.wait_ge(h2_ready, NG)
                for f in range(FC):
                    last = mm(ps[:, b, 0:BLK], mean_w[:], hT[:, f, b * BLK:(b + 1) * BLK], start=f == 0, stop=f == FC - 1)
                last.then_inc(mean2_ready, 1)
            for b in range(NB):
                pe.wait_ge(sq2_ready, b + 1)
                for f in range(FC):
                    last = mm(ps[:, 3 + b, 0:BLK], mean_w[:], sq2[:, f, :], start=f == 0, stop=f == FC - 1)
                last.then_inc(var2_ready, 1)

            def router_q(c, s, load, first=False):
                pe.wait_ge(ld_wqc[s], load)
                if not first:
                    pe.wait_ge(qb_ready, c - 1)
                for b in range(NB):
                    for f in range(FC):
                        last = mm(ps[:, 3 * s + b, 0:BLK], wqc[:, s, f, :], xnT[:, f, b * BLK:(b + 1) * BLK],
                                  start=f == 0, stop=f == FC - 1)
                last.then_inc(fq_ready, 1)

            def router_sim(c, s, first=False):
                pe.wait_ge(qb_ready, c + 1)
                if not first:
                    pe.wait_ge(sim_copied, c)
                for t in range(NT):
                    last = mm(ps[:, 6 + t // 8, (t % 8) * KEYS:(t % 8 + 1) * KEYS], qb[:, s, t * 128:(t + 1) * 128],
                              keysT[:, ds(c, 1), :].rearrange("p o k -> p (o k)"), start=True, stop=True)
                last.then_inc(sim_ready, 1)

            pe.wait_ge(xn_ready, NB)
            router_q(0, 0, 16, first=True)
            router_q(1, 1, 16, first=True)
            pe.wait_ge(ld_keys, 16)
            router_sim(0, 0, first=True)
            router_q(2, 0, 32)
            router_sim(1, 1)
            with pe.Fori(1, NC2 // 2 - 1) as j:
                router_q(2 * j + 1, 1, 16 * j + 16)
                router_sim(2 * j, 0)
                router_q(2 * j + 2, 0, 16 * j + 32)
                router_sim(2 * j + 1, 1)
            router_q(NC2 - 1, 1, 16 * (NC2 // 2))
            router_sim(NC2 - 2, 0)
            router_sim(NC2 - 1, 1)

            def down_product(t, k, first=False):
                if not first:
                    pe.wait_ge(gelu_ready, t * NHG + k - 1)
                for i in range(HG):
                    c = HG * k + i
                    for f in range(FC):
                        last = mm(ps[:, k % 2, i * 128:(i + 1) * 128], downT[:, f, c * 128:(c + 1) * 128],
                                  xnT[:, f, ds(t * 128, 128)], start=f == 0, stop=f == FC - 1)
                last.then_inc(down_ready, 1)

            def transpose_picks(t):
                pe.wait_ge(lohi2_ready, t + 1)
                pe.wait_ge(gate2_ready, t + 1)
                for n, a in enumerate((lo2, hi2, gate2)):
                    last = nc.tensor.transpose(ps[:, 6, n * 128:(n + 1) * 128], a[:].rearrange("p a b -> p (a b)"), ident[:])
                last.then_inc(picks_tr, 1)

            def gate_matrices(t, first=False):
                pe.wait_ge(lo_hot, t + 1)
                pe.wait_ge(gated, t + 1)
                for k in range(NTG):
                    if not (first and k < 4):
                        pe.wait_ge(acts_ready, t * NTG + k - 3)
                    for n in range(TG):
                        tok = k * TG + n
                        last = mm(ps[:, 2 + k % 4, n * EC:(n + 1) * EC], onehot_lo[:, :, tok], gated_hi[:, :, tok],
                                  start=True, stop=True)
                    last.then_inc(gate_mm, 1)

            def up_product(t, first=False):
                pe.wait_ge(acts_ready, (t + 1) * NTG)
                if not first:
                    pe.wait_ge(up_copied, t)
                for c in range(EC):
                    for f in range(FC):
                        last = mm(ps[:, 6 + f, 0:128], up[:, c, f * 128:(f + 1) * 128],
                                  act_h[:, ds(t % 2, 1), c, :].rearrange("p o t -> p (o t)"), start=c == 0, stop=c == EC - 1)
                last.then_inc(up_ready, 1)

            pe.wait_ge(ld_down, 16)
            pe.wait_ge(ld_up, 16)
            pe.wait_ge(sim_copied, NC2)
            for k in range(NHG):
                down_product(0, k, first=k < 2)
            transpose_picks(0)

            def expert_tile(t, first=False, last=False):
                gate_matrices(t, first)
                if not last:
                    for k in range(NHG - 2):
                        down_product(t + 1, k)
                    if not first:
                        pe.wait_ge(up_copied, t)
                    transpose_picks(t + 1)
                    for k in range(NHG - 2, NHG):
                        down_product(t + 1, k)
                    pe.wait_ge(picks_copied, t + 2)
                up_product(t, first)

            expert_tile(0, first=True)
            with pe.Fori(1, NT - 1) as t:
                expert_tile(t)
            expert_tile(NT - 1, last=True)

        @block.scalar
        def _(act):
            A = nc.scalar.activation
            act.dma_start(posb[:], pos).then_inc(ld_pos, 16)
            act.dma_start(tokb[:], tok_b).then_inc(ld_tokb, 16)
            act.dma_start(ident[:], ident_in).then_inc(ld_ident, 16)
            act.dma_start(qw[:], qw_in).then_inc(ld_qw, 16)
            act.dma_start(kw[:], kw_in).then_inc(ld_kw, 16)
            act.dma_start(wq[:], wq_in).then_inc(ld_wq, 16)
            act.dma_start(wkv[:], wkv_in).then_inc(ld_wkv, 16)

            def square_d(g, first=False):
                act.wait_ge(d_ready, g + 1)
                if not first:
                    act.wait_ge(var_ready, g)
                A(sq1[:], d1[:], ACT.Square).then_inc(sq_ready, 1)

            def square_qk(g, first=False):
                if not first:
                    act.wait_ge(msum_ready, g)
                act.wait_ge(q0_ready, g + 1)
                A(sqq[:, 0:8, :].rearrange("p h d -> p (h d)"), ps[0:GT, 1, :], ACT.Square)
                act.wait_ge(q1_ready, g + 1)
                A(sqq[:, 8:16, :].rearrange("p h d -> p (h d)"), ps[0:GT, 2, :], ACT.Square)
                act.wait_ge(kv_ready, g + 1)
                A(sqq[:, 16:20, :].rearrange("p h d -> p (h d)"), ps[0:GT, 3, 0:256], ACT.Square).then_inc(sqq_ready, 1)

            def copy_v(g):
                act.wait_ge(rinv_ready, g + 1)
                A(vall[:, ds(g, 1), :].rearrange("p o n -> p (o n)"), ps[0:GT, 3, 256:512], ACT.Copy,
                  scale=rinv[:, HEADS + KV_HEADS:HEADS + KV_HEADS + 1]).then_inc(v_ready, 1)

            def copy_qk(g, first=False):
                act.wait_ge(qkt_ready, g + 1)
                if not first:
                    act.wait_ge(score_ready[KV_HEADS - 1], g)
                for n in range(2):
                    A(qT[:, 4 * n:4 * n + 4, :], ps[:, 1 + n, 0:4 * GT].rearrange("p (c t) -> p c t", t=GT), ACT.Copy)
                A(kT[:], ps[:, 3, 0:2 * GT].rearrange("p (c t) -> p c t", t=GT), ACT.Copy,
                  scale=kscale[:, 0:1]).then_inc(qkt_copied, 1)

            def exps(g):
                for kv in range(KV_HEADS):
                    act.wait_ge(max_ready[kv], g + 1)
                    for i in range(REP):
                        last = A(sm[:, kv, i, :], sm[:, kv, i, :], ACT.Exp, bias=nmax[:, kv, i:i + 1],
                                 accum_out=psums[:, REP * kv + i:REP * kv + i + 1])
                last.then_inc(exp_ready, 1)

            def copy_pt(g):
                act.wait_ge(pt_ready, g + 1)
                for kv in range(2):
                    last = A(pT[:, kv].rearrange("p i q -> p (i q)"), ps[0:GT, 4 + kv, 0:REP * GT], ACT.Copy)
                last.then_inc(pt_copied_act, 1)

            def copy_o(g):
                act.wait_ge(o_ready, g + 1)
                A(oT[:, 0:QC:2, :], ps[:, 4, 0:REP * GT].rearrange("p (c t) -> p c t", t=GT), ACT.Copy).then_inc(o_copied_act, 1)

            act.wait_ge(kscale_ready, 1)
            square_d(0, first=True)
            square_qk(0, first=True)
            copy_v(0)
            square_d(1)
            copy_qk(0, first=True)
            exps(0)
            square_qk(1)
            copy_v(1)
            square_d(2)
            copy_qk(1)
            with act.Fori(1, NG - 2) as i:
                exps(i)
                square_qk(i + 1)
                copy_pt(i - 1)
                copy_v(i + 1)
                copy_o(i - 1)
                square_d(i + 2)
                copy_qk(i + 1)
            exps(NG - 2)
            square_qk(NG - 1)
            copy_pt(NG - 3)
            copy_v(NG - 1)
            copy_o(NG - 3)
            copy_qk(NG - 1)
            exps(NG - 1)
            copy_pt(NG - 2)
            copy_o(NG - 2)
            copy_pt(NG - 1)
            copy_o(NG - 1)

            for b in range(NB):
                act.wait_ge(d2_ready, b + 1)
                if b:
                    act.wait_ge(var2_ready, b)
                A(sq2[:], xnT[:, :, b * BLK:(b + 1) * BLK], ACT.Square).then_inc(sq2_ready, 1)
                act.wait_ge(var2_ready, b + 1)
                if b > 1:
                    act.wait_ge(xn_ready, b - 1)
                A(root[:, b % 2], ps[:, 3 + b, 0:BLK], ACT.Sqrt, bias=eps_ln[:, 0:1]).then_inc(root_ready, 1)

            def affine(c, s, first=False):
                act.wait_ge(bnb_ready, c + 1)
                if not first:
                    act.wait_ge(sim_ready, c - 1)
                for b in range(NB):
                    last = A(qb[:, s, b * BLK:(b + 1) * BLK], ps[:, 3 * s + b, 0:BLK], ACT.Identity,
                             bias=bnb[:, s:s + 1], scale=bna[:, s:s + 1])
                last.then_inc(qb_ready, 1)

            def copy_sim(c, s, first=False):
                act.wait_ge(sim_ready, c + 1)
                if not first:
                    act.wait_ge(topi_ready, c - 1)
                A(sims[:, s, 0:8, :].rearrange("p t k -> p (t k)"), ps[:, 6, :], ACT.Copy)
                A(sims[:, s, 8, :], ps[:, 7, 0:KEYS], ACT.Copy).then_inc(sim_copied, 1)

            affine(0, 0, first=True)
            affine(1, 1, first=True)
            copy_sim(0, 0, first=True)
            affine(2, 0)
            copy_sim(1, 1, first=True)
            with act.Fori(1, NC2 // 2 - 1) as j:
                affine(2 * j + 1, 1)
                copy_sim(2 * j, 0)
                affine(2 * j + 2, 0)
                copy_sim(2 * j + 1, 1)
            affine(NC2 - 1, 1)
            copy_sim(NC2 - 2, 0)
            copy_sim(NC2 - 1, 1)

            def gelu(t, k):
                act.wait_ge(down_ready, t * NHG + k + 1)
                A(act_h[:, ds(t % 2, 1), HG * k:HG * (k + 1), :].rearrange("p o c t -> p (o c t)"), ps[:, k % 2, :],
                  ACT.Gelu_apprx_tanh).then_inc(gelu_ready, 1)

            def exp_gates(t):
                act.wait_ge(dif_ready, t + 1)
                A(ex[:], dif[:], ACT.Exp).then_inc(ex_ready, 1)

            def copy_picks(t, first=False):
                act.wait_ge(picks_tr, t + 1)
                if not first:
                    act.wait_ge(gated, t)
                A(picksT[:].rearrange("p n t -> p (n t)"), ps[:, 6, 0:384], ACT.Copy).then_inc(picks_copied, 1)

            def copy_up(t, first=False):
                act.wait_ge(up_ready, t + 1)
                if not first:
                    act.wait_ge(sum_ready, t)
                for f in range(FC):
                    last = A(upout[:, f, :], ps[:, 6 + f, 0:128], ACT.Copy)
                last.then_inc(up_copied, 1)

            def expert_tile(t, first=False):
                for k in range(3):
                    gelu(t + 1, k)
                exp_gates(t + 1)
                for k in range(3, NHG - 2):
                    gelu(t + 1, k)
                copy_picks(t + 1)
                for k in range(NHG - 2, NHG):
                    gelu(t + 1, k)
                copy_up(t, first)

            exp_gates(0)
            for k in range(NHG):
                gelu(0, k)
            copy_picks(0, first=True)
            expert_tile(0, first=True)
            with act.Fori(1, NT - 1) as t:
                expert_tile(t)
            copy_up(NT - 1)

        @block.vector
        def _(dve):
            V = nc.vector

            def centre(g, first=False):
                dve.wait_ge(mean_ready, g + 1)
                if not first:
                    dve.wait_ge(kv_ready, g)
                    dve.wait_ge(sq_ready, g)
                V.tensor_tensor(d1[:], hT[:, :, ds(g * GT, GT)], spread(ps[:, 0, 0:GT], 1, FC), ALU.subtract).then_inc(d_ready, 1)

            def rms_sums(g, first=False):
                dve.wait_ge(var_ready, g + 1)
                if not first:
                    dve.wait_ge(rinv_ready, g)
                V.tensor_scalar(rmsv[:, HEADS + KV_HEADS:], ps[0:GT, 0, 256:257], LN_EPS, None, ALU.add)
                V.tensor_scalar(vare[:], ps[0:GT, 0, 256:257], LN_EPS, RMS_EPS, ALU.add, ALU.mult).then_inc(vare_ready, 1)
                dve.wait_ge(sqq_ready, g + 1)
                V.reduce_sum(msum[:], sqq[:], AX.X).then_inc(msum_ready, 1)
                dve.wait_ge(msum_ready, g + 1)
                dve.wait_ge(vare_ready, g + 1)
                V.tensor_scalar(rmsv[:, 0:HEADS + KV_HEADS], msum[:], 1.0 / HD, vare[:, 0:1], ALU.mult, ALU.add).then_inc(rmsv_ready, 1)

            def normalise_qk(g, first=False):
                dve.wait_ge(rinv_ready, g + 1)
                if not first:
                    dve.wait_ge(qkt_ready, g)
                for bank, h0, n in ((1, 0, 8), (2, 8, 8), (3, 16, 4)):
                    if bank == 3:
                        dve.wait_ge(v_ready, g + 1)
                    last = V.tensor_tensor(qkn[:, h0:h0 + n, :], ps[0:GT, bank, 0:n * HD].rearrange("p (h d) -> p h d", d=HD),
                                           spread(rinv[:, h0:h0 + n], 2, HD), ALU.mult)
                last.then_inc(qkn_ready, 1)

            def bias_scores(g, first=False):
                if not first:
                    dve.wait_ge(pn_ready, g)

                def add_bias(kv):
                    dve.wait_ge(score_ready[kv], g + 1)
                    V.tensor_tensor(sm[:, kv].rearrange("p i k -> p (i k)"), ps[0:GT, 4 + kv, 0:REP * GT],
                                    bias[:, kv].rearrange("p i k -> p (i k)"), ALU.add).then_inc(biased[kv], 1)

                def neg_max(kv):
                    dve.wait_ge(biased[kv], g + 1)
                    V.reduce_max(nmax[:, kv, :], sm[:, kv], AX.X, negate=True).then_inc(max_ready[kv], 1)

                add_bias(0)
                for kv in range(1, KV_HEADS):
                    add_bias(kv)
                    neg_max(kv - 1)
                neg_max(KV_HEADS - 1)

            def invert_sums(g):
                dve.wait_ge(exp_ready, g + 1)
                V.reciprocal(pinv[:], psums[:]).then_inc(pinv_ready, 1)

            def copy_pt(g):
                dve.wait_ge(pt_ready, g + 1)
                for kv in range(2, KV_HEADS):
                    last = V.tensor_copy(pT[:, kv].rearrange("p i q -> p (i q)"), ps[0:GT, 4 + kv, 0:REP * GT])
                last.then_inc(pt_copied_dve, 1)

            def copy_o(g):
                dve.wait_ge(o_ready, g + 1)
                V.tensor_copy(oT[:, 1:QC:2, :], ps[:, 5, 0:REP * GT].rearrange("p (c t) -> p c t", t=GT)).then_inc(o_copied_dve, 1)

            def residual(g):
                dve.wait_ge(wo_ready, g + 1)
                V.tensor_tensor(hT[:, :, ds(g * GT, GT)], hT[:, :, ds(g * GT, GT)],
                                ps[:, 6, 0:FC * GT].rearrange("p (f t) -> p f t", t=GT), ALU.add).then_inc(h2_ready, 1)

            dve.wait_ge(ld_pos, 16)
            dve.wait_ge(ld_tokb, 16)
            V.tensor_tensor(posb[:], posb[:], spread(tokb[:], 2, PATCHES), ALU.add).then_inc(posb_ready, 1)
            dve.wait_ge(ld_qw, 16)
            dve.wait_ge(ld_kw, 16)
            V.tensor_scalar(kscale[:], qw[:], kw[:, 0:1], HD ** -0.5, ALU.mult, ALU.mult).then_inc(kscale_ready, 1)
            dve.wait_ge(posb_ready, 1)
            for b, (t0, n) in enumerate(blocks1):
                for f in range(FC):
                    dve.wait_ge(embedded, 2 * b + f + 1)
                    V.tensor_tensor(hT[:, f, t0:t0 + n].rearrange("p (b t) -> p b t", t=PATCHES),
                                    ps[:, 2 * b + f, 0:n].rearrange("p (b t) -> p b t", t=PATCHES),
                                    spread(posb[:, f, :], 1, n // PATCHES), ALU.add).then_inc(h_ready, 1)
            dve.wait_ge(h_ready, FC * len(blocks1))
            dve.wait_ge(const_ready, 1)
            dve.wait_ge(ld_bias, 16)
            centre(0, first=True)
            rms_sums(0, first=True)
            normalise_qk(0, first=True)
            centre(1)
            bias_scores(0, first=True)
            rms_sums(1)
            invert_sums(0)
            normalise_qk(1)
            centre(2)
            bias_scores(1)
            with dve.Fori(1, NG - 2) as i:
                rms_sums(i + 1)
                invert_sums(i)
                copy_pt(i - 1)
                normalise_qk(i + 1)
                copy_o(i - 1)
                residual(i - 1)
                centre(i + 2)
                bias_scores(i + 1)
            rms_sums(NG - 1)
            invert_sums(NG - 2)
            copy_pt(NG - 3)
            normalise_qk(NG - 1)
            copy_o(NG - 3)
            residual(NG - 3)
            bias_scores(NG - 1)
            copy_pt(NG - 2)
            invert_sums(NG - 1)
            copy_o(NG - 2)
            residual(NG - 2)
            copy_pt(NG - 1)
            copy_o(NG - 1)
            residual(NG - 1)

            dve.wait_ge(h2_ready, NG)
            for b in range(NB):
                dve.wait_ge(mean2_ready, b + 1)
                V.tensor_tensor(xnT[:, :, b * BLK:(b + 1) * BLK], hT[:, :, b * BLK:(b + 1) * BLK],
                                spread(ps[:, b, 0:BLK], 1, FC), ALU.subtract).then_inc(d2_ready, 1)
            for b in range(NB):
                dve.wait_ge(root_ready, b + 1)
                V.reciprocal(root[:, b % 2], root[:, b % 2]).then_inc(rroot_ready, 1)
                dve.wait_ge(rroot_ready, b + 1)
                V.tensor_tensor(xnT[:, :, b * BLK:(b + 1) * BLK], xnT[:, :, b * BLK:(b + 1) * BLK],
                                spread(root[:, b % 2], 1, FC), ALU.mult).then_inc(xn_ready, 1)

            def batch_norm(c, s, first=False):
                dve.wait_ge(fq_ready, c + 1)
                for b in range(NB):
                    last = V.bn_stats(stats[:, b, :], ps[:, 3 * s + b, 0:BLK])
                last.then_inc(stats_ready, 1)
                dve.wait_ge(stats_ready, c + 1)
                dve.nop(nofuse=True)
                V.bn_aggr(mv[:], stats[:].rearrange("p b n -> p (b n)")).then_inc(mv_ready, 1)
                dve.wait_ge(mv_ready, c + 1)
                V.tensor_scalar(bnv[:], mv[:, 1:2], LN_EPS, None, ALU.add).then_inc(bnv_ready, 1)
                dve.wait_ge(rstd_ready, c + 1)
                if not first:
                    dve.wait_ge(qb_ready, c - 1)
                V.tensor_scalar(bna[:, s:s + 1], gamma[:, ds(c, 1)], rstd[:, 0:1], None, ALU.mult).then_inc(bna_ready, 1)
                dve.wait_ge(bna_ready, c + 1)
                V.tensor_scalar(bnm[:], mv[:, 0:1], bna[:, s:s + 1], None, ALU.mult).then_inc(bnm_ready, 1)
                dve.wait_ge(bnm_ready, c + 1)
                V.tensor_scalar(bnb[:, s:s + 1], beta[:, ds(c, 1)], bnm[:, 0:1], None, ALU.subtract).then_inc(bnb_ready, 1)

            def top_keys(c, s, first=False):
                dve.wait_ge(sim_copied, c + 1)
                if not first:
                    dve.wait_ge(top_kept, c - 1)
                dve.nop(nofuse=True)
                for t in range(NT):
                    last = V.max(best_s[:, s, t, :], sims[:, s, t, :])
                last.then_inc(tops_ready, 1)
                dve.wait_ge(tops_ready, c + 1)
                dve.nop(nofuse=True)
                for t in range(NT):
                    last = V.max_index(best_i[:, s, t, :], best_s[:, s, t, :], sims[:, s, t, :])
                last.then_inc(topi_ready, 1)

            dve.wait_ge(ld_gamma, 16)
            dve.wait_ge(ld_beta, 16)
            batch_norm(0, 0, first=True)
            batch_norm(1, 1, first=True)
            top_keys(0, 0, first=True)
            batch_norm(2, 0)
            top_keys(1, 1, first=True)
            with dve.Fori(1, NC2 // 2 - 1) as j:
                batch_norm(2 * j + 1, 1)
                top_keys(2 * j, 0)
                batch_norm(2 * j + 2, 0)
                top_keys(2 * j + 1, 1)
            batch_norm(NC2 - 1, 1)
            top_keys(NC2 - 2, 0)
            top_keys(NC2 - 1, 1)

            def choose(t, first=False):
                sx = top_s[:, ds(t, 1), 0:FH, :].rearrange("p o h k -> p (o h) k")
                sy = top_s[:, ds(t, 1), FH:NC2, :].rearrange("p o h k -> p (o h) k")
                ix = top_i[:, ds(t, 1), 0:FH, :].rearrange("p o h k -> p (o h) k")
                iy = top_i[:, ds(t, 1), FH:NC2, :].rearrange("p o h k -> p (o h) k")
                V.tensor_tensor(comb[:], spread(sx, 3, TOPK), spread(sy, 2, TOPK), ALU.add).then_inc(comb_ready, 1)
                dve.wait_ge(comb_ready, t + 1)
                dve.nop(nofuse=True)
                for h in range(FH):
                    last = V.max(best[:, h, :], comb[:, h].rearrange("p a b -> p (a b)"))
                last.then_inc(best_ready, 1)
                dve.wait_ge(best_ready, t + 1)
                if not first:
                    dve.wait_ge(ex_ready, t)
                V.tensor_tensor(dif[:], best[:], best[:, :, 0:1].broadcast_to([128, FH, TOPK]), ALU.subtract).then_inc(dif_ready, 1)
                for h in range(FH):
                    last = V.max_index(pick[:, h, :], best[:, h, :], comb[:, h].rearrange("p a b -> p (a b)"))
                last.then_inc(pick_ready, 1)
                dve.wait_ge(pick_ready, t + 1)
                V.tensor_scalar(pick_a[:], pick[:].bitcast(i32), 3, None, ALU.logical_shift_right)
                V.tensor_scalar(pick_b[:], pick[:].bitcast(i32), TOPK - 1, None, ALU.bitwise_and).then_inc(pickab_ready, 1)
                dve.wait_ge(pickab_ready, t + 1)
                ranks = spread(spread(iota8[:], 1, TOPK), 1, FH)
                V.tensor_tensor(mask_a[:], spread(pick_a[:], 3, TOPK), ranks, ALU.is_equal)
                V.tensor_tensor(mask_b[:], spread(pick_b[:], 3, TOPK), ranks, ALU.is_equal).then_inc(mask_ready, 1)
                dve.wait_ge(mask_ready, t + 1)
                V.tensor_tensor(mask_a[:], mask_a[:], spread(ix, 2, TOPK), ALU.mult)
                V.tensor_tensor(mask_b[:], mask_b[:], spread(iy, 2, TOPK), ALU.mult).then_inc(masked_ready, 1)
                dve.wait_ge(masked_ready, t + 1)
                V.reduce_sum(key_i[:], mask_a[:], AX.X)
                V.reduce_sum(key_j[:], mask_b[:], AX.X).then_inc(key_ready, 1)
                dve.wait_ge(key_ready, t + 1)
                V.scalar_tensor_tensor(expert[:], key_i[:].rearrange("p h k -> p (h k)"), float(KEYS),
                                       key_j[:].rearrange("p h k -> p (h k)"), ALU.mult, ALU.add).then_inc(expert_ready, 1)
                dve.wait_ge(expert_ready, t + 1)
                V.tensor_scalar(e_lo[:], expert[:], 127, None, ALU.bitwise_and)
                V.tensor_scalar(e_hi[:], expert[:], 7, None, ALU.logical_shift_right).then_inc(elohi_ready, 1)
                dve.wait_ge(elohi_ready, t + 1)
                if not first:
                    dve.wait_ge(picks_tr, t)
                V.tensor_copy(lo2[:], spread(e_lo[:], 1, 2))
                V.tensor_copy(hi2[:], spread(e_hi[:], 1, 2)).then_inc(lohi2_ready, 1)
                dve.wait_ge(ex_ready, t + 1)
                V.reduce_sum(zs[:], ex[:], AX.X).then_inc(zs_ready, 1)
                dve.wait_ge(zs_ready, t + 1)
                V.reciprocal(zi[:], zs[:]).then_inc(zi_ready, 1)
                dve.wait_ge(zi_ready, t + 1)
                V.scalar_tensor_tensor(gate2[:, 0, :].rearrange("p (h k) -> p h k", k=TOPK), ex[:], GATE_SCALE,
                                       spread(zi[:], 2, TOPK), ALU.mult, ALU.mult).then_inc(gate_ready, 1)
                dve.wait_ge(gate_ready, t + 1)
                V.tensor_copy(gate16[:], gate2[:, 0, :]).then_inc(gate16_ready, 1)
                dve.wait_ge(gate16_ready, t + 1)
                V.tensor_tensor(gate2[:, 1, :], gate2[:, 0, :], gate16[:], ALU.subtract).then_inc(gate2_ready, 1)

            def one_hots(t, first=False):
                dve.wait_ge(picks_copied, t + 1)
                for m in range(3):
                    last = V.tensor_scalar(loT[:, m, :], picksT[:, 0, :], -32.0 * (m + 1), None, ALU.add)
                last.then_inc(lot_ready, 1)
                if not first:
                    dve.wait_ge(gate_mm, t * NTG)
                V.tensor_tensor(gated_hi[:], iota32[:], spread(picksT[:, 1, :], 1, EC), ALU.is_equal).then_inc(hi_hot, 1)
                dve.wait_ge(lot_ready, t + 1)
                for m in range(4):
                    src = picksT[:, 0, :] if m == 0 else loT[:, m - 1, :]
                    last = V.tensor_tensor(onehot_lo[:, 32 * m:32 * m + 32, :], iota32[:], spread(src, 1, EC), ALU.is_equal)
                last.then_inc(lo_hot, 1)
                dve.wait_ge(hi_hot, t + 1)
                V.tensor_tensor(gated_hi[:], gated_hi[:], spread(picksT[:, 2, :], 1, EC), ALU.mult).then_inc(gated, 1)

            def gate_hidden(t):
                dve.wait_ge(gelu_ready, (t + 1) * NHG)
                for k in range(NTG):
                    dve.wait_ge(gate_mm, t * NTG + k + 1)
                    h = act_h[:, ds(t % 2, 1), :, k * TG:(k + 1) * TG].rearrange("p o c t -> p (o c) t")
                    V.scalar_tensor_tensor(h, ps[:, 2 + k % 4, :].rearrange("p (t c) -> p c t", c=EC), 1.0 / GATE_SCALE, h,
                                           ALU.mult, ALU.mult).then_inc(acts_ready, 1)

            dve.wait_ge(top_kept, NC2)
            dve.wait_ge(iota_ready, 1)
            choose(0, first=True)
            one_hots(0, first=True)
            gate_hidden(0)
            choose(1)
            one_hots(1)
            with dve.Fori(1, NT - 1) as t:
                gate_hidden(t)
                choose(t + 1)
                one_hots(t + 1)
            gate_hidden(NT - 1)

        @block.gpsimd
        def _(pool):
            P = nc.gpsimd
            NQK = HEADS + KV_HEADS + 1

            def inverse_roots(g, first=False):
                pool.wait_ge(rmsv_ready, g + 1)
                if not first:
                    pool.wait_ge(v_ready, g)
                    pool.wait_ge(qkn_ready, g)
                P.tensor_tensor(rinv[:], rmsv[:], half_neg[0:GT, 0:NQK], ALU.pow).then_inc(rinv_ready, 1)

            def normalise_p(g, first=False):
                pool.wait_ge(pinv_ready, g + 1)
                if not first:
                    pool.wait_ge(pt_ready, g)
                P.tensor_tensor(pn[:], sm[:].rearrange("p a b k -> p (a b) k"), spread(pinv[:], 2, GT), ALU.mult).then_inc(pn_ready, 1)

            def current_v(g, first=False):
                pool.wait_ge(v_ready, g + 1)
                if not first:
                    pool.wait_ge(o_ready, g)
                P.tensor_copy(vcur[:], vall[:, ds(g, 1), :].rearrange("p o n -> p (o n)")).then_inc(vcur_ready, 1)

            P.memset(mean_w[:], 1.0 / DIM)
            P.memset(half_neg[:], -0.5)
            P.memset(eps_ln[:], LN_EPS)
            P.memset(hT[:, :, TOK:PAD_TOK], 0.0).then_inc(const_ready, 1)
            pool.wait_ge(const_ready, 1)
            inverse_roots(0, first=True)
            inverse_roots(1)
            normalise_p(0, first=True)
            current_v(0, first=True)
            with pool.Fori(1, NG - 1) as i:
                inverse_roots(i + 1)
                normalise_p(i)
                current_v(i)
            normalise_p(NG - 1)
            current_v(NG - 1)

            pool.wait_ge(h2_ready, NG)
            P.iota(iota8[:], [[1, TOPK]], base=0, channel_multiplier=0, allow_small_or_imprecise_dtypes=True)
            P.iota(iota32[:], [[1, EC], [0, 128]], base=0, channel_multiplier=0, allow_small_or_imprecise_dtypes=True).then_inc(iota_ready, 1)

            def batch_root(c):
                pool.wait_ge(bnv_ready, c + 1)
                P.tensor_tensor(rstd[:], bnv[:], half_neg[:, 0:1], ALU.pow).then_inc(rstd_ready, 1)

            def keep_top(c, s):
                pool.wait_ge(topi_ready, c + 1)
                P.tensor_copy(top_s[:, :, ds(c, 1), :].rearrange("p t o k -> p t (o k)"), best_s[:, s])
                P.tensor_copy(top_i[:, :, ds(c, 1), :].rearrange("p t o k -> p t (o k)"), best_i[:, s]).then_inc(top_kept, 1)

            batch_root(0)
            batch_root(1)
            keep_top(0, 0)
            batch_root(2)
            keep_top(1, 1)
            with pool.Fori(1, NC2 // 2 - 1) as j:
                batch_root(2 * j + 1)
                keep_top(2 * j, 0)
                batch_root(2 * j + 2)
                keep_top(2 * j + 1, 1)
            batch_root(NC2 - 1)
            keep_top(NC2 - 2, 0)
            keep_top(NC2 - 1, 1)

            def final_sum(t, s, wait_store):
                pool.wait_ge(up_copied, t + 1)
                if wait_store is not None:
                    pool.wait_ge(stored[s], wait_store)
                P.tensor_tensor(outs[:, s], upout[:], hT[:, :, ds(t * 128, 128)], ALU.add).then_inc(sum_ready, 1)

            for t in range(NT):
                final_sum(t, t % 2, 16 * (t // 2) if t >= 2 else None)


def kernel(**inputs):
    import numpy as np
    import concourse.bacc as bacc
    from concourse import mybir
    from concourse.bass_utils import run_bass_kernel_spmd

    f = np.float32
    a = {k: np.asarray(v) for k, v in inputs.items()}
    side = 6
    x = a["x"].reshape(IMAGES, 3, side, 16, side, 16).transpose(1, 3, 5, 0, 2, 4).reshape(KC, 128, TOK)

    def rows(w, chunks):
        return w.reshape(chunks, 128, -1).transpose(1, 0, 2)

    q, k = np.arange(GT)[:, None], np.arange(GT)[None, :]
    rel = (k - q).astype(f)
    hidden = (k > q) | (k < q - 16) | (k // PATCHES != q // PATCHES)
    slopes = (2.0 ** -0.5) ** np.arange(1, HEADS + 1, dtype=f)
    table = np.where(hidden[None], f(-1e30), slopes[:, None, None].astype(f) * rel[None]).astype(f)
    table = table.reshape(REP, KV_HEADS, GT, GT).transpose(2, 1, 0, 3)

    arrays = {
        "x_t": x,
        "tok_w": rows(a["L0_tok_W"].T, KC),
        "tok_b": a["L0_tok_b"].reshape(FC, 128).T,
        "pos": rows(a["L0_tok_pos_embd"].reshape(PATCHES, DIM).T, FC),
        "ident": np.eye(128, dtype=f),
        "bias": table,
        "wq": rows(a["L0_attn_wq"].T, FC),
        "wkv": rows(np.concatenate([a["L0_attn_wk"].T, a["L0_attn_wv"].T], axis=1), FC),
        "wo": rows(a["L0_attn_wo"].T, QC),
        "qw": np.concatenate([a["L0_attn_q_norm_w"]] * 2).reshape(128, 1),
        "kw": np.concatenate([a["L0_attn_k_norm_w"]] * 2).reshape(128, 1),
        "ffn_wq": a["L0_ffn_w_q"].reshape(FC, 128, NC2, KD).transpose(2, 1, 0, 3),
        "gamma": a["L0_ffn_bn_gamma"].reshape(NC2, 128).T,
        "beta": a["L0_ffn_bn_beta"].reshape(NC2, 128).T,
        "keys": a["L0_ffn_keys"].transpose(3, 2, 0, 1).reshape(KD, NC2, KEYS),
        "down": rows(a["L0_ffn_down_embed"].T, FC),
        "up": rows(a["L0_ffn_up_embed"], EC),
    }
    arrays = {n: np.ascontiguousarray(v) for n, v in arrays.items()}
    nc = bacc.Bacc("TRN2", target_bir_lowering=False, num_devices=1)
    args = [nc.dram_tensor("in_" + n, v.shape, mybir.dt.from_np(v.dtype), kind="ExternalInput").ap() for n, v in arrays.items()]
    out = nc.dram_tensor("out", (128, FC, TOK), mybir.dt.float32, kind="ExternalOutput").ap()
    vit_block(nc, *args, out)
    r = run_bass_kernel_spmd(nc, [{"in_" + n: v for n, v in arrays.items()}], core_ids=[0])
    return r.results[0]["out"].transpose(2, 1, 0).reshape(IMAGES, PATCHES, DIM)
```

```python
import concourse.bass as bass
from concourse import mybir
from contextlib import ExitStack

IMAGES = 32
PATCHES = 36
TOK = IMAGES * PATCHES
DIM = 256
FC = DIM // 128
PATCH_DIM = 768
KC = PATCH_DIM // 128
HEADS, KV_HEADS, HD = 16, 4, 64
REP = HEADS // KV_HEADS
QC = HEADS * HD // 128
GIMG = 3
GT = GIMG * PATCHES
NG = -(-IMAGES // GIMG)
PAD_TOK = NG * GT
FH, KD, KEYS, TOPK = 8, 128, 64, 8
NC2 = 2 * FH
EXPERTS = KEYS * KEYS
EC = EXPERTS // 128
NT = TOK // 128
BLK = 384
NB = TOK // BLK
TG = 16
NTG = 128 // TG
HG = 4
NHG = EC // HG
RMS_EPS = 0.01
LN_EPS = 1e-5
GATE_SCALE = 4096.0


def vit_block(nc, x_t, tok_w, tok_b, pos, ident_in, bias_in, wq_in, wkv_in, wo_in, qw_in, kw_in,
              ffn_wq, gamma_in, beta_in, keys_in, down_in, up_in, out):
    fp32 = mybir.dt.float32
    fp16 = mybir.dt.float16
    u32 = mybir.dt.uint32
    i32 = mybir.dt.int32
    ALU = mybir.AluOpType
    ACT = mybir.ActivationFunctionType
    AX = mybir.AxisListType
    ds = bass.ds

    ctx = ExitStack()
    with ctx:
        def sb(name, shape, dt, scope=ctx):
            return scope.enter_context(nc.sbuf_tensor(name, shape, dt))

        def sem(name):
            return ctx.enter_context(nc.semaphore(name))

        def spread(ap, axis, n):
            v = ap.unsqueeze(axis)
            shape = list(v.shape)
            shape[axis] = n
            return v.broadcast_to(shape)

        hT = sb("hT", [128, FC, PAD_TOK], fp32)
        xnT = sb("xnT", [128, FC, TOK], fp32)
        downT = sb("downT", [128, FC, EXPERTS], fp32)
        up = sb("up", [128, EC, DIM], fp32)
        ident = sb("ident", [128, 128], fp32)
        mean_w = sb("mean_w", [128, 128], fp32)
        gamma = sb("gamma", [128, NC2], fp32)
        beta = sb("beta", [128, NC2], fp32)
        half_neg = sb("half_neg", [128, HEADS + KV_HEADS + 1], fp32)
        eps_ln = sb("eps_ln", [128, 1], fp32)

        p1 = ExitStack()
        xT = sb("xT", [128, KC, TOK], fp32, p1)
        tokw = sb("tokw", [128, KC, DIM], fp32, p1)
        posb = sb("posb", [128, FC, PATCHES], fp32, p1)
        tokb = sb("tokb", [128, FC], fp32, p1)
        wq = sb("wq", [128, FC, HEADS * HD], fp32, p1)
        wkv = sb("wkv", [128, FC, 2 * KV_HEADS * HD], fp32, p1)
        wo = sb("wo", [128, QC, DIM], fp32, p1)
        qw = sb("qw", [128, 1], fp32, p1)
        kw = sb("kw", [128, 1], fp32, p1)
        kscale = sb("kscale", [128, 1], fp32, p1)
        bias = sb("bias", [GT, KV_HEADS, REP, GT], fp32, p1)
        d1 = sb("d1", [128, FC, GT], fp32, p1)
        sq1 = sb("sq1", [128, FC, GT], fp32, p1)
        sqq = sb("sqq", [GT, HEADS + KV_HEADS, HD], fp32, p1)
        msum = sb("msum", [GT, HEADS + KV_HEADS], fp32, p1)
        rmsv = sb("rmsv", [GT, HEADS + KV_HEADS + 1], fp32, p1)
        vare = sb("vare", [GT, 1], fp32, p1)
        rinv = sb("rinv", [GT, HEADS + KV_HEADS + 1], fp32, p1)
        qkn = sb("qkn", [GT, HEADS + KV_HEADS, HD], fp32, p1)
        qT = sb("qT", [128, QC, GT], fp32, p1)
        kT = sb("kT", [128, KV_HEADS // 2, GT], fp32, p1)
        vall = sb("vall", [GT, NG, KV_HEADS * HD], fp32, p1)
        vcur = sb("vcur", [GT, KV_HEADS * HD], fp32, p1)
        sm = sb("sm", [GT, KV_HEADS, REP, GT], fp32, p1)
        nmax = sb("nmax", [GT, KV_HEADS, REP], fp32, p1)
        psums = sb("psums", [GT, HEADS], fp32, p1)
        pinv = sb("pinv", [GT, HEADS], fp32, p1)
        pn = sb("pn", [GT, HEADS, GT], fp32, p1)
        pT = sb("pT", [GT, KV_HEADS, REP, GT], fp32, p1)
        oT = sb("oT", [128, QC, GT], fp32, p1)
        p1.close()

        p2 = ctx
        stats = sb("stats", [128, NB, 6], fp32, p2)
        mv = sb("mv", [128, 2], fp32, p2)
        bnv = sb("bnv", [128, 1], fp32, p2)
        rstd = sb("rstd", [128, 1], fp32, p2)
        bna = sb("bna", [128, 2], fp32, p2)
        bnb = sb("bnb", [128, 2], fp32, p2)
        bnm = sb("bnm", [128, 1], fp32, p2)
        top_s = sb("top_s", [128, NT, NC2, TOPK], fp32, p2)
        top_i = sb("top_i", [128, NT, NC2, TOPK], fp32, p2)
        best_s = sb("best_s", [128, 2, NT, TOPK], fp32, p2)
        best_i = sb("best_i", [128, 2, NT, TOPK], u32, p2)
        comb = sb("comb", [128, FH, TOPK, TOPK], fp32, p2)
        best = sb("best", [128, FH, TOPK], fp32, p2)
        pick = sb("pick", [128, FH, TOPK], u32, p2)
        pick_a = sb("pick_a", [128, FH, TOPK], i32, p2)
        pick_b = sb("pick_b", [128, FH, TOPK], i32, p2)
        iota8 = sb("iota8", [128, TOPK], fp32, p2)
        mask_a = sb("mask_a", [128, FH, TOPK, TOPK], fp32, p2)
        mask_b = sb("mask_b", [128, FH, TOPK, TOPK], fp32, p2)
        key_i = sb("key_i", [128, FH, TOPK], fp32, p2)
        key_j = sb("key_j", [128, FH, TOPK], fp32, p2)
        expert = sb("expert", [128, FH * TOPK], i32, p2)
        e_lo = sb("e_lo", [128, FH * TOPK], i32, p2)
        e_hi = sb("e_hi", [128, FH * TOPK], i32, p2)
        lo2 = sb("lo2", [128, 2, FH * TOPK], fp32, p2)
        hi2 = sb("hi2", [128, 2, FH * TOPK], fp32, p2)
        dif = sb("dif", [128, FH, TOPK], fp32, p2)
        ex = sb("ex", [128, FH, TOPK], fp32, p2)
        zs = sb("zs", [128, FH], fp32, p2)
        zi = sb("zi", [128, FH], fp32, p2)
        gate2 = sb("gate2", [128, 2, FH * TOPK], fp32, p2)
        gate16 = sb("gate16", [128, FH * TOPK], fp16, p2)
        picksT = sb("picksT", [128, 3, 128], fp16, p2)
        loT = sb("loT", [128, 3, 128], fp16, p2)
        iota32 = sb("iota32", [128, EC, 128], fp16, p2)
        p3 = ExitStack()
        sq2 = sb("sq2", [128, FC, BLK], fp32, p3)
        root = sb("root", [128, 2, BLK], fp32, p3)
        wqc = sb("wqc", [128, 2, FC, KD], fp32, p3)
        keysT = sb("keysT", [128, NC2, KEYS], fp32, p3)
        qb = sb("qb", [128, 2, TOK], fp32, p3)
        sims = sb("sims", [128, 2, NT, KEYS], fp32, p3)
        p3.close()
        onehot_lo = sb("onehot_lo", [128, 128, 128], fp16, p2)
        gated_hi = sb("gated_hi", [128, EC, 128], fp16, p2)
        act_h = sb("act_h", [128, 2, EC, 128], fp32, p2)
        upout = sb("upout", [128, FC, 128], fp32, p2)
        outs = sb("outs", [128, FC, 128], fp32, p2)

        ps = ctx.enter_context(nc.psum_tensor("ps", [128, 8, 512], fp32))

        QK_PARTS = ((1, 0, 8), (2, 8, 8), (3, 16, 4))

        ld_x = [sem(f"ld_x{k}") for k in range(KC)]
        ld_tokw = [sem(f"ld_tokw{k}") for k in range(KC)]
        ld_pos, ld_tokb, ld_ident, ld_bias = (sem(n) for n in ("ld_pos", "ld_tokb", "ld_ident", "ld_bias"))
        ld_wq, ld_wkv, ld_wo, ld_qw, ld_kw = (sem(n) for n in ("ld_wq", "ld_wkv", "ld_wo", "ld_qw", "ld_kw"))
        ld_gamma, ld_beta, ld_keys, ld_down, ld_up = (sem(n) for n in ("ld_gamma", "ld_beta", "ld_keys", "ld_down", "ld_up"))
        ld_wqc = [sem(f"ld_wqc{s}") for s in range(2)]
        const_ready, iota_ready = sem("const_ready"), sem("iota_ready")
        embedded, posb_ready, h_ready = sem("embedded"), sem("posb_ready"), sem("h_ready")
        kscale_ready = sem("kscale_ready")
        mean_ready, d_ready, sq_ready, var_ready = sem("mean_ready"), sem("d_ready"), sem("sq_ready"), sem("var_ready")
        q0_ready, q1_ready, kv_ready = sem("q0_ready"), sem("q1_ready"), sem("kv_ready")
        sqq_ready = [sem(f"sqq_ready{n}") for n in range(3)]
        msum_ready, vare_ready = sem("msum_ready"), sem("vare_ready")
        rmsv_ready, rinv_ready, v_ready, qkn_ready = sem("rmsv_ready"), sem("rinv_ready"), sem("v_ready"), sem("qkn_ready")
        qkt_ready, qkt_copied = sem("qkt_ready"), sem("qkt_copied")
        score_ready = [sem(f"score_ready{g}") for g in range(KV_HEADS)]
        biased = [sem(f"biased{g}") for g in range(KV_HEADS)]
        max_ready = [sem(f"max_ready{g}") for g in range(KV_HEADS)]
        exp_ready, pinv_ready, pn_ready, vcur_ready = sem("exp_ready"), sem("pinv_ready"), sem("pn_ready"), sem("vcur_ready")
        pt_ready, pt_copied_act, pt_copied_dve = sem("pt_ready"), sem("pt_copied_act"), sem("pt_copied_dve")
        o_ready, o_copied_act, o_copied_dve = sem("o_ready"), sem("o_copied_act"), sem("o_copied_dve")
        wo_ready, h2_ready = sem("wo_ready"), sem("h2_ready")
        mean2_ready, d2_ready, sq2_ready, var2_ready = sem("mean2_ready"), sem("d2_ready"), sem("sq2_ready"), sem("var2_ready")
        root_ready, rroot_ready, xn_ready = sem("root_ready"), sem("rroot_ready"), sem("xn_ready")
        fq_ready, stats_ready, mv_ready, bnv_ready, rstd_ready = (sem(n) for n in ("fq_ready", "stats_ready", "mv_ready", "bnv_ready", "rstd_ready"))
        bna_ready, bnm_ready, bnb_ready, qb_ready = (sem(n) for n in ("bna_ready", "bnm_ready", "bnb_ready", "qb_ready"))
        sim_ready, sim_copied, tops_ready, topi_ready = (sem(n) for n in ("sim_ready", "sim_copied", "tops_ready", "topi_ready"))
        top_kept = sem("top_kept")
        comb_ready, best_ready, pick_ready, dif_ready, ex_ready = (sem(n) for n in ("comb_ready", "best_ready", "pick_ready", "dif_ready", "ex_ready"))
        zs_ready, zi_ready, gate_ready, gate16_ready, gate2_ready = (sem(n) for n in ("zs_ready", "zi_ready", "gate_ready", "gate16_ready", "gate2_ready"))
        pickab_ready, mask_ready, masked_ready, key_ready = (sem(n) for n in ("pickab_ready", "mask_ready", "masked_ready", "key_ready"))
        expert_ready, elohi_ready, lohi2_ready = (sem(n) for n in ("expert_ready", "elohi_ready", "lohi2_ready"))
        picks_tr, picks_copied, lot_ready, lo_hot, hi_hot, gated = (sem(n) for n in ("picks_tr", "picks_copied", "lot_ready", "lo_hot", "hi_hot", "gated"))
        down_ready, gelu_ready, gate_mm, acts_ready = (sem(n) for n in ("down_ready", "gelu_ready", "gate_mm", "acts_ready"))
        up_ready, up_copied, sum_ready = sem("up_ready"), sem("up_copied"), sem("sum_ready")
        stored = sem("stored")

        block = ctx.enter_context(nc.Block())

        blocks1 = [(0, 432), (432, 432), (864, 288)]

        @block.sync
        def _(sp):
            for k in range(KC):
                sp.dma_start(tokw[:, k, :], tok_w[:, k, :]).then_inc(ld_tokw[k], 16)
                sp.dma_start(xT[:, k, :], x_t[k]).then_inc(ld_x[k], 16)
            sp.dma_start(bias[:], bias_in).then_inc(ld_bias, 16)
            sp.dma_start(wo[:], wo_in).then_inc(ld_wo, 16)
            sp.dma_start(downT[:], down_in).then_inc(ld_down, 16)
            sp.dma_start(up[:], up_in).then_inc(ld_up, 16)
            sp.dma_start(gamma[:], gamma_in).then_inc(ld_gamma, 16)
            sp.dma_start(beta[:], beta_in).then_inc(ld_beta, 16)
            sp.wait_ge(h2_ready, NG)
            sp.dma_start(wqc[:, 0], ffn_wq[0]).then_inc(ld_wqc[0], 16)
            sp.dma_start(wqc[:, 1], ffn_wq[1]).then_inc(ld_wqc[1], 16)
            sp.dma_start(keysT[:], keys_in).then_inc(ld_keys, 16)
            with sp.Fori(1, NC2 // 2) as j:
                for s in range(2):
                    sp.wait_ge(fq_ready, 2 * j + s - 1)
                    sp.dma_start(wqc[:, s], ffn_wq[ds(2 * j + s, 1)].rearrange("o p f n -> p (o f) n")).then_inc(ld_wqc[s], 16)
            with sp.Fori(0, NT) as t:
                sp.wait_ge(sum_ready, t + 1)
                sp.dma_start(out[:, :, ds(t * 128, 128)], outs[:]).then_inc(stored, 16)
            sp.wait_ge(stored, 16 * NT)

        @block.tensor
        def _(pe):
            mm = nc.tensor.matmul

            def mean_of_group(g, first=False):
                if not first:
                    pe.wait_ge(d_ready, g)
                    pe.wait_ge(vare_ready, g)
                for f in range(FC):
                    last = mm(ps[:, 0, 0:GT], mean_w[:], hT[:, f, ds(g * GT, GT)], start=f == 0, stop=f == FC - 1)
                last.then_inc(mean_ready, 1)

            def variance_of_group(g):
                pe.wait_ge(sq_ready, g + 1)
                for f in range(FC):
                    last = mm(ps[0:GT, 0, 256:257], sq1[:, f, :], mean_w[:, 0:1], start=f == 0, stop=f == FC - 1)
                last.then_inc(var_ready, 1)

            def project(bank, w, c0, done):
                for f in range(FC):
                    last = mm(ps[0:GT, bank, :], d1[:, f, :], w[:, f, c0:c0 + 512], start=f == 0, stop=f == FC - 1)
                last.then_inc(done, 1)

            def transpose_qk(g, free=None):
                pe.wait_ge(qkn_ready, g + 1)
                if free is not None:
                    pe.wait_ge(o_copied_act, free)
                    pe.wait_ge(o_copied_dve, free)
                flat = qkn[:].rearrange("p h d -> p (h d)")
                for c in range(QC + KV_HEADS // 2):
                    last = nc.tensor.transpose(ps[:, (4, 5, 7)[c // 4], (c % 4) * GT:(c % 4 + 1) * GT],
                                               flat[:, c * 128:(c + 1) * 128], ident[0:GT, 0:GT])
                last.then_inc(qkt_ready, 1)

            def score_group(g, free=None):
                pe.wait_ge(qkt_copied, g + 1)
                for kv in (0, 1, 3, 2):
                    if kv == 2 and free is not None:
                        pe.wait_ge(h2_ready, free)
                    r0 = 64 * (kv % 2)
                    for i in range(REP):
                        h = kv + KV_HEADS * i
                        last = mm(ps[0:GT, 4 + kv, i * GT:(i + 1) * GT], qT[r0:r0 + 64, h // 2, :],
                                  kT[r0:r0 + 64, kv // 2, :], start=True, stop=True)
                    last.then_inc(score_ready[kv], 1)

            def transpose_p(g, next_scores=True):
                pe.wait_ge(pn_ready, g + 1)
                if not next_scores:
                    pe.wait_ge(o_copied_act, g)
                    pe.wait_ge(o_copied_dve, g)
                    pe.wait_ge(h2_ready, g)
                for kv in (0, 1, 3, 2):
                    if next_scores:
                        pe.wait_ge(biased[kv], g + 2)
                    for i in range(REP):
                        last = nc.tensor.transpose(ps[0:GT, 4 + kv, i * GT:(i + 1) * GT], pn[:, REP * kv + i, :],
                                                   ident[0:GT, 0:GT])
                    last.then_inc(pt_ready, 1)

            def attend_group(g):
                pe.wait_ge(vcur_ready, g + 1)
                pe.wait_ge(pt_copied_act, g + 1)
                for kv in range(KV_HEADS):
                    if kv == 2:
                        pe.wait_ge(pt_copied_dve, g + 1)
                    r0 = 64 * (kv % 2)
                    last = mm(ps[r0:r0 + 64, 4 + kv // 2, 0:REP * GT], vcur[:, kv * HD:(kv + 1) * HD],
                              pT[:, kv].rearrange("p i q -> p (i q)"), start=True, stop=True)
                    if kv % 2:
                        last.then_inc(o_ready, 1)
                pe.wait_ge(o_copied_act, g + 1)
                for f in range(FC):
                    for n, c in enumerate((0, 2, 4, 6, 1, 3, 5, 7)):
                        if f == 0 and n == 4:
                            pe.wait_ge(o_copied_dve, g + 1)
                        last = mm(ps[:, 6, f * GT:(f + 1) * GT], wo[:, c, f * 128:(f + 1) * 128], oT[:, c, :],
                                  start=n == 0, stop=n == QC - 1)
                last.then_inc(wo_ready, 1)

            for k in range(KC):
                pe.wait_ge(ld_tokw[k], 16)
                pe.wait_ge(ld_x[k], 16)
                for b, (t0, n) in enumerate(blocks1):
                    for f in range(FC):
                        last = mm(ps[:, 2 * b + f, 0:n], tokw[:, k, f * 128:(f + 1) * 128], xT[:, k, t0:t0 + n],
                                  start=k == 0, stop=k == KC - 1)
                        if k == KC - 1:
                            last.then_inc(embedded, 1)

            pe.wait_ge(const_ready, 1)
            pe.wait_ge(h_ready, FC * len(blocks1))
            pe.wait_ge(ld_ident, 16)
            pe.wait_ge(ld_wq, 16)
            pe.wait_ge(ld_wkv, 16)
            mean_of_group(0, first=True)
            variance_of_group(0)
            project(1, wq, 0, q0_ready)
            project(2, wq, 512, q1_ready)
            project(3, wkv, 0, kv_ready)
            mean_of_group(1)
            transpose_qk(0)
            variance_of_group(1)
            project(1, wq, 0, q0_ready)
            score_group(0)
            project(2, wq, 512, q1_ready)
            project(3, wkv, 0, kv_ready)
            mean_of_group(2)
            pe.wait_ge(ld_wo, 16)

            def attention_step(i, first=False, projections=True, means=True):
                if first:
                    for kv in range(KV_HEADS):
                        pe.wait_ge(biased[kv], 1)
                transpose_qk(i + 1, None if first else i)
                if projections:
                    variance_of_group(i + 2)
                    project(1, wq, 0, q0_ready)
                score_group(i + 1, None if first else i)
                if projections:
                    project(2, wq, 512, q1_ready)
                    project(3, wkv, 0, kv_ready)
                transpose_p(i)
                if means:
                    mean_of_group(i + 3)
                attend_group(i)

            attention_step(0, first=True)
            with pe.Fori(1, NG - 3) as i:
                attention_step(i)
            attention_step(NG - 3, means=False)
            attention_step(NG - 2, projections=False, means=False)
            transpose_p(NG - 1, next_scores=False)
            attend_group(NG - 1)

            for b in range(NB):
                pe.wait_ge(h2_ready, NG)
                for f in range(FC):
                    last = mm(ps[:, b, 0:BLK], mean_w[:], hT[:, f, b * BLK:(b + 1) * BLK], start=f == 0, stop=f == FC - 1)
                last.then_inc(mean2_ready, 1)
            for b in range(NB):
                pe.wait_ge(sq2_ready, b + 1)
                for f in range(FC):
                    last = mm(ps[:, 3 + b, 0:BLK], mean_w[:], sq2[:, f, :], start=f == 0, stop=f == FC - 1)
                last.then_inc(var2_ready, 1)

            def router_q(c, s, load, first=False):
                pe.wait_ge(ld_wqc[s], load)
                if not first:
                    pe.wait_ge(qb_ready, c - 1)
                for b in range(NB):
                    for f in range(FC):
                        last = mm(ps[:, 3 * s + b, 0:BLK], wqc[:, s, f, :], xnT[:, f, b * BLK:(b + 1) * BLK],
                                  start=f == 0, stop=f == FC - 1)
                last.then_inc(fq_ready, 1)

            def router_sim(c, s, first=False):
                pe.wait_ge(qb_ready, c + 1)
                if not first:
                    pe.wait_ge(sim_copied, c)
                for t in range(NT):
                    last = mm(ps[:, 6 + t // 8, (t % 8) * KEYS:(t % 8 + 1) * KEYS], qb[:, s, t * 128:(t + 1) * 128],
                              keysT[:, ds(c, 1), :].rearrange("p o k -> p (o k)"), start=True, stop=True)
                last.then_inc(sim_ready, 1)

            pe.wait_ge(xn_ready, NB)
            router_q(0, 0, 16, first=True)
            router_q(1, 1, 16, first=True)
            pe.wait_ge(ld_keys, 16)
            router_sim(0, 0, first=True)
            router_q(2, 0, 32)
            router_sim(1, 1)
            with pe.Fori(1, NC2 // 2 - 1) as j:
                router_q(2 * j + 1, 1, 16 * j + 16)
                router_sim(2 * j, 0)
                router_q(2 * j + 2, 0, 16 * j + 32)
                router_sim(2 * j + 1, 1)
            router_q(NC2 - 1, 1, 16 * (NC2 // 2))
            router_sim(NC2 - 2, 0)
            router_sim(NC2 - 1, 1)

            def down_products(t, picks=None):
                for k in range(NHG):
                    if k == 0 and picks is not None:
                        pe.wait_ge(picks_copied, picks)
                    if picks is not None or k > 1:
                        pe.wait_ge(gelu_ready, t * NHG + k - 1)
                    for i in range(HG):
                        c = HG * k + i
                        for f in range(FC):
                            last = mm(ps[:, k % 2, i * 128:(i + 1) * 128], downT[:, f, c * 128:(c + 1) * 128],
                                      xnT[:, f, ds(t * 128, 128)], start=f == 0, stop=f == FC - 1)
                    last.then_inc(down_ready, 1)

            def transpose_picks(t, hidden):
                pe.wait_ge(gelu_ready, hidden * NHG)
                pe.wait_ge(lohi2_ready, t + 1)
                pe.wait_ge(gate2_ready, t + 1)
                for n, a in enumerate((lo2, hi2, gate2)):
                    last = nc.tensor.transpose(ps[:, 0, n * 128:(n + 1) * 128], a[:].rearrange("p a b -> p (a b)"), ident[:])
                last.then_inc(picks_tr, 1)

            def gate_matrices(t, first=False):
                pe.wait_ge(lo_hot, t + 1)
                pe.wait_ge(gated, t + 1)
                for k in range(NTG):
                    if not (first and k < 4):
                        pe.wait_ge(acts_ready, t * NTG + k - 3)
                    for n in range(TG):
                        tok = k * TG + n
                        last = mm(ps[:, 2 + k % 4, n * EC:(n + 1) * EC], onehot_lo[:, :, tok], gated_hi[:, :, tok],
                                  start=True, stop=True)
                    last.then_inc(gate_mm, 1)

            def up_product(t, first=False):
                pe.wait_ge(acts_ready, (t + 1) * NTG)
                if not first:
                    pe.wait_ge(up_copied, t)
                for c in range(EC):
                    for f in range(FC):
                        last = mm(ps[:, 6 + f, 0:128], up[:, c, f * 128:(f + 1) * 128],
                                  act_h[:, ds(t % 2, 1), c, :].rearrange("p o t -> p (o t)"), start=c == 0, stop=c == EC - 1)
                last.then_inc(up_ready, 1)

            pe.wait_ge(ld_down, 16)
            pe.wait_ge(ld_up, 16)
            pe.wait_ge(sim_copied, NC2)
            down_products(0)
            transpose_picks(0, 1)
            down_products(1, picks=1)
            gate_matrices(0, first=True)
            transpose_picks(1, 2)
            up_product(0, first=True)
            gate_matrices(1)
            transpose_picks(2, 2)
            down_products(2, picks=3)
            with pe.Fori(2, NT - 1) as t:
                gate_matrices(t)
                transpose_picks(t + 1, t + 1)
                up_product(t - 1)
                down_products(t + 1, picks=t + 2)
            gate_matrices(NT - 1)
            up_product(NT - 2)
            up_product(NT - 1)

        @block.scalar
        def _(act):
            A = nc.scalar.activation
            act.dma_start(posb[:], pos).then_inc(ld_pos, 16)
            act.dma_start(tokb[:], tok_b).then_inc(ld_tokb, 16)
            act.dma_start(ident[:], ident_in).then_inc(ld_ident, 16)
            act.dma_start(qw[:], qw_in).then_inc(ld_qw, 16)
            act.dma_start(kw[:], kw_in).then_inc(ld_kw, 16)
            act.dma_start(wq[:], wq_in).then_inc(ld_wq, 16)
            act.dma_start(wkv[:], wkv_in).then_inc(ld_wkv, 16)

            def square_d(g, first=False):
                act.wait_ge(d_ready, g + 1)
                if not first:
                    act.wait_ge(var_ready, g)
                A(sq1[:], d1[:], ACT.Square).then_inc(sq_ready, 1)

            def square_qk(g, part, first=False):
                bank, h0, n = QK_PARTS[part]
                if not first:
                    act.wait_ge(msum_ready, g * 3)
                act.wait_ge((q0_ready, q1_ready, kv_ready)[part], g + 1)
                A(sqq[:, h0:h0 + n, :].rearrange("p h d -> p (h d)"), ps[0:GT, bank, 0:n * HD],
                  ACT.Square).then_inc(sqq_ready[part], 1)

            def copy_v(g):
                act.wait_ge(rinv_ready, g + 1)
                A(vall[:, ds(g, 1), :].rearrange("p o n -> p (o n)"), ps[0:GT, 3, 256:512], ACT.Copy,
                  scale=rinv[:, HEADS + KV_HEADS:HEADS + KV_HEADS + 1]).then_inc(v_ready, 1)

            def copy_qk(g, first=False):
                act.wait_ge(qkt_ready, g + 1)
                if not first:
                    act.wait_ge(score_ready[2], g)
                for n in range(2):
                    A(qT[:, 4 * n:4 * n + 4, :], ps[:, 4 + n, 0:4 * GT].rearrange("p (c t) -> p c t", t=GT), ACT.Copy)
                A(kT[:], ps[:, 7, 0:2 * GT].rearrange("p (c t) -> p c t", t=GT), ACT.Copy,
                  scale=kscale[:, 0:1]).then_inc(qkt_copied, 1)

            def exps(g, kv):
                act.wait_ge(max_ready[kv], g + 1)
                for i in range(REP):
                    last = A(sm[:, kv, i, :], sm[:, kv, i, :], ACT.Exp, bias=nmax[:, kv, i:i + 1],
                             accum_out=psums[:, REP * kv + i:REP * kv + i + 1])
                last.then_inc(exp_ready, 1)

            def copy_pt(g):
                act.wait_ge(pt_ready, g * KV_HEADS + 2)
                for kv in range(2):
                    last = A(pT[:, kv].rearrange("p i q -> p (i q)"), ps[0:GT, 4 + kv, 0:REP * GT], ACT.Copy)
                last.then_inc(pt_copied_act, 1)

            def copy_o(g):
                act.wait_ge(o_ready, g * 2 + 1)
                A(oT[:, 0:QC:2, :], ps[:, 4, 0:REP * GT].rearrange("p (c t) -> p c t", t=GT), ACT.Copy).then_inc(o_copied_act, 1)

            act.wait_ge(kscale_ready, 1)
            square_d(0, first=True)
            for part in range(3):
                square_qk(0, part, first=True)
            square_d(1)
            copy_v(0)
            copy_qk(0, first=True)
            square_qk(1, 0)
            exps(0, 0)
            exps(0, 1)
            square_qk(1, 1)
            exps(0, 3)
            square_qk(1, 2)
            exps(0, 2)
            square_d(2)
            copy_v(1)

            def attention_step(i, projections=True, means=True):
                copy_qk(i + 1)
                if projections:
                    square_qk(i + 2, 0)
                exps(i + 1, 0)
                exps(i + 1, 1)
                if projections:
                    square_qk(i + 2, 1)
                exps(i + 1, 3)
                if projections:
                    square_qk(i + 2, 2)
                copy_pt(i)
                exps(i + 1, 2)
                if means:
                    square_d(i + 3)
                copy_o(i)
                if projections:
                    copy_v(i + 2)

            with act.Fori(0, NG - 3) as i:
                attention_step(i)
            attention_step(NG - 3, means=False)
            attention_step(NG - 2, projections=False, means=False)
            copy_pt(NG - 1)
            copy_o(NG - 1)

            for b in range(NB):
                act.wait_ge(d2_ready, b + 1)
                if b:
                    act.wait_ge(var2_ready, b)
                A(sq2[:], xnT[:, :, b * BLK:(b + 1) * BLK], ACT.Square).then_inc(sq2_ready, 1)
                act.wait_ge(var2_ready, b + 1)
                if b > 1:
                    act.wait_ge(xn_ready, b - 1)
                A(root[:, b % 2], ps[:, 3 + b, 0:BLK], ACT.Sqrt, bias=eps_ln[:, 0:1]).then_inc(root_ready, 1)

            def affine(c, s, first=False):
                act.wait_ge(bnb_ready, c + 1)
                if not first:
                    act.wait_ge(sim_ready, c - 1)
                for b in range(NB):
                    last = A(qb[:, s, b * BLK:(b + 1) * BLK], ps[:, 3 * s + b, 0:BLK], ACT.Identity,
                             bias=bnb[:, s:s + 1], scale=bna[:, s:s + 1])
                last.then_inc(qb_ready, 1)

            def copy_sim(c, s, first=False):
                act.wait_ge(sim_ready, c + 1)
                if not first:
                    act.wait_ge(topi_ready, c - 1)
                A(sims[:, s, 0:8, :].rearrange("p t k -> p (t k)"), ps[:, 6, :], ACT.Copy)
                A(sims[:, s, 8, :], ps[:, 7, 0:KEYS], ACT.Copy).then_inc(sim_copied, 1)

            affine(0, 0, first=True)
            affine(1, 1, first=True)
            copy_sim(0, 0, first=True)
            affine(2, 0)
            copy_sim(1, 1, first=True)
            affine(3, 1)
            with act.Fori(2, NC2 // 2) as j:
                copy_sim(2 * j - 2, 0)
                affine(2 * j, 0)
                copy_sim(2 * j - 1, 1)
                affine(2 * j + 1, 1)
            copy_sim(NC2 - 2, 0)
            copy_sim(NC2 - 1, 1)

            def gelus(t):
                for k in range(NHG):
                    act.wait_ge(down_ready, t * NHG + k + 1)
                    A(act_h[:, ds(t % 2, 1), HG * k:HG * (k + 1), :].rearrange("p o c t -> p (o c t)"), ps[:, k % 2, :],
                      ACT.Gelu_apprx_tanh).then_inc(gelu_ready, 1)

            def exp_gates(t):
                act.wait_ge(dif_ready, t + 1)
                A(ex[:], dif[:], ACT.Exp).then_inc(ex_ready, 1)

            def copy_picks(t, first=False):
                act.wait_ge(picks_tr, t + 1)
                if not first:
                    act.wait_ge(gated, t)
                A(picksT[:].rearrange("p n t -> p (n t)"), ps[:, 0, 0:384], ACT.Copy).then_inc(picks_copied, 1)

            def copy_up(t, first=False):
                act.wait_ge(up_ready, t + 1)
                if not first:
                    act.wait_ge(sum_ready, t)
                for f in range(FC):
                    last = A(upout[:, f, :], ps[:, 6 + f, 0:128], ACT.Copy)
                last.then_inc(up_copied, 1)

            exp_gates(0)
            gelus(0)
            exp_gates(1)
            copy_picks(0, first=True)
            gelus(1)
            copy_picks(1)
            copy_up(0, first=True)
            exp_gates(2)
            copy_picks(2)
            exp_gates(3)
            gelus(2)
            with act.Fori(2, NT - 2) as t:
                copy_picks(t + 1)
                exp_gates(t + 2)
                copy_up(t - 1)
                gelus(t + 1)
            copy_picks(NT - 1)
            copy_up(NT - 3)
            gelus(NT - 1)
            copy_up(NT - 2)
            copy_up(NT - 1)

        @block.vector
        def _(dve):
            V = nc.vector

            def centre(g, first=False):
                dve.wait_ge(mean_ready, g + 1)
                if not first:
                    dve.wait_ge(kv_ready, g)
                    dve.wait_ge(sq_ready, g)
                V.tensor_tensor(d1[:], hT[:, :, ds(g * GT, GT)], spread(ps[:, 0, 0:GT], 1, FC), ALU.subtract).then_inc(d_ready, 1)

            def layer_norm_variance(g, first=False):
                dve.wait_ge(var_ready, g + 1)
                if not first:
                    dve.wait_ge(rinv_ready, g)
                V.tensor_scalar(rmsv[:, HEADS + KV_HEADS:], ps[0:GT, 0, 256:257], LN_EPS, None, ALU.add)
                V.tensor_scalar(vare[:], ps[0:GT, 0, 256:257], LN_EPS, RMS_EPS, ALU.add, ALU.mult).then_inc(vare_ready, 1)

            def rms_sums(g, part):
                _, h0, n = QK_PARTS[part]
                dve.wait_ge(sqq_ready[part], g + 1)
                V.reduce_sum(msum[:, h0:h0 + n], sqq[:, h0:h0 + n, :], AX.X).then_inc(msum_ready, 1)

            def rms_values(g):
                dve.wait_ge(msum_ready, g * 3 + 3)
                dve.wait_ge(vare_ready, g + 1)
                V.tensor_scalar(rmsv[:, 0:HEADS + KV_HEADS], msum[:], 1.0 / HD, vare[:, 0:1], ALU.mult, ALU.add).then_inc(rmsv_ready, 1)

            def normalise_qk(g, first=False):
                dve.wait_ge(rinv_ready, g + 1)
                if not first:
                    dve.wait_ge(qkt_ready, g)
                for bank, h0, n in QK_PARTS:
                    if bank == 3:
                        dve.wait_ge(v_ready, g + 1)
                    last = V.tensor_tensor(qkn[:, h0:h0 + n, :], ps[0:GT, bank, 0:n * HD].rearrange("p (h d) -> p h d", d=HD),
                                           spread(rinv[:, h0:h0 + n], 2, HD), ALU.mult)
                last.then_inc(qkn_ready, 1)

            def add_bias(g, kv, first=False):
                if kv == 0 and not first:
                    dve.wait_ge(pn_ready, g)
                dve.wait_ge(score_ready[kv], g + 1)
                V.tensor_tensor(sm[:, kv].rearrange("p i k -> p (i k)"), ps[0:GT, 4 + kv, 0:REP * GT],
                                bias[:, kv].rearrange("p i k -> p (i k)"), ALU.add).then_inc(biased[kv], 1)

            def neg_max(g, kv):
                dve.wait_ge(biased[kv], g + 1)
                V.reduce_max(nmax[:, kv, :], sm[:, kv], AX.X, negate=True).then_inc(max_ready[kv], 1)

            def invert_sums(g):
                dve.wait_ge(exp_ready, (g + 1) * KV_HEADS)
                V.reciprocal(pinv[:], psums[:]).then_inc(pinv_ready, 1)

            def copy_pt(g):
                dve.wait_ge(pt_ready, (g + 1) * KV_HEADS)
                for kv in range(2, KV_HEADS):
                    last = V.tensor_copy(pT[:, kv].rearrange("p i q -> p (i q)"), ps[0:GT, 4 + kv, 0:REP * GT])
                last.then_inc(pt_copied_dve, 1)

            def copy_o(g):
                dve.wait_ge(o_ready, (g + 1) * 2)
                V.tensor_copy(oT[:, 1:QC:2, :], ps[:, 5, 0:REP * GT].rearrange("p (c t) -> p c t", t=GT)).then_inc(o_copied_dve, 1)

            def residual(g):
                dve.wait_ge(wo_ready, g + 1)
                V.tensor_tensor(hT[:, :, ds(g * GT, GT)], hT[:, :, ds(g * GT, GT)],
                                ps[:, 6, 0:FC * GT].rearrange("p (f t) -> p f t", t=GT), ALU.add).then_inc(h2_ready, 1)

            dve.wait_ge(ld_pos, 16)
            dve.wait_ge(ld_tokb, 16)
            V.tensor_tensor(posb[:], posb[:], spread(tokb[:], 2, PATCHES), ALU.add).then_inc(posb_ready, 1)
            dve.wait_ge(ld_qw, 16)
            dve.wait_ge(ld_kw, 16)
            V.tensor_scalar(kscale[:], qw[:], kw[:, 0:1], HD ** -0.5, ALU.mult, ALU.mult).then_inc(kscale_ready, 1)
            dve.wait_ge(posb_ready, 1)
            for b, (t0, n) in enumerate(blocks1):
                for f in range(FC):
                    dve.wait_ge(embedded, 2 * b + f + 1)
                    V.tensor_tensor(hT[:, f, t0:t0 + n].rearrange("p (b t) -> p b t", t=PATCHES),
                                    ps[:, 2 * b + f, 0:n].rearrange("p (b t) -> p b t", t=PATCHES),
                                    spread(posb[:, f, :], 1, n // PATCHES), ALU.add).then_inc(h_ready, 1)
            dve.wait_ge(h_ready, FC * len(blocks1))
            dve.wait_ge(const_ready, 1)
            dve.wait_ge(ld_bias, 16)
            centre(0, first=True)
            layer_norm_variance(0, first=True)
            for part in range(3):
                rms_sums(0, part)
            rms_values(0)
            centre(1)
            normalise_qk(0, first=True)

            def softmax_step(g, first=False, projections=True):
                if projections:
                    layer_norm_variance(g + 1)
                add_bias(g, 0, first)
                if projections:
                    rms_sums(g + 1, 0)
                add_bias(g, 1, first)
                neg_max(g, 0)
                add_bias(g, 3, first)
                neg_max(g, 1)
                add_bias(g, 2, first)
                neg_max(g, 3)
                neg_max(g, 2)
                if projections:
                    rms_sums(g + 1, 1)
                    rms_sums(g + 1, 2)
                    rms_values(g + 1)

            softmax_step(0, first=True)
            centre(2)
            invert_sums(0)
            normalise_qk(1)

            def attention_step(i, projections=True, means=True):
                softmax_step(i + 1, projections=projections)
                copy_pt(i)
                if means:
                    centre(i + 3)
                invert_sums(i + 1)
                copy_o(i)
                if projections:
                    normalise_qk(i + 2)
                residual(i)

            with dve.Fori(0, NG - 3) as i:
                attention_step(i)
            attention_step(NG - 3, means=False)
            attention_step(NG - 2, projections=False, means=False)
            copy_pt(NG - 1)
            copy_o(NG - 1)
            residual(NG - 1)

            dve.wait_ge(h2_ready, NG)
            for b in range(NB):
                dve.wait_ge(mean2_ready, b + 1)
                V.tensor_tensor(xnT[:, :, b * BLK:(b + 1) * BLK], hT[:, :, b * BLK:(b + 1) * BLK],
                                spread(ps[:, b, 0:BLK], 1, FC), ALU.subtract).then_inc(d2_ready, 1)
            for b in range(NB):
                dve.wait_ge(root_ready, b + 1)
                V.reciprocal(root[:, b % 2], root[:, b % 2]).then_inc(rroot_ready, 1)
                dve.wait_ge(rroot_ready, b + 1)
                V.tensor_tensor(xnT[:, :, b * BLK:(b + 1) * BLK], xnT[:, :, b * BLK:(b + 1) * BLK],
                                spread(root[:, b % 2], 1, FC), ALU.mult).then_inc(xn_ready, 1)

            def batch_variance(c, s):
                dve.wait_ge(fq_ready, c + 1)
                for b in range(NB):
                    last = V.bn_stats(stats[:, b, :], ps[:, 3 * s + b, 0:BLK])
                last.then_inc(stats_ready, 1)
                dve.wait_ge(stats_ready, c + 1)
                dve.nop(nofuse=True)
                V.bn_aggr(mv[:], stats[:].rearrange("p b n -> p (b n)")).then_inc(mv_ready, 1)
                dve.wait_ge(mv_ready, c + 1)
                V.tensor_scalar(bnv[:], mv[:, 1:2], LN_EPS, None, ALU.add).then_inc(bnv_ready, 1)

            def batch_scale(c, s, first=False):
                dve.wait_ge(rstd_ready, c + 1)
                if not first:
                    dve.wait_ge(qb_ready, c - 1)
                V.tensor_scalar(bna[:, s:s + 1], gamma[:, ds(c, 1)], rstd[:, 0:1], None, ALU.mult).then_inc(bna_ready, 1)
                dve.wait_ge(bna_ready, c + 1)
                V.tensor_scalar(bnm[:], mv[:, 0:1], bna[:, s:s + 1], None, ALU.mult).then_inc(bnm_ready, 1)
                dve.wait_ge(bnm_ready, c + 1)
                V.tensor_scalar(bnb[:, s:s + 1], beta[:, ds(c, 1)], bnm[:, 0:1], None, ALU.subtract).then_inc(bnb_ready, 1)

            def top_values(c, s, first=False):
                dve.wait_ge(sim_copied, c + 1)
                if not first:
                    dve.wait_ge(top_kept, c - 1)
                dve.nop(nofuse=True)
                for t in range(NT):
                    last = V.max(best_s[:, s, t, :], sims[:, s, t, :])
                last.then_inc(tops_ready, 1)

            def top_places(c, s):
                dve.wait_ge(tops_ready, c + 1)
                dve.nop(nofuse=True)
                for t in range(NT):
                    last = V.max_index(best_i[:, s, t, :], best_s[:, s, t, :], sims[:, s, t, :])
                last.then_inc(topi_ready, 1)

            dve.wait_ge(ld_gamma, 16)
            dve.wait_ge(ld_beta, 16)
            for c in range(2):
                batch_variance(c, c)
                batch_scale(c, c, first=True)

            def router_step(c, s, first=False):
                batch_variance(c, s)
                top_values(c - 2, s, first)
                batch_scale(c, s)
                top_places(c - 2, s)

            router_step(2, 0, first=True)
            router_step(3, 1, first=True)
            with dve.Fori(2, NC2 // 2) as j:
                router_step(2 * j, 0)
                router_step(2 * j + 1, 1)
            for s in range(2):
                top_values(NC2 - 2 + s, s)
                top_places(NC2 - 2 + s, s)

            def best_scores(t, first=False):
                sx = top_s[:, ds(t, 1), 0:FH, :].rearrange("p o h k -> p (o h) k")
                sy = top_s[:, ds(t, 1), FH:NC2, :].rearrange("p o h k -> p (o h) k")
                V.tensor_tensor(comb[:], spread(sx, 3, TOPK), spread(sy, 2, TOPK), ALU.add).then_inc(comb_ready, 1)
                dve.wait_ge(comb_ready, t + 1)
                dve.nop(nofuse=True)
                for h in range(FH):
                    last = V.max(best[:, h, :], comb[:, h].rearrange("p a b -> p (a b)"))
                last.then_inc(best_ready, 1)
                dve.wait_ge(best_ready, t + 1)
                if not first:
                    dve.wait_ge(ex_ready, t)
                V.tensor_tensor(dif[:], best[:], best[:, :, 0:1].broadcast_to([128, FH, TOPK]), ALU.subtract).then_inc(dif_ready, 1)

            def choose(t, first=False):
                ix = top_i[:, ds(t, 1), 0:FH, :].rearrange("p o h k -> p (o h) k")
                iy = top_i[:, ds(t, 1), FH:NC2, :].rearrange("p o h k -> p (o h) k")
                for h in range(FH):
                    last = V.max_index(pick[:, h, :], best[:, h, :], comb[:, h].rearrange("p a b -> p (a b)"))
                last.then_inc(pick_ready, 1)
                dve.wait_ge(pick_ready, t + 1)
                V.tensor_scalar(pick_a[:], pick[:].bitcast(i32), 3, None, ALU.logical_shift_right)
                V.tensor_scalar(pick_b[:], pick[:].bitcast(i32), TOPK - 1, None, ALU.bitwise_and).then_inc(pickab_ready, 1)
                dve.wait_ge(pickab_ready, t + 1)
                ranks = spread(spread(iota8[:], 1, TOPK), 1, FH)
                V.tensor_tensor(mask_a[:], spread(pick_a[:], 3, TOPK), ranks, ALU.is_equal)
                V.tensor_tensor(mask_b[:], spread(pick_b[:], 3, TOPK), ranks, ALU.is_equal).then_inc(mask_ready, 1)
                dve.wait_ge(mask_ready, t + 1)
                V.tensor_tensor(mask_a[:], mask_a[:], spread(ix, 2, TOPK), ALU.mult)
                V.tensor_tensor(mask_b[:], mask_b[:], spread(iy, 2, TOPK), ALU.mult).then_inc(masked_ready, 1)
                dve.wait_ge(masked_ready, t + 1)
                V.reduce_sum(key_i[:], mask_a[:], AX.X)
                V.reduce_sum(key_j[:], mask_b[:], AX.X).then_inc(key_ready, 1)
                dve.wait_ge(key_ready, t + 1)
                V.scalar_tensor_tensor(expert[:], key_i[:].rearrange("p h k -> p (h k)"), float(KEYS),
                                       key_j[:].rearrange("p h k -> p (h k)"), ALU.mult, ALU.add).then_inc(expert_ready, 1)
                dve.wait_ge(expert_ready, t + 1)
                V.tensor_scalar(e_lo[:], expert[:], 127, None, ALU.bitwise_and)
                V.tensor_scalar(e_hi[:], expert[:], 7, None, ALU.logical_shift_right).then_inc(elohi_ready, 1)
                dve.wait_ge(elohi_ready, t + 1)
                if not first:
                    dve.wait_ge(picks_tr, t)
                V.tensor_copy(lo2[:], spread(e_lo[:], 1, 2))
                V.tensor_copy(hi2[:], spread(e_hi[:], 1, 2)).then_inc(lohi2_ready, 1)
                dve.wait_ge(ex_ready, t + 1)
                V.reduce_sum(zs[:], ex[:], AX.X).then_inc(zs_ready, 1)
                dve.wait_ge(zs_ready, t + 1)
                V.reciprocal(zi[:], zs[:]).then_inc(zi_ready, 1)
                dve.wait_ge(zi_ready, t + 1)
                V.scalar_tensor_tensor(gate2[:, 0, :].rearrange("p (h k) -> p h k", k=TOPK), ex[:], GATE_SCALE,
                                       spread(zi[:], 2, TOPK), ALU.mult, ALU.mult).then_inc(gate_ready, 1)
                dve.wait_ge(gate_ready, t + 1)
                V.tensor_copy(gate16[:], gate2[:, 0, :]).then_inc(gate16_ready, 1)
                dve.wait_ge(gate16_ready, t + 1)
                V.tensor_tensor(gate2[:, 1, :], gate2[:, 0, :], gate16[:], ALU.subtract).then_inc(gate2_ready, 1)

            def one_hots(t, first=False):
                dve.wait_ge(picks_copied, t + 1)
                for m in range(3):
                    last = V.tensor_scalar(loT[:, m, :], picksT[:, 0, :], -32.0 * (m + 1), None, ALU.add)
                last.then_inc(lot_ready, 1)
                if not first:
                    dve.wait_ge(gate_mm, t * NTG)
                V.tensor_tensor(gated_hi[:], iota32[:], spread(picksT[:, 1, :], 1, EC), ALU.is_equal).then_inc(hi_hot, 1)
                dve.wait_ge(lot_ready, t + 1)
                for m in range(4):
                    src = picksT[:, 0, :] if m == 0 else loT[:, m - 1, :]
                    last = V.tensor_tensor(onehot_lo[:, 32 * m:32 * m + 32, :], iota32[:], spread(src, 1, EC), ALU.is_equal)
                last.then_inc(lo_hot, 1)
                dve.wait_ge(hi_hot, t + 1)
                V.tensor_tensor(gated_hi[:], gated_hi[:], spread(picksT[:, 2, :], 1, EC), ALU.mult).then_inc(gated, 1)

            def gate_hidden(t):
                dve.wait_ge(gelu_ready, (t + 1) * NHG)
                for k in range(NTG):
                    dve.wait_ge(gate_mm, t * NTG + k + 1)
                    h = act_h[:, ds(t % 2, 1), :, k * TG:(k + 1) * TG].rearrange("p o c t -> p (o c) t")
                    V.scalar_tensor_tensor(h, ps[:, 2 + k % 4, :].rearrange("p (t c) -> p c t", c=EC), 1.0 / GATE_SCALE, h,
                                           ALU.mult, ALU.mult).then_inc(acts_ready, 1)

            dve.wait_ge(top_kept, NC2)
            dve.wait_ge(iota_ready, 1)
            best_scores(0, first=True)
            choose(0, first=True)
            best_scores(1)
            one_hots(0, first=True)
            choose(1)

            def expert_step(t):
                gate_hidden(t)
                best_scores(t + 2)
                one_hots(t + 1)
                choose(t + 2)

            with dve.Fori(0, NT - 2) as t:
                expert_step(t)
            gate_hidden(NT - 2)
            one_hots(NT - 1)
            gate_hidden(NT - 1)

        @block.gpsimd
        def _(pool):
            P = nc.gpsimd
            NQK = HEADS + KV_HEADS + 1

            def inverse_roots(g, first=False):
                pool.wait_ge(rmsv_ready, g + 1)
                if not first:
                    pool.wait_ge(v_ready, g)
                    pool.wait_ge(qkn_ready, g)
                P.tensor_tensor(rinv[:], rmsv[:], half_neg[0:GT, 0:NQK], ALU.pow).then_inc(rinv_ready, 1)

            def normalise_p(g, first=False):
                pool.wait_ge(pinv_ready, g + 1)
                if not first:
                    pool.wait_ge(pt_ready, g)
                P.tensor_tensor(pn[:], sm[:].rearrange("p a b k -> p (a b) k"), spread(pinv[:], 2, GT), ALU.mult).then_inc(pn_ready, 1)

            def current_v(g, first=False):
                pool.wait_ge(v_ready, g + 1)
                if not first:
                    pool.wait_ge(o_ready, g * 2)
                P.tensor_copy(vcur[:], vall[:, ds(g, 1), :].rearrange("p o n -> p (o n)")).then_inc(vcur_ready, 1)

            P.memset(mean_w[:], 1.0 / DIM)
            P.memset(half_neg[:], -0.5)
            P.memset(eps_ln[:], LN_EPS)
            P.memset(hT[:, :, TOK:PAD_TOK], 0.0).then_inc(const_ready, 1)
            pool.wait_ge(const_ready, 1)
            inverse_roots(0, first=True)
            inverse_roots(1)
            normalise_p(0, first=True)
            current_v(0, first=True)
            with pool.Fori(1, NG - 1) as i:
                inverse_roots(i + 1)
                normalise_p(i)
                current_v(i)
            normalise_p(NG - 1)
            current_v(NG - 1)

            pool.wait_ge(h2_ready, NG)
            P.iota(iota8[:], [[1, TOPK]], base=0, channel_multiplier=0, allow_small_or_imprecise_dtypes=True)
            P.iota(iota32[:], [[1, EC], [0, 128]], base=0, channel_multiplier=0, allow_small_or_imprecise_dtypes=True).then_inc(iota_ready, 1)

            def batch_root(c):
                pool.wait_ge(bnv_ready, c + 1)
                P.tensor_tensor(rstd[:], bnv[:], half_neg[:, 0:1], ALU.pow).then_inc(rstd_ready, 1)

            def keep_top(c, s):
                pool.wait_ge(topi_ready, c + 1)
                P.tensor_copy(top_s[:, :, ds(c, 1), :].rearrange("p t o k -> p t (o k)"), best_s[:, s])
                P.tensor_copy(top_i[:, :, ds(c, 1), :].rearrange("p t o k -> p t (o k)"), best_i[:, s]).then_inc(top_kept, 1)

            batch_root(0)
            batch_root(1)
            with pool.Fori(1, NC2 // 2) as j:
                batch_root(2 * j)
                keep_top(2 * j - 2, 0)
                batch_root(2 * j + 1)
                keep_top(2 * j - 1, 1)
            keep_top(NC2 - 2, 0)
            keep_top(NC2 - 1, 1)

            def final_sum(t, first=False):
                pool.wait_ge(up_copied, t + 1)
                if not first:
                    pool.wait_ge(stored, t * 16)
                P.tensor_tensor(outs[:], upout[:], hT[:, :, ds(t * 128, 128)], ALU.add).then_inc(sum_ready, 1)

            final_sum(0, first=True)
            with pool.Fori(1, NT) as t:
                final_sum(t)


def kernel(**inputs):
    import numpy as np
    import concourse.bacc as bacc
    from concourse import mybir
    from concourse.bass_utils import run_bass_kernel_spmd

    f = np.float32
    a = {k: np.asarray(v) for k, v in inputs.items()}
    side = 6
    x = a["x"].reshape(IMAGES, 3, side, 16, side, 16).transpose(1, 3, 5, 0, 2, 4).reshape(KC, 128, TOK)

    def rows(w, chunks):
        return w.reshape(chunks, 128, -1).transpose(1, 0, 2)

    q, k = np.arange(GT)[:, None], np.arange(GT)[None, :]
    rel = (k - q).astype(f)
    hidden = (k > q) | (k < q - 16) | (k // PATCHES != q // PATCHES)
    slopes = (2.0 ** -0.5) ** np.arange(1, HEADS + 1, dtype=f)
    table = np.where(hidden[None], f(-1e30), slopes[:, None, None].astype(f) * rel[None]).astype(f)
    table = table.reshape(REP, KV_HEADS, GT, GT).transpose(2, 1, 0, 3)

    arrays = {
        "x_t": x,
        "tok_w": rows(a["L0_tok_W"].T, KC),
        "tok_b": a["L0_tok_b"].reshape(FC, 128).T,
        "pos": rows(a["L0_tok_pos_embd"].reshape(PATCHES, DIM).T, FC),
        "ident": np.eye(128, dtype=f),
        "bias": table,
        "wq": rows(a["L0_attn_wq"].T, FC),
        "wkv": rows(np.concatenate([a["L0_attn_wk"].T, a["L0_attn_wv"].T], axis=1), FC),
        "wo": rows(a["L0_attn_wo"].T, QC),
        "qw": np.concatenate([a["L0_attn_q_norm_w"]] * 2).reshape(128, 1),
        "kw": np.concatenate([a["L0_attn_k_norm_w"]] * 2).reshape(128, 1),
        "ffn_wq": a["L0_ffn_w_q"].reshape(FC, 128, NC2, KD).transpose(2, 1, 0, 3),
        "gamma": a["L0_ffn_bn_gamma"].reshape(NC2, 128).T,
        "beta": a["L0_ffn_bn_beta"].reshape(NC2, 128).T,
        "keys": a["L0_ffn_keys"].transpose(3, 2, 0, 1).reshape(KD, NC2, KEYS),
        "down": rows(a["L0_ffn_down_embed"].T, FC),
        "up": rows(a["L0_ffn_up_embed"], EC),
    }
    arrays = {n: np.ascontiguousarray(v) for n, v in arrays.items()}
    nc = bacc.Bacc("TRN2", target_bir_lowering=False, num_devices=1)
    args = [nc.dram_tensor("in_" + n, v.shape, mybir.dt.from_np(v.dtype), kind="ExternalInput").ap() for n, v in arrays.items()]
    out = nc.dram_tensor("out", (128, FC, TOK), mybir.dt.float32, kind="ExternalOutput").ap()
    vit_block(nc, *args, out)
    r = run_bass_kernel_spmd(nc, [{"in_" + n: v for n, v in arrays.items()}], core_ids=[0])
    return r.results[0]["out"].transpose(2, 1, 0).reshape(IMAGES, PATCHES, DIM)
```

```python
import concourse.bass as bass
from concourse import mybir
from contextlib import ExitStack

IMAGES = 32
PATCHES = 36
TOK = IMAGES * PATCHES
DIM = 256
FC = DIM // 128
PATCH_DIM = 768
KC = PATCH_DIM // 128
KF = 2
HEADS, KV_HEADS, HD = 16, 4, 64
REP = HEADS // KV_HEADS
QC = HEADS * HD // 128
GIMG = 3
GT = GIMG * PATCHES
NG = -(-IMAGES // GIMG)
PAD_TOK = NG * GT
FH, KD, KEYS, TOPK = 8, 128, 64, 8
NC2 = 2 * FH
EXPERTS = KEYS * KEYS
EC = EXPERTS // 128
NT = TOK // 128
BLK = 384
NB = TOK // BLK
BT = BLK // 128
TG = 16
NTG = 128 // TG
HG = 4
NHG = EC // HG
RMS_EPS = 0.01
LN_EPS = 1e-5
GATE_SCALE = 4096.0
X_SCALE = 2.0 ** 9
W_SCALE = 2.0 ** 11
A_SCALE = 2.0 ** 4
WCH = 8
WN = FC * EXPERTS // WCH
SQN = 2 * WN


def vit_block(nc, x_t, tok_w, tok_b, pos, ident_in, bias_in, wq_in, wkv_in, wo_in, qw_in, kw_in,
              ffn_wq, gamma_in, beta_in, keys_in, down_in, up_in, out):
    fp32 = mybir.dt.float32
    fp16 = mybir.dt.float16
    bf16 = mybir.dt.bfloat16
    f32r = mybir.dt.float32r
    u32 = mybir.dt.uint32
    i32 = mybir.dt.int32
    ALU = mybir.AluOpType
    ACT = mybir.ActivationFunctionType
    AX = mybir.AxisListType
    ds = bass.ds

    ctx = ExitStack()
    with ctx:
        def sb(name, shape, dt, scope=ctx):
            return scope.enter_context(nc.sbuf_tensor(name, shape, dt))

        def sem(name):
            return ctx.enter_context(nc.semaphore(name))

        def spread(ap, axis, n):
            v = ap.unsqueeze(axis)
            shape = list(v.shape)
            shape[axis] = n
            return v.broadcast_to(shape)

        hT = sb("hT", [128, FC, PAD_TOK], fp32)
        tables = sb("tables", [128, 2 * (WCH + 1), WN], fp32)
        halves = tables[:].bitcast(fp16)
        wsq = sb("wsq", [128, 2, FC * EXPERTS // SQN], fp32)
        wsum = sb("wsum", [128, 2], fp32)
        wmean = sb("wmean", [128, 2], fp32)
        wpow = sb("wpow", [128, 2], fp32)
        winv = sb("winv", [128, 2], fp32)
        wscale = sb("wscale", [128, 2], fp32)
        hscale = sb("hscale", [128, 1], fp32)
        ascale = sb("ascale", [128, 1], fp32)
        oscale = sb("oscale", [128, 1], fp32)
        ident = sb("ident", [128, 128], fp32)
        mean_w = sb("mean_w", [128, 128], fp32)
        gamma = sb("gamma", [128, NC2], fp32)
        beta = sb("beta", [128, NC2], fp32)
        half_neg = sb("half_neg", [128, HEADS + KV_HEADS + 1], fp32)
        digit_shift = sb("digit_shift", [128, 3], fp32)
        eps_bn = sb("eps_bn", [128, 1], fp32)

        p1 = ExitStack()
        posb = sb("posb", [128, FC, PATCHES], fp32, p1)
        tokb = sb("tokb", [128, FC], fp32, p1)
        wqr = sb("wqr", [128, 2, FC, HEADS * HD], f32r, p1)
        wkvr = sb("wkvr", [128, 2, FC, 2 * KV_HEADS * HD], f32r, p1)
        wo = sb("wo", [128, QC, DIM], fp32, p1)
        qw = sb("qw", [128, 1], fp32, p1)
        kw = sb("kw", [128, 1], fp32, p1)
        kscale = sb("kscale", [128, 1], fp32, p1)
        bias = sb("bias", [GT, KV_HEADS, REP, GT], fp32, p1)
        d1 = sb("d1", [128, FC, GT], fp32, p1)
        d1r = sb("d1r", [128, 2, FC, 128], f32r, p1)
        sq1 = sb("sq1", [128, FC, GT], fp32, p1)
        p0 = ExitStack()
        xT = sb("xT", [128, KC, TOK], fp32, p0)
        tokw = sb("tokw", [128, KC, DIM], fp32, p0)
        xer = sb("xer", [128, 3, 2, TOK], f32r, p0)
        tokwr = sb("tokwr", [128, 3, 2, DIM], f32r, p0)
        wq = sb("wq", [128, FC, HEADS * HD], fp32, p0)
        wkv = sb("wkv", [128, FC, 2 * KV_HEADS * HD], fp32, p0)
        p0.close()
        sqq = sb("sqq", [GT, HEADS + KV_HEADS, HD], fp32, p1)
        msum = sb("msum", [GT, HEADS + KV_HEADS], fp32, p1)
        rmsv = sb("rmsv", [GT, HEADS + KV_HEADS + 1], fp32, p1)
        vare = sb("vare", [GT, 1], fp32, p1)
        rinv = sb("rinv", [GT, HEADS + KV_HEADS + 1], fp32, p1)
        qkn = sb("qkn", [GT, HEADS + KV_HEADS, HD], fp32, p1)
        qT = sb("qT", [128, QC, GT], fp32, p1)
        kT = sb("kT", [128, KV_HEADS // 2, GT], fp32, p1)
        vall = sb("vall", [GT, NG, KV_HEADS * HD], fp32, p1)
        vcur = sb("vcur", [GT, KV_HEADS * HD], fp32, p1)
        sm = sb("sm", [GT, KV_HEADS, REP, GT], fp32, p1)
        nmax = sb("nmax", [GT, KV_HEADS, REP], fp32, p1)
        psums = sb("psums", [GT, HEADS], fp32, p1)
        pinv = sb("pinv", [GT, HEADS], fp32, p1)
        pn = sb("pn", [GT, HEADS, GT], fp32, p1)
        pT = sb("pT", [GT, KV_HEADS, REP, GT], fp32, p1)
        oT = sb("oT", [128, QC, GT], fp32, p1)
        p1.close()

        p2 = ctx
        xh = sb("xh", [128, FC, TOK], fp16, p2)
        xl = sb("xl", [128, FC, TOK], fp16, p2)
        stats = sb("stats", [128, 2, NB, 6], fp32, p2)
        mv = sb("mv", [128, 2, 2], fp32, p2)
        bnv = sb("bnv", [128, 1], fp32, p2)
        rstd = sb("rstd", [128, 1], fp32, p2)
        bna = sb("bna", [128, 2], fp32, p2)
        bnb = sb("bnb", [128, 2], fp32, p2)
        bnm = sb("bnm", [128, 1], fp32, p2)
        top_s = sb("top_s", [128, NT, NC2, TOPK], fp32, p2)
        top_i = sb("top_i", [128, NT, NC2, TOPK], fp16, p2)
        best_s = sb("best_s", [128, 2, NT, TOPK], fp32, p2)
        best_i = sb("best_i", [128, 2, NT, TOPK], u32, p2)
        comb = sb("comb", [128, FH, TOPK, TOPK], fp32, p2)
        best = sb("best", [128, FH, TOPK], fp32, p2)
        pick = sb("pick", [128, FH, TOPK], u32, p2)
        pick_a = sb("pick_a", [128, FH, TOPK], i32, p2)
        pick_b = sb("pick_b", [128, FH, TOPK], i32, p2)
        iota8 = sb("iota8", [128, TOPK], fp32, p2)
        mask_a = sb("mask_a", [128, FH, TOPK, TOPK], fp16, p2)
        mask_b = sb("mask_b", [128, FH, TOPK, TOPK], fp16, p2)
        key_i = sb("key_i", [128, FH, TOPK], fp32, p2)
        key_j = sb("key_j", [128, FH, TOPK], fp32, p2)
        expert = sb("expert", [128, FH * TOPK], i32, p2)
        e_lo = sb("e_lo", [128, FH * TOPK], i32, p2)
        e_hi = sb("e_hi", [128, FH * TOPK], i32, p2)
        lo2 = sb("lo2", [128, 2, FH * TOPK], fp32, p2)
        hi2 = sb("hi2", [128, 2, FH * TOPK], fp32, p2)
        dif = sb("dif", [128, FH, TOPK], fp32, p2)
        ex = sb("ex", [128, FH, TOPK], fp32, p2)
        zs = sb("zs", [128, FH], fp32, p2)
        zi = sb("zi", [128, FH], fp32, p2)
        gate2 = sb("gate2", [128, 2, FH * TOPK], fp32, p2)
        gate16 = sb("gate16", [128, FH * TOPK], fp16, p2)
        picksT = sb("picksT", [128, 3, 128], fp16, p2)
        loT = sb("loT", [128, 3, 128], fp16, p2)
        iota32 = sb("iota32", [128, EC, 128], fp16, p2)
        p3 = ExitStack()
        xnT = sb("xnT", [128, FC, TOK], fp32, p3)
        sq2 = sb("sq2", [128, 2, FC, BLK], fp32, p3)
        var2 = sb("var2", [128, NT], fp32, p3)
        rstd2 = sb("rstd2", [128, NT], fp32, p3)
        diag = sb("diag", [128, NT, 128], fp32, p3)
        wqc = sb("wqc", [128, 2, FC, KD], fp32, p3)
        keysT = sb("keysT", [128, NC2, KEYS], fp32, p3)
        qb = sb("qb", [128, 2, TOK], fp32, p3)
        sims = sb("sims", [128, 2, NT, KEYS], fp32, p3)
        xr = sb("xr", [128, 2, FC, TOK], f32r, p3)
        wr = sb("wr", [128, 2, 2, FC, KD], f32r, p3)
        p3.close()
        onehot_lo = sb("onehot_lo", [128, 128, 128], fp16, p2)
        gated_hi = sb("gated_hi", [128, EC, 128], fp16, p2)
        act_h = sb("act_h", [128, EC, 128], fp32, p2)
        ah = sb("ah", [128, 2, EC, 128], fp16, p2)
        al = sb("al", [128, 2, EC, 128], fp16, p2)
        upout = sb("upout", [128, FC, 128], fp32, p2)

        ps = ctx.enter_context(nc.psum_tensor("ps", [128, 8, 512], fp32))

        QK_PARTS = ((1, 0, 8), (2, 8, 8), (3, 16, 4))

        ld_x = [sem(f"ld_x{k}") for k in range(KC)]
        ld_tokw = [sem(f"ld_tokw{k}") for k in range(KC)]
        ld_pos, ld_tokb, ld_ident, ld_bias = (sem(n) for n in ("ld_pos", "ld_tokb", "ld_ident", "ld_bias"))
        ld_wq, ld_wkv, ld_wo, ld_qw, ld_kw = (sem(n) for n in ("ld_wq", "ld_wkv", "ld_wo", "ld_qw", "ld_kw"))
        ld_gamma, ld_beta, ld_keys, ld_down, ld_up = (sem(n) for n in ("ld_gamma", "ld_beta", "ld_keys", "ld_down", "ld_up"))
        ld_wqc = [sem(f"ld_wqc{s}") for s in range(2)]
        emb_high, emb_low, emb_used = sem("emb_high"), sem("emb_low"), sem("emb_used")
        const_ready, iota_ready = sem("const_ready"), sem("iota_ready")
        embedded, posb_ready, h_ready = sem("embedded"), sem("posb_ready"), sem("h_ready")
        kscale_ready = sem("kscale_ready")
        wqkv_high, wqkv_low, pad_ready, dr_high, dr_low = (sem(n) for n in ("wqkv_high", "wqkv_low", "pad_ready", "dr_high", "dr_low"))
        mean_ready, d_ready, sq_ready, var_ready = sem("mean_ready"), sem("d_ready"), sem("sq_ready"), sem("var_ready")
        q0_ready, q1_ready, kv_ready = sem("q0_ready"), sem("q1_ready"), sem("kv_ready")
        sqq_ready = [sem(f"sqq_ready{n}") for n in range(3)]
        msum_ready, vare_ready = sem("msum_ready"), sem("vare_ready")
        rmsv_ready, rinv_ready, v_ready, qkn_ready = sem("rmsv_ready"), sem("rinv_ready"), sem("v_ready"), sem("qkn_ready")
        qkt_ready, qkt_copied = sem("qkt_ready"), sem("qkt_copied")
        score_ready = [sem(f"score_ready{g}") for g in range(KV_HEADS)]
        biased = [sem(f"biased{g}") for g in range(KV_HEADS)]
        max_ready = [sem(f"max_ready{g}") for g in range(KV_HEADS)]
        exp_ready, pinv_ready, pn_ready, vcur_ready = sem("exp_ready"), sem("pinv_ready"), sem("pn_ready"), sem("vcur_ready")
        pt_ready, pt_copied_act, pt_copied_dve = sem("pt_ready"), sem("pt_copied_act"), sem("pt_copied_dve")
        o_ready, o_copied_act, o_copied_dve = sem("o_ready"), sem("o_copied_act"), sem("o_copied_dve")
        wo_ready, h2_ready = sem("wo_ready"), sem("h2_ready")
        mean2_ready, d2_ready, sq2_ready, var2_ready = sem("mean2_ready"), sem("d2_ready"), sem("sq2_ready"), sem("var2_ready")
        veps_ready, rstd2_ready, diag_ready, spread_ready, xn_ready = (sem(n) for n in ("veps_ready", "rstd2_ready", "diag_ready", "spread_ready", "xn_ready"))
        fq_ready, stats_ready, mv_ready, bnv_ready, rstd_ready = (sem(n) for n in ("fq_ready", "stats_ready", "mv_ready", "bnv_ready", "rstd_ready"))
        bna_ready, bnm_ready, bnb_ready, qb_ready = (sem(n) for n in ("bna_ready", "bnm_ready", "bnb_ready", "qb_ready"))
        sim_ready, sim_copied, tops_ready, topi_ready = (sem(n) for n in ("sim_ready", "sim_copied", "tops_ready", "topi_ready"))
        top_kept = sem("top_kept")
        comb_ready, best_ready, pick_ready, dif_ready, ex_ready = (sem(n) for n in ("comb_ready", "best_ready", "pick_ready", "dif_ready", "ex_ready"))
        zs_ready, zi_ready, gate_ready, gate16_ready, gate2_ready = (sem(n) for n in ("zs_ready", "zi_ready", "gate_ready", "gate16_ready", "gate2_ready"))
        pickab_ready, mask_ready, masked_ready, key_ready = (sem(n) for n in ("pickab_ready", "mask_ready", "masked_ready", "key_ready"))
        expert_ready, elohi_ready, lohi2_ready = (sem(n) for n in ("expert_ready", "elohi_ready", "lohi2_ready"))
        picks_tr, picks_copied, lo_hot, hi_hot, gated = (sem(n) for n in ("picks_tr", "picks_copied", "lo_hot", "hi_hot", "gated"))
        down_ready, gelu_ready, gate_mm, acts_ready = (sem(n) for n in ("down_ready", "gelu_ready", "gate_mm", "acts_ready"))
        wsq_ready, wsum_ready, wtotal_ready, wmean_ready = (sem(n) for n in ("wsq_ready", "wsum_ready", "wtotal_ready", "wmean_ready"))
        wroot_ready, wpow_ready, winv_ready = sem("wroot_ready"), sem("wpow_ready"), sem("winv_ready")
        xr_high, xr_low, wr_high, wr_low = (sem(n) for n in ("xr_high", "xr_low", "wr_high", "wr_low"))
        down_high, down_low, up_high, up_low = (sem(n) for n in ("down_high", "down_low", "up_high", "up_low"))
        x_high, x_low, a_high, a_low = (sem(n) for n in ("x_high", "x_low", "a_high", "a_low"))
        up_ready, up_copied, sum_ready = sem("up_ready"), sem("up_copied"), sem("sum_ready")
        stored = sem("stored")

        block = ctx.enter_context(nc.Block())

        blocks1 = [(0, 432), (432, 432), (864, 288)]

        @block.sync
        def _(sp):
            for k in range(KC):
                sp.dma_start(tokw[:, k, :], tok_w[:, k, :]).then_inc(ld_tokw[k], 16)
                sp.dma_start(xT[:, k, :], x_t[k]).then_inc(ld_x[k], 16)
            sp.dma_start(bias[:], bias_in).then_inc(ld_bias, 16)
            sp.dma_start(wo[:], wo_in).then_inc(ld_wo, 16)
            sp.dma_start(tables[:, 1:WCH + 1, :], down_in).then_inc(ld_down, 16)
            sp.dma_start(tables[:, WCH + 2:, :], up_in).then_inc(ld_up, 16)
            sp.dma_start(gamma[:], gamma_in).then_inc(ld_gamma, 16)
            sp.dma_start(beta[:], beta_in).then_inc(ld_beta, 16)
            sp.wait_ge(h2_ready, NG)
            sp.dma_start(wqc[:, 0], ffn_wq[0]).then_inc(ld_wqc[0], 16)
            sp.dma_start(wqc[:, 1], ffn_wq[1]).then_inc(ld_wqc[1], 16)
            sp.dma_start(keysT[:], keys_in).then_inc(ld_keys, 16)
            with sp.Fori(1, NC2 // 2) as j:
                for s in range(2):
                    sp.wait_ge(wr_low, 2 * j + s - 1)
                    sp.dma_start(wqc[:, s], ffn_wq[ds(2 * j + s, 1)].rearrange("o p f n -> p (o f) n")).then_inc(ld_wqc[s], 16)
            with sp.Fori(0, NT) as t:
                sp.wait_ge(sum_ready, t + 1)
                sp.dma_start(out[:, :, ds(t * 128, 128)], hT[:, :, ds(t * 128, 128)]).then_inc(stored, 16)
            sp.wait_ge(stored, 16 * NT)

        @block.tensor
        def _(pe):
            mm = nc.tensor.matmul

            def mean_of_group(g, first=False):
                if not first:
                    pe.wait_ge(d_ready, g)
                    pe.wait_ge(vare_ready, g)
                for f in range(FC):
                    last = mm(ps[:, 0, 0:GT], mean_w[:], hT[:, f, ds(g * GT, GT)], start=f == 0, stop=f == FC - 1)
                last.then_inc(mean_ready, 1)

            def variance_of_group(g):
                pe.wait_ge(sq_ready, g + 1)
                for f in range(FC):
                    last = mm(ps[0:GT, 0, 256:257], sq1[:, f, :], mean_w[:, 0:1], start=f == 0, stop=f == FC - 1)
                last.then_inc(var_ready, 1)

            def project(g, bank, w, c0, done):
                pe.wait_ge(dr_low, g + 1)
                for f in range(FC):
                    for n, (pd, pw) in enumerate(((0, 0), (1, 0), (0, 1))):
                        last = mm(ps[:, bank, :], d1r[:, pd, f, :], w[:, pw, f, c0:c0 + 512],
                                  start=f == 0 and n == 0, stop=f == FC - 1 and n == 2)
                last.then_inc(done, 1)

            def transpose_qk(g, free=None):
                pe.wait_ge(qkn_ready, g + 1)
                if free is not None:
                    pe.wait_ge(o_copied_act, free)
                    pe.wait_ge(o_copied_dve, free)
                flat = qkn[:].rearrange("p h d -> p (h d)")
                for c in range(QC + KV_HEADS // 2):
                    last = nc.tensor.transpose(ps[:, (4, 5, 7)[c // 4], (c % 4) * GT:(c % 4 + 1) * GT],
                                               flat[:, c * 128:(c + 1) * 128], ident[0:GT, 0:GT])
                last.then_inc(qkt_ready, 1)

            def score_group(g, free=None):
                pe.wait_ge(qkt_copied, g + 1)
                for kv in (0, 1, 3, 2):
                    if kv == 2 and free is not None:
                        pe.wait_ge(h2_ready, free)
                    r0 = 64 * (kv % 2)
                    for i in range(REP):
                        h = kv + KV_HEADS * i
                        last = mm(ps[0:GT, 4 + kv, i * GT:(i + 1) * GT], qT[r0:r0 + 64, h // 2, :],
                                  kT[r0:r0 + 64, kv // 2, :], start=True, stop=True)
                    last.then_inc(score_ready[kv], 1)

            def transpose_p(g, next_scores=True):
                pe.wait_ge(pn_ready, g + 1)
                if not next_scores:
                    pe.wait_ge(o_copied_act, g)
                    pe.wait_ge(o_copied_dve, g)
                    pe.wait_ge(h2_ready, g)
                for kv in (0, 1, 3, 2):
                    if next_scores:
                        pe.wait_ge(biased[kv], g + 2)
                    for i in range(REP):
                        last = nc.tensor.transpose(ps[0:GT, 4 + kv, i * GT:(i + 1) * GT], pn[:, REP * kv + i, :],
                                                   ident[0:GT, 0:GT])
                    last.then_inc(pt_ready, 1)

            def attend_group(g):
                pe.wait_ge(vcur_ready, g + 1)
                pe.wait_ge(pt_copied_act, g + 1)
                for kv in range(KV_HEADS):
                    if kv == 2:
                        pe.wait_ge(pt_copied_dve, g + 1)
                    r0 = 64 * (kv % 2)
                    last = mm(ps[r0:r0 + 64, 4 + kv // 2, 0:REP * GT], vcur[:, kv * HD:(kv + 1) * HD],
                              pT[:, kv].rearrange("p i q -> p (i q)"), start=True, stop=True)
                    if kv % 2:
                        last.then_inc(o_ready, 1)
                pe.wait_ge(o_copied_act, g + 1)
                for f in range(FC):
                    for n, c in enumerate((0, 2, 4, 6, 1, 3, 5, 7)):
                        if f == 0 and n == 4:
                            pe.wait_ge(o_copied_dve, g + 1)
                        last = mm(ps[:, 6, f * GT:(f + 1) * GT], wo[:, c, f * 128:(f + 1) * 128], oT[:, c, :],
                                  start=n == 0, stop=n == QC - 1)
                last.then_inc(wo_ready, 1)

            for k in range(KC):
                if k < KF:
                    pe.wait_ge(ld_tokw[k], 16)
                    pe.wait_ge(ld_x[k], 16)
                else:
                    pe.wait_ge(emb_low, 2 * (k - KF) + 2)
                for b, (t0, n) in enumerate(blocks1):
                    for f in range(FC):
                        if k < KF:
                            last = mm(ps[:, 2 * b + f, 0:n], tokw[:, k, f * 128:(f + 1) * 128], xT[:, k, t0:t0 + n],
                                      start=k == 0, stop=False)
                            continue
                        for i, (pw, px) in enumerate(((0, 0), (0, 1), (1, 0))):
                            last = mm(ps[:, 2 * b + f, 0:n], tokwr[:, k % 3, pw, f * 128:(f + 1) * 128],
                                      xer[:, k % 3, px, t0:t0 + n], start=False, stop=k == KC - 1 and i == 2)
                        if k == KC - 1:
                            last.then_inc(embedded, 1)
                if KF <= k < KC - 1:
                    last.then_inc(emb_used, 1)

            pe.wait_ge(const_ready, 1)
            pe.wait_ge(h_ready, FC * len(blocks1))
            pe.wait_ge(ld_ident, 16)
            pe.wait_ge(wqkv_low, 2)
            pe.wait_ge(pad_ready, 2)
            mean_of_group(0, first=True)
            variance_of_group(0)
            project(0, 1, wqr, 0, q0_ready)
            project(0, 2, wqr, 512, q1_ready)
            project(0, 3, wkvr, 0, kv_ready)
            mean_of_group(1)
            transpose_qk(0)
            variance_of_group(1)
            project(1, 1, wqr, 0, q0_ready)
            score_group(0)
            project(1, 2, wqr, 512, q1_ready)
            project(1, 3, wkvr, 0, kv_ready)
            mean_of_group(2)
            pe.wait_ge(ld_wo, 16)

            def attention_step(i, first=False, projections=True, means=True):
                if first:
                    for kv in range(KV_HEADS):
                        pe.wait_ge(biased[kv], 1)
                transpose_qk(i + 1, None if first else i)
                if projections:
                    variance_of_group(i + 2)
                    project(i + 2, 1, wqr, 0, q0_ready)
                score_group(i + 1, None if first else i)
                if projections:
                    project(i + 2, 2, wqr, 512, q1_ready)
                transpose_p(i)
                if projections:
                    project(i + 2, 3, wkvr, 0, kv_ready)
                if means:
                    mean_of_group(i + 3)
                attend_group(i)

            attention_step(0, first=True)
            pe.wait_ge(wsum_ready, 1)
            pe.wait_ge(d_ready, 4)
            pe.wait_ge(vare_ready, 3)
            mm(ps[:, 0, 300:302], mean_w[:], wsum[:], start=True, stop=True).then_inc(wtotal_ready, 1)
            pe.wait_ge(wmean_ready, 1)
            with pe.Fori(1, NG - 3) as i:
                attention_step(i)
            attention_step(NG - 3, means=False)
            attention_step(NG - 2, projections=False, means=False)

            def block_mean(b):
                pe.wait_ge(h2_ready, min(NG, -(-(b + 1) * BLK // GT)))
                for f in range(FC):
                    last = mm(ps[:, b, 0:BLK], mean_w[:], hT[:, f, b * BLK:(b + 1) * BLK], start=f == 0, stop=f == FC - 1)
                last.then_inc(mean2_ready, 1)

            pe.wait_ge(vare_ready, NG)
            for b in range(NB - 1):
                block_mean(b)
            transpose_p(NG - 1, next_scores=False)
            attend_group(NG - 1)
            block_mean(NB - 1)
            for b in range(NB):
                pe.wait_ge(sq2_ready, b + 1)
                if b > 1:
                    pe.wait_ge(veps_ready, b - 1)
                for t in range(BT):
                    for f in range(FC):
                        last = mm(ps[:, 6 + b % 2, t:t + 1], sq2[:, b % 2, f, t * 128:(t + 1) * 128], mean_w[:, 0:1],
                                  start=f == 0, stop=f == FC - 1)
                last.then_inc(var2_ready, 1)
            for b in range(NB):
                pe.wait_ge(diag_ready, b + 1)
                last = mm(ps[:, 3 + b, 0:BLK], mean_w[:], diag[:, b * BT:(b + 1) * BT, :].rearrange("p t n -> p (t n)"),
                          start=True, stop=True)
                last.then_inc(spread_ready, 1)

            def router_q(c, s, first=False):
                pe.wait_ge(wr_low, c + 1)
                if not first:
                    pe.wait_ge(qb_ready, c - 1)
                for b in range(NB):
                    if first and c == 0:
                        pe.wait_ge(xr_low, b + 1)
                    for f in range(FC):
                        for n, (pw, px) in enumerate(((0, 0), (0, 1), (1, 0))):
                            last = mm(ps[:, 3 * s + b, 0:BLK], wr[:, s, pw, f, :], xr[:, px, f, b * BLK:(b + 1) * BLK],
                                      start=f == 0 and n == 0, stop=f == FC - 1 and n == 2)
                last.then_inc(fq_ready, 1)

            def router_sim(c, s, first=False):
                pe.wait_ge(qb_ready, c + 1)
                if not first:
                    pe.wait_ge(sim_copied, c)
                for t in range(NT):
                    last = mm(ps[:, 6 + t // 8, (t % 8) * KEYS:(t % 8 + 1) * KEYS], qb[:, s, t * 128:(t + 1) * 128],
                              keysT[:, ds(c, 1), :].rearrange("p o k -> p (o k)"), start=True, stop=True)
                last.then_inc(sim_ready, 1)

            router_q(0, 0, first=True)
            pe.wait_ge(xn_ready, NB)
            router_q(1, 1, first=True)
            pe.wait_ge(ld_keys, 16)
            router_q(2, 0)
            router_sim(0, 0, first=True)
            router_q(3, 1)
            router_sim(1, 1)
            with pe.Fori(1, NC2 // 2 - 1) as j:
                for s in range(2):
                    router_q(2 * j + 2 + s, s)
                    router_sim(2 * j + s, s)
            router_sim(NC2 - 2, 0)
            router_sim(NC2 - 1, 1)

            def down_products(t, ks=range(NHG), picks=None):
                for k in ks:
                    if k == 0 and picks is not None:
                        pe.wait_ge(picks_copied, picks)
                    if picks is not None or k > 1:
                        pe.wait_ge(gelu_ready, t * NHG + k - 1)
                    for i in range(HG):
                        for f in range(FC):
                            w0 = f * (WN // FC) + i * 128
                            for n, (part, x) in enumerate(((0, xh), (0, xl), (1, xh))):
                                last = mm(ps[:, k % 2, i * 128:(i + 1) * 128],
                                          halves[:, k, part * WN + w0:part * WN + w0 + 128],
                                          x[:, f, ds(t * 128, 128)],
                                          start=f == 0 and n == 0, stop=f == FC - 1 and n == 2)
                    last.then_inc(down_ready, 1)

            def transpose_picks(t, hidden, bank=0):
                if bank == 0:
                    pe.wait_ge(gelu_ready, hidden * NHG)
                pe.wait_ge(lohi2_ready, t + 1)
                pe.wait_ge(gate2_ready, t + 1)
                for n, a in enumerate((lo2, hi2, gate2)):
                    last = nc.tensor.transpose(ps[:, bank, n * 128:(n + 1) * 128], a[:].rearrange("p a b -> p (a b)"), ident[:])
                last.then_inc(picks_tr, 1)

            def gate_matrices(t, ks, first=False):
                if ks[0] == 0:
                    pe.wait_ge(lo_hot, t + 1)
                    pe.wait_ge(gated, t + 1)
                for k in ks:
                    if not (first and k < 4):
                        pe.wait_ge(acts_ready, t * NTG + k - 3)
                    for n in range(TG):
                        tok = k * TG + n
                        last = mm(ps[:, 2 + k % 4, n * EC:(n + 1) * EC], onehot_lo[:, :, tok], gated_hi[:, :, tok],
                                  start=True, stop=True)
                    last.then_inc(gate_mm, 1)

            def up_product(t, k0, k1, first=False):
                if k0 == 0:
                    pe.wait_ge(a_high, (t + 1) * 2)
                    pe.wait_ge(a_low, (t + 1) * 2)
                    if not first:
                        pe.wait_ge(up_copied, t)
                for c in range(HG * k0, HG * k1):
                    for f in range(FC):
                        w0 = (c % HG) * DIM + f * 128
                        for n, (part, a) in enumerate(((0, ah), (0, al), (1, ah))):
                            last = mm(ps[:, 6 + f, 0:128],
                                      halves[:, WCH + 1 + c // HG, part * WN + w0:part * WN + w0 + 128],
                                      a[:, ds(t % 2, 1), c, :].rearrange("p o t -> p (o t)"),
                                      start=c == 0 and n == 0, stop=c == EC - 1 and n == 2)
                if k1 == NHG:
                    last.then_inc(up_ready, 1)

            pe.wait_ge(down_low, WCH + 1)
            pe.wait_ge(up_low, WCH + 1)
            pe.wait_ge(x_low, NB)
            FRONT, BACK = range(0, 4), range(4, NTG)
            down_products(0, range(0, 6))
            transpose_picks(0, 1, bank=2)
            down_products(0, range(6, NHG))
            gate_matrices(0, FRONT, first=True)
            gate_matrices(0, BACK, first=True)
            transpose_picks(1, 1)
            down_products(1, picks=2)

            def expert_step(t, first=False, more=True):
                gate_matrices(t, FRONT)
                if more:
                    transpose_picks(t + 1, t + 1)
                up_product(t - 1, 0, NHG // 4, first)
                gate_matrices(t, BACK)
                up_product(t - 1, NHG // 4, NHG)
                if more:
                    down_products(t + 1, picks=t + 2)

            pe.wait_ge(sim_copied, NC2)
            expert_step(1, first=True)
            with pe.Fori(2, NT - 1) as t:
                expert_step(t)
            expert_step(NT - 1, more=False)
            up_product(NT - 1, 0, NHG)

        @block.scalar
        def _(act):
            A = nc.scalar.activation
            act.dma_start(posb[:], pos).then_inc(ld_pos, 16)
            act.dma_start(tokb[:], tok_b).then_inc(ld_tokb, 16)
            act.dma_start(ident[:], ident_in).then_inc(ld_ident, 16)
            act.dma_start(qw[:], qw_in).then_inc(ld_qw, 16)
            act.dma_start(kw[:], kw_in).then_inc(ld_kw, 16)
            act.dma_start(wq[:], wq_in).then_inc(ld_wq, 16)
            act.dma_start(wkv[:], wkv_in).then_inc(ld_wkv, 16)

            def square_d(g, first=False):
                act.wait_ge(d_ready, g + 1)
                if not first:
                    act.wait_ge(var_ready, g)
                A(sq1[:], d1[:], ACT.Square).then_inc(sq_ready, 1)
                if not first:
                    act.wait_ge(kv_ready, g)
                A(d1r[:, 0, :, 0:GT], d1[:], ACT.Copy).then_inc(dr_high, 1)

            def square_qk(g, part, first=False):
                bank, h0, n = QK_PARTS[part]
                if not first:
                    act.wait_ge(msum_ready, g * 3)
                act.wait_ge((q0_ready, q1_ready, kv_ready)[part], g + 1)
                A(sqq[:, h0:h0 + n, :].rearrange("p h d -> p (h d)"), ps[0:GT, bank, 0:n * HD],
                  ACT.Square).then_inc(sqq_ready[part], 1)

            def copy_v(g):
                act.wait_ge(rinv_ready, g * 2 + 2)
                A(vall[:, ds(g, 1), :].rearrange("p o n -> p (o n)"), ps[0:GT, 3, 256:512], ACT.Copy,
                  scale=rinv[:, HEADS + KV_HEADS:HEADS + KV_HEADS + 1]).then_inc(v_ready, 1)

            def copy_qk(g, first=False):
                act.wait_ge(qkt_ready, g + 1)
                if not first:
                    act.wait_ge(score_ready[2], g)
                for n in range(2):
                    A(qT[:, 4 * n:4 * n + 4, :], ps[:, 4 + n, 0:4 * GT].rearrange("p (c t) -> p c t", t=GT), ACT.Copy)
                A(kT[:], ps[:, 7, 0:2 * GT].rearrange("p (c t) -> p c t", t=GT), ACT.Copy,
                  scale=kscale[:, 0:1]).then_inc(qkt_copied, 1)

            def exps(g, kv):
                act.wait_ge(max_ready[kv], g + 1)
                for i in range(REP):
                    last = A(sm[:, kv, i, :], sm[:, kv, i, :], ACT.Exp, bias=nmax[:, kv, i:i + 1],
                             accum_out=psums[:, REP * kv + i:REP * kv + i + 1])
                last.then_inc(exp_ready, 1)

            def copy_pt(g):
                act.wait_ge(pt_ready, g * KV_HEADS + 2)
                for kv in range(2):
                    last = A(pT[:, kv].rearrange("p i q -> p (i q)"), ps[0:GT, 4 + kv, 0:REP * GT], ACT.Copy)
                last.then_inc(pt_copied_act, 1)

            def copy_o(g):
                act.wait_ge(o_ready, g * 2 + 1)
                A(oT[:, 0:QC:2, :], ps[:, 4, 0:REP * GT].rearrange("p (c t) -> p c t", t=GT), ACT.Copy).then_inc(o_copied_act, 1)

            def square_table(n):
                table, piece = n // (FC * EXPERTS // SQN), n % (FC * EXPERTS // SQN)
                act.wait_ge((ld_down, ld_up)[table], 16)
                if n:
                    act.wait_ge(wsq_ready, n)
                slot = table * (WCH + 1) + 1 + piece * (SQN // WN)
                A(tables[:, 0, :].bitcast(bf16), tables[:, slot:slot + SQN // WN, :].rearrange("p s n -> p (s n)"),
                  ACT.Square, accum_out=wsq[:, table, piece:piece + 1]).then_inc(wsq_ready, 1)

            def table_high(n):
                for table, low, high in ((0, down_low, down_high), (1, up_low, up_high)):
                    act.wait_ge(low, n + 1)
                    s0 = table * (WCH + 1)
                    A(halves[:, ds(n + s0, 1), 0:WN].rearrange("p o n -> p (o n)"),
                      tables[:, ds(n + s0 + 1, 1), :].rearrange("p o n -> p (o n)"), ACT.Copy,
                      scale=wscale[:, table:table + 1]).then_inc(high, 1)

            for k in range(KF, KC):
                act.wait_ge(ld_tokw[k], 16)
                if k > KF + 2:
                    act.wait_ge(emb_used, k - KF - 2)
                A(tokwr[:, k % 3, 0], tokw[:, k, :], ACT.Copy).then_inc(emb_high, 1)
                act.wait_ge(ld_x[k], 16)
                A(xer[:, k % 3, 0], xT[:, k, :], ACT.Copy).then_inc(emb_high, 1)
                if k == KC - 1:
                    act.wait_ge(ld_wq, 16)
                    A(wqr[:, 0], wq[:], ACT.Copy).then_inc(wqkv_high, 1)
                    act.wait_ge(ld_wkv, 16)
                    A(wkvr[:, 0], wkv[:], ACT.Copy).then_inc(wqkv_high, 1)
            act.wait_ge(kscale_ready, 1)
            square_d(0, first=True)
            for part in range(3):
                square_qk(0, part, first=True)
            square_d(1)
            square_table(0)
            copy_v(0)
            square_table(1)
            square_table(2)
            copy_qk(0, first=True)
            square_table(3)
            square_qk(1, 0)
            square_table(4)
            exps(0, 0)
            exps(0, 1)
            square_qk(1, 1)
            exps(0, 3)
            square_qk(1, 2)
            exps(0, 2)
            square_d(2)
            copy_v(1)
            square_table(5)

            def attention_step(i, projections=True, means=True, first=False):
                copy_qk(i + 1)
                if first:
                    square_table(6)
                if projections:
                    square_qk(i + 2, 0)
                if first:
                    square_table(7)
                elif projections:
                    table_high(i - 1)
                exps(i + 1, 0)
                if projections:
                    square_qk(i + 2, 1)
                exps(i + 1, 1)
                copy_pt(i)
                if projections:
                    square_qk(i + 2, 2)
                copy_o(i)
                exps(i + 1, 3)
                if projections:
                    copy_v(i + 2)
                exps(i + 1, 2)
                if means:
                    square_d(i + 3)

            attention_step(0, first=True)
            with act.Fori(1, NG - 3) as i:
                attention_step(i)
            attention_step(NG - 3, means=False)
            attention_step(NG - 2, projections=False, means=False)
            copy_pt(NG - 1)
            copy_o(NG - 1)

            for b in range(NB):
                act.wait_ge(d2_ready, b + 1)
                if b > 1:
                    act.wait_ge(var2_ready, b - 1)
                A(sq2[:, b % 2], xnT[:, :, b * BLK:(b + 1) * BLK], ACT.Square).then_inc(sq2_ready, 1)

            def weights_high(c, s, load, first=False):
                act.wait_ge(ld_wqc[s], load)
                if not first:
                    act.wait_ge(fq_ready, c - 1)
                A(wr[:, s, 0], wqc[:, s], ACT.Copy).then_inc(wr_high, 1)

            weights_high(0, 0, 16, first=True)
            weights_high(1, 1, 16, first=True)
            for b in range(NB):
                act.wait_ge(xn_ready, b + 1)
                A(xr[:, 0, :, b * BLK:(b + 1) * BLK], xnT[:, :, b * BLK:(b + 1) * BLK], ACT.Copy).then_inc(xr_high, 1)
            for b in range(NB):
                A(xh[:, :, b * BLK:(b + 1) * BLK], xnT[:, :, b * BLK:(b + 1) * BLK], ACT.Copy).then_inc(x_high, 1)

            def affine(c, s, first=False):
                act.wait_ge(bnb_ready, c + 1)
                if not first:
                    act.wait_ge(sim_ready, c - 1)
                for b in range(NB):
                    last = A(qb[:, s, b * BLK:(b + 1) * BLK], ps[:, 3 * s + b, 0:BLK], ACT.Identity,
                             bias=bnb[:, s:s + 1], scale=bna[:, s:s + 1])
                last.then_inc(qb_ready, 1)

            def copy_sim(c, s, first=False):
                act.wait_ge(sim_ready, c + 1)
                if not first:
                    act.wait_ge(topi_ready, c - 1)
                A(sims[:, s, 0:8, :].rearrange("p t k -> p (t k)"), ps[:, 6, :], ACT.Copy)
                A(sims[:, s, 8, :], ps[:, 7, 0:KEYS], ACT.Copy).then_inc(sim_copied, 1)

            weights_high(2, 0, 32)
            affine(0, 0, first=True)
            weights_high(3, 1, 32)
            affine(1, 1, first=True)
            copy_sim(0, 0, first=True)
            weights_high(4, 0, 48)
            affine(2, 0)
            copy_sim(1, 1, first=True)
            weights_high(5, 1, 48)
            affine(3, 1)
            copy_sim(2, 0)
            with act.Fori(2, NC2 // 2 - 1) as j:
                for s in range(2):
                    weights_high(2 * j + 2 + s, s, 16 * j + 32)
                    affine(2 * j + s, s)
                    copy_sim(2 * j + s - 1, 1 - s)
            affine(NC2 - 2, 0)
            copy_sim(NC2 - 3, 1)
            affine(NC2 - 1, 1)
            copy_sim(NC2 - 2, 0)
            copy_sim(NC2 - 1, 1)

            def gelus(t, ks=range(NHG), first=False):
                if not first:
                    act.wait_ge(a_low, t * 2)
                for k in ks:
                    act.wait_ge(down_ready, t * NHG + k + 1)
                    A(act_h[:, HG * k:HG * (k + 1), :].rearrange("p c t -> p (c t)"), ps[:, k % 2, :],
                      ACT.Gelu_apprx_tanh, scale=hscale[:, 0:1]).then_inc(gelu_ready, 1)

            def high_parts(t, half, first=False):
                act.wait_ge(acts_ready, t * NTG + (half + 1) * (NTG // 2))
                if half == 0 and not first:
                    act.wait_ge(up_ready, t - 1)
                A(ah[:, ds(t % 2, 1), :, half * 64:half * 64 + 64].rearrange("p o c t -> p (o c) t"),
                  act_h[:, :, half * 64:half * 64 + 64], ACT.Copy).then_inc(a_high, 1)

            def exp_gates(t):
                act.wait_ge(dif_ready, t + 1)
                A(ex[:], dif[:], ACT.Exp).then_inc(ex_ready, 1)

            def copy_picks(t, first=False, bank=0):
                act.wait_ge(picks_tr, t + 1)
                if not first:
                    act.wait_ge(gated, t)
                    act.wait_ge(lo_hot, t)
                A(picksT[:].rearrange("p n t -> p (n t)"), ps[:, bank, 0:384], ACT.Copy)
                for m in range(3):
                    last = A(loT[:, m, :], ps[:, bank, 0:128], ACT.Identity, bias=digit_shift[:, m:m + 1])
                last.then_inc(picks_copied, 1)

            def copy_up(t, first=False):
                act.wait_ge(up_ready, t + 1)
                if not first:
                    act.wait_ge(sum_ready, t)
                for f in range(FC):
                    last = A(upout[:, f, :], ps[:, 6 + f, 0:128], ACT.Copy, scale=oscale[:, 0:1])
                last.then_inc(up_copied, 1)

            gelus(0, range(0, 2), first=True)
            exp_gates(0)
            gelus(0, range(2, 6), first=True)
            copy_picks(0, first=True, bank=2)
            gelus(0, range(6, NHG), first=True)
            exp_gates(1)
            high_parts(0, 0, first=True)
            high_parts(0, 1, first=True)
            copy_picks(1)
            exp_gates(2)
            gelus(1)

            def expert_step(t, first=False, scores=True, more=True):
                if more:
                    copy_picks(t + 1)
                high_parts(t, 0, first)
                if scores:
                    exp_gates(t + 2)
                high_parts(t, 1, first)
                copy_up(t - 1, first)
                if more:
                    gelus(t + 1)

            expert_step(1, first=True)
            with act.Fori(2, NT - 2) as t:
                expert_step(t)
            expert_step(NT - 2, scores=False)
            expert_step(NT - 1, scores=False, more=False)
            copy_up(NT - 1)

        @block.vector
        def _(dve):
            V = nc.vector

            def centre(g, first=False):
                dve.wait_ge(mean_ready, g + 1)
                if not first:
                    dve.wait_ge(dr_high, g)
                    dve.wait_ge(dr_low, g)
                V.tensor_tensor(d1[:], hT[:, :, ds(g * GT, GT)], spread(ps[:, 0, 0:GT], 1, FC), ALU.subtract).then_inc(d_ready, 1)

            def centred_low(g, first=False):
                dve.wait_ge(dr_high, g + 1)
                if not first:
                    dve.wait_ge(kv_ready, g)
                V.tensor_tensor(d1r[:, 1, :, 0:GT], d1[:], d1r[:, 0, :, 0:GT].bitcast(fp32), ALU.subtract).then_inc(dr_low, 1)

            def layer_norm_variance(g, first=False):
                dve.wait_ge(var_ready, g + 1)
                if not first:
                    dve.wait_ge(rinv_ready, g * 2)
                V.tensor_scalar(rmsv[:, HEADS + KV_HEADS:], ps[0:GT, 0, 256:257], LN_EPS, None, ALU.add)
                V.tensor_scalar(vare[:], ps[0:GT, 0, 256:257], LN_EPS, RMS_EPS, ALU.add, ALU.mult).then_inc(vare_ready, 1)

            def rms_sums(g, part):
                _, h0, n = QK_PARTS[part]
                dve.wait_ge(sqq_ready[part], g + 1)
                V.reduce_sum(msum[:, h0:h0 + n], sqq[:, h0:h0 + n, :], AX.X).then_inc(msum_ready, 1)

            def rms_values(g, part):
                dve.wait_ge(msum_ready, g * 3 + 2 + part)
                dve.wait_ge(vare_ready, g + 1)
                h0, h1 = ((0, HEADS), (HEADS, HEADS + KV_HEADS))[part]
                V.tensor_scalar(rmsv[:, h0:h1], msum[:, h0:h1], 1.0 / HD, vare[:, 0:1], ALU.mult, ALU.add).then_inc(rmsv_ready, 1)

            def normalise_qk(g, first=False):
                dve.wait_ge(rinv_ready, g * 2 + 1)
                if not first:
                    dve.wait_ge(qkt_ready, g)
                for bank, h0, n in QK_PARTS:
                    if bank == 3:
                        dve.wait_ge(rinv_ready, g * 2 + 2)
                        dve.wait_ge(v_ready, g + 1)
                    last = V.tensor_tensor(qkn[:, h0:h0 + n, :], ps[0:GT, bank, 0:n * HD].rearrange("p (h d) -> p h d", d=HD),
                                           spread(rinv[:, h0:h0 + n], 2, HD), ALU.mult)
                last.then_inc(qkn_ready, 1)

            def add_bias(g, kv, first=False):
                if kv == 0 and not first:
                    dve.wait_ge(pn_ready, g)
                dve.wait_ge(score_ready[kv], g + 1)
                V.tensor_tensor(sm[:, kv].rearrange("p i k -> p (i k)"), ps[0:GT, 4 + kv, 0:REP * GT],
                                bias[:, kv].rearrange("p i k -> p (i k)"), ALU.add).then_inc(biased[kv], 1)

            def neg_max(g, kv):
                dve.wait_ge(biased[kv], g + 1)
                V.reduce_max(nmax[:, kv, :], sm[:, kv], AX.X, negate=True).then_inc(max_ready[kv], 1)

            def invert_sums(g):
                dve.wait_ge(exp_ready, (g + 1) * KV_HEADS)
                V.reciprocal(pinv[:], psums[:]).then_inc(pinv_ready, 1)

            def copy_pt(g):
                dve.wait_ge(pt_ready, (g + 1) * KV_HEADS)
                for kv in range(2, KV_HEADS):
                    last = V.tensor_copy(pT[:, kv].rearrange("p i q -> p (i q)"), ps[0:GT, 4 + kv, 0:REP * GT])
                last.then_inc(pt_copied_dve, 1)

            def copy_o(g):
                dve.wait_ge(o_ready, (g + 1) * 2)
                V.tensor_copy(oT[:, 1:QC:2, :], ps[:, 5, 0:REP * GT].rearrange("p (c t) -> p c t", t=GT)).then_inc(o_copied_dve, 1)

            def residual(g):
                dve.wait_ge(wo_ready, g + 1)
                V.tensor_tensor(hT[:, :, ds(g * GT, GT)], hT[:, :, ds(g * GT, GT)],
                                ps[:, 6, 0:FC * GT].rearrange("p (f t) -> p f t", t=GT), ALU.add).then_inc(h2_ready, 1)

            dve.wait_ge(ld_pos, 16)
            dve.wait_ge(ld_tokb, 16)
            V.tensor_tensor(posb[:], posb[:], spread(tokb[:], 2, PATCHES), ALU.add).then_inc(posb_ready, 1)
            dve.wait_ge(ld_qw, 16)
            dve.wait_ge(ld_kw, 16)
            V.tensor_scalar(kscale[:], qw[:], kw[:, 0:1], HD ** -0.5, ALU.mult, ALU.mult).then_inc(kscale_ready, 1)
            V.memset(d1[:], 0.0).then_inc(pad_ready, 1)
            dve.wait_ge(pad_ready, 1)
            V.tensor_copy(d1r[:, :, :, GT:128], d1[:, :, 0:2 * (128 - GT)].rearrange("p f (a t) -> p a f t", a=2)).then_inc(pad_ready, 1)
            for k in range(KF, KC):
                for i, (split, raw) in enumerate(((tokwr, tokw), (xer, xT))):
                    dve.wait_ge(emb_high, 2 * (k - KF) + i + 1)
                    V.tensor_tensor(split[:, k % 3, 1], raw[:, k, :], split[:, k % 3, 0].bitcast(fp32), ALU.subtract).then_inc(emb_low, 1)
                if k == KC - 1:
                    for n, (raw, split) in enumerate(((wq, wqr), (wkv, wkvr))):
                        dve.wait_ge(wqkv_high, n + 1)
                        V.tensor_tensor(split[:, 1], raw[:], split[:, 0].bitcast(fp32), ALU.subtract).then_inc(wqkv_low, 1)
            dve.wait_ge(posb_ready, 1)
            for b, (t0, n) in enumerate(blocks1):
                for f in range(FC):
                    dve.wait_ge(embedded, 2 * b + f + 1)
                    V.tensor_tensor(hT[:, f, t0:t0 + n].rearrange("p (b t) -> p b t", t=PATCHES),
                                    ps[:, 2 * b + f, 0:n].rearrange("p (b t) -> p b t", t=PATCHES),
                                    spread(posb[:, f, :], 1, n // PATCHES), ALU.add).then_inc(h_ready, 1)
            dve.wait_ge(h_ready, FC * len(blocks1))
            dve.wait_ge(const_ready, 1)
            dve.wait_ge(ld_bias, 16)
            dve.wait_ge(pad_ready, 2)
            centre(0, first=True)
            centred_low(0, first=True)
            layer_norm_variance(0, first=True)
            rms_sums(0, 0)
            rms_sums(0, 1)
            rms_values(0, 0)
            rms_sums(0, 2)
            rms_values(0, 1)
            centre(1)
            centred_low(1)
            normalise_qk(0, first=True)

            def softmax_step(g, first=False, projections=True, last=None):
                if projections:
                    layer_norm_variance(g + 1)
                add_bias(g, 0, first)
                if projections:
                    rms_sums(g + 1, 0)
                add_bias(g, 1, first)
                neg_max(g, 0)
                add_bias(g, 3, first)
                neg_max(g, 1)
                add_bias(g, 2, first)
                neg_max(g, 3)
                neg_max(g, 2)
                if projections:
                    rms_sums(g + 1, 1)
                    rms_values(g + 1, 0)
                if last is not None:
                    copy_pt(last)
                if projections:
                    rms_sums(g + 1, 2)
                    rms_values(g + 1, 1)

            def table_sums():
                dve.wait_ge(wsq_ready, 2 * FC * EXPERTS // SQN)
                V.reduce_sum(wsum[:], wsq[:], AX.X).then_inc(wsum_ready, 1)

            def table_scales():
                dve.wait_ge(wtotal_ready, 1)
                V.tensor_scalar(wmean[:], ps[:, 0, 300:302], 1e-30, None, ALU.max).then_inc(wmean_ready, 1)
                dve.wait_ge(wroot_ready, 1)
                V.tensor_scalar(wpow[:].bitcast(i32), wpow[:].bitcast(i32), 0x7F800000, None, ALU.bitwise_and).then_inc(wpow_ready, 1)
                dve.wait_ge(wpow_ready, 1)
                V.reciprocal(winv[:], wpow[:]).then_inc(winv_ready, 1)
                V.tensor_scalar(wscale[:], wpow[:], W_SCALE, None, ALU.mult)
                V.tensor_scalar(ascale[:], wpow[:, 0:1], A_SCALE / GATE_SCALE, None, ALU.mult)
                dve.wait_ge(winv_ready, 1)
                V.tensor_scalar(hscale[:], winv[:, 0:1], 1.0 / (X_SCALE * W_SCALE), None, ALU.mult).then_inc(down_low, 1)
                V.tensor_scalar(oscale[:], winv[:, 0:1], winv[:, 1:2], 1.0 / (A_SCALE * W_SCALE), ALU.mult, ALU.mult).then_inc(up_low, 1)

            def table_low(n, tables_of):
                for table, low, high in tables_of:
                    dve.wait_ge(high, n + 1)
                    s0 = table * (WCH + 1)
                    V.scalar_tensor_tensor(halves[:, ds(n + s0, 1), WN:].rearrange("p o n -> p (o n)"),
                                           tables[:, ds(n + s0 + 1, 1), :].rearrange("p o n -> p (o n)"),
                                           wscale[:, table:table + 1],
                                           halves[:, ds(n + s0, 1), 0:WN].rearrange("p o n -> p (o n)"),
                                           ALU.mult, ALU.subtract).then_inc(low, 1)

            softmax_step(0, first=True)
            centre(2)
            invert_sums(0)
            centred_low(2)
            normalise_qk(1)

            def attention_step(i, projections=True, means=True, first=False):
                softmax_step(i + 1, projections=projections, last=i)
                if first:
                    table_sums()
                copy_o(i)
                if means:
                    centre(i + 3)
                if projections:
                    normalise_qk(i + 2)
                invert_sums(i + 1)
                residual(i)
                if means:
                    centred_low(i + 3)
                if first:
                    table_scales()
                elif projections:
                    table_low(i - 1, ((0, down_low, down_high), (1, up_low, up_high)))

            attention_step(0, first=True)
            with dve.Fori(1, NG - 3) as i:
                attention_step(i)
            attention_step(NG - 3, means=False)
            attention_step(NG - 2, projections=False, means=False)
            copy_pt(NG - 1)
            copy_o(NG - 1)
            residual(NG - 1)

            dve.wait_ge(h2_ready, NG)
            for b in range(NB):
                dve.wait_ge(mean2_ready, b + 1)
                V.tensor_tensor(xnT[:, :, b * BLK:(b + 1) * BLK], hT[:, :, b * BLK:(b + 1) * BLK],
                                spread(ps[:, b, 0:BLK], 1, FC), ALU.subtract).then_inc(d2_ready, 1)
            def token_low(b):
                dve.wait_ge(xr_high, b + 1)
                V.tensor_tensor(xr[:, 1, :, b * BLK:(b + 1) * BLK], xnT[:, :, b * BLK:(b + 1) * BLK],
                                xr[:, 0, :, b * BLK:(b + 1) * BLK].bitcast(fp32), ALU.subtract).then_inc(xr_low, 1)

            for b in range(NB):
                dve.wait_ge(var2_ready, b + 1)
                V.tensor_scalar(var2[:, b * BT:(b + 1) * BT], ps[:, 6 + b % 2, 0:BT], LN_EPS, None, ALU.add).then_inc(veps_ready, 1)
            for b in range(NB):
                dve.wait_ge(rstd2_ready, b + 1)
                for t in range(b * BT, (b + 1) * BT):
                    last = V.tensor_scalar(diag[:, t, :], ident[:], rstd2[:, t:t + 1], X_SCALE * DIM, ALU.mult, ALU.mult)
                last.then_inc(diag_ready, 1)

            def normalise_block(b):
                dve.wait_ge(spread_ready, b + 1)
                V.tensor_tensor(xnT[:, :, b * BLK:(b + 1) * BLK], xnT[:, :, b * BLK:(b + 1) * BLK],
                                spread(ps[:, 3 + b, 0:BLK], 1, FC), ALU.mult).then_inc(xn_ready, 1)

            normalise_block(0)
            normalise_block(1)
            token_low(0)
            normalise_block(2)
            token_low(1)
            token_low(2)

            def batch_variance(c, s, first=False):
                dve.wait_ge(fq_ready, c + 1)
                if not first:
                    dve.wait_ge(mv_ready, c - 1)
                for b in range(NB):
                    last = V.bn_stats(stats[:, s, b, :], ps[:, 3 * s + b, 0:BLK])
                last.then_inc(stats_ready, 1)
                dve.wait_ge(stats_ready, c + 1)
                if not first:
                    dve.wait_ge(bnb_ready, c - 1)
                dve.nop(nofuse=True)
                V.bn_aggr(mv[:, s], stats[:, s].rearrange("p b n -> p (b n)")).then_inc(mv_ready, 1)

            def top_values(c, s, first=False):
                dve.wait_ge(sim_copied, c + 1)
                if not first:
                    dve.wait_ge(top_kept, c - 1)
                dve.nop(nofuse=True)
                for t in range(NT):
                    last = V.max(best_s[:, s, t, :], sims[:, s, t, :])
                last.then_inc(tops_ready, 1)

            def top_places(c, s):
                dve.wait_ge(tops_ready, c + 1)
                dve.nop(nofuse=True)
                for t in range(NT):
                    last = V.max_index(best_i[:, s, t, :], best_s[:, s, t, :], sims[:, s, t, :])
                last.then_inc(topi_ready, 1)

            for c in range(2):
                batch_variance(c, c, first=True)

            def router_step(c, s, first=False):
                batch_variance(c, s)
                if not (first and c == 2):
                    top_places(c - 3, 1 - s)
                top_values(c - 2, s, first)

            router_step(2, 0, first=True)
            router_step(3, 1, first=True)
            with dve.Fori(2, NC2 // 2) as j:
                router_step(2 * j, 0)
                router_step(2 * j + 1, 1)
            top_places(NC2 - 3, 1)
            top_values(NC2 - 2, 0)
            top_places(NC2 - 2, 0)
            top_values(NC2 - 1, 1)
            top_places(NC2 - 1, 1)

            def best_scores(t, first=False):
                sx = top_s[:, ds(t, 1), 0:FH, :].rearrange("p o h k -> p (o h) k")
                sy = top_s[:, ds(t, 1), FH:NC2, :].rearrange("p o h k -> p (o h) k")
                V.tensor_tensor(comb[:], spread(sx, 3, TOPK), spread(sy, 2, TOPK), ALU.add).then_inc(comb_ready, 1)
                dve.wait_ge(comb_ready, t + 1)
                dve.nop(nofuse=True)
                for h in range(FH):
                    last = V.max(best[:, h, :], comb[:, h].rearrange("p a b -> p (a b)"))
                last.then_inc(best_ready, 1)
                dve.wait_ge(best_ready, t + 1)
                if not first:
                    dve.wait_ge(ex_ready, t)
                V.tensor_tensor(dif[:], best[:], best[:, :, 0:1].broadcast_to([128, FH, TOPK]), ALU.subtract).then_inc(dif_ready, 1)

            def choose(t, first=False):
                ix = top_i[:, ds(t, 1), 0:FH, :].rearrange("p o h k -> p (o h) k")
                iy = top_i[:, ds(t, 1), FH:NC2, :].rearrange("p o h k -> p (o h) k")
                for h in range(FH):
                    last = V.max_index(pick[:, h, :], best[:, h, :], comb[:, h].rearrange("p a b -> p (a b)"))
                last.then_inc(pick_ready, 1)
                dve.wait_ge(ex_ready, t + 1)
                V.reduce_sum(zs[:], ex[:], AX.X).then_inc(zs_ready, 1)
                dve.wait_ge(pick_ready, t + 1)
                V.tensor_scalar(pick_a[:], pick[:].bitcast(i32), 3, None, ALU.logical_shift_right)
                V.tensor_scalar(pick_b[:], pick[:].bitcast(i32), TOPK - 1, None, ALU.bitwise_and).then_inc(pickab_ready, 1)
                dve.wait_ge(zs_ready, t + 1)
                V.reciprocal(zi[:], zs[:]).then_inc(zi_ready, 1)
                dve.wait_ge(pickab_ready, t + 1)
                ranks = spread(spread(iota8[:], 1, TOPK), 1, FH)
                V.tensor_tensor(mask_a[:], spread(pick_a[:], 3, TOPK), ranks, ALU.is_equal)
                V.tensor_tensor(mask_b[:], spread(pick_b[:], 3, TOPK), ranks, ALU.is_equal).then_inc(mask_ready, 1)
                dve.wait_ge(zi_ready, t + 1)
                if not first:
                    dve.wait_ge(picks_tr, t)
                V.scalar_tensor_tensor(gate2[:, 0, :].rearrange("p (h k) -> p h k", k=TOPK), ex[:], GATE_SCALE,
                                       spread(zi[:], 2, TOPK), ALU.mult, ALU.mult).then_inc(gate_ready, 1)
                dve.wait_ge(mask_ready, t + 1)
                V.tensor_tensor(mask_a[:], mask_a[:], spread(ix, 2, TOPK), ALU.mult)
                V.tensor_tensor(mask_b[:], mask_b[:], spread(iy, 2, TOPK), ALU.mult).then_inc(masked_ready, 1)
                dve.wait_ge(gate_ready, t + 1)
                V.tensor_copy(gate16[:], gate2[:, 0, :]).then_inc(gate16_ready, 1)
                dve.wait_ge(masked_ready, t + 1)
                V.reduce_sum(key_i[:], mask_a[:], AX.X)
                V.reduce_sum(key_j[:], mask_b[:], AX.X).then_inc(key_ready, 1)
                dve.wait_ge(gate16_ready, t + 1)
                V.tensor_tensor(gate2[:, 1, :], gate2[:, 0, :], gate16[:], ALU.subtract).then_inc(gate2_ready, 1)
                dve.wait_ge(key_ready, t + 1)
                V.scalar_tensor_tensor(expert[:], key_i[:].rearrange("p h k -> p (h k)"), float(KEYS),
                                       key_j[:].rearrange("p h k -> p (h k)"), ALU.mult, ALU.add).then_inc(expert_ready, 1)
                dve.wait_ge(expert_ready, t + 1)
                V.tensor_scalar(e_lo[:], expert[:], 127, None, ALU.bitwise_and)
                V.tensor_scalar(e_hi[:], expert[:], 7, None, ALU.logical_shift_right).then_inc(elohi_ready, 1)
                dve.wait_ge(elohi_ready, t + 1)
                V.tensor_copy(lo2[:], spread(e_lo[:], 1, 2))
                V.tensor_copy(hi2[:], spread(e_hi[:], 1, 2)).then_inc(lohi2_ready, 1)

            def one_hots(t, first=False):
                dve.wait_ge(picks_copied, t + 1)
                if not first:
                    dve.wait_ge(gate_mm, t * NTG)
                V.tensor_tensor(gated_hi[:], iota32[:], spread(picksT[:, 1, :], 1, EC), ALU.is_equal).then_inc(hi_hot, 1)
                for m in range(4):
                    src = picksT[:, 0, :] if m == 0 else loT[:, m - 1, :]
                    last = V.tensor_tensor(onehot_lo[:, 32 * m:32 * m + 32, :], iota32[:], spread(src, 1, EC), ALU.is_equal)
                last.then_inc(lo_hot, 1)

            def gate_hidden(t, ks):
                if ks[0] == 0:
                    dve.wait_ge(gelu_ready, (t + 1) * NHG)
                for k in ks:
                    dve.wait_ge(gate_mm, t * NTG + k + 1)
                    h = act_h[:, :, k * TG:(k + 1) * TG]
                    V.scalar_tensor_tensor(h, ps[:, 2 + k % 4, :].rearrange("p (t c) -> p c t", c=EC), ascale[:, 0:1], h,
                                           ALU.mult, ALU.mult).then_inc(acts_ready, 1)

            dve.wait_ge(top_kept, NC2)
            dve.wait_ge(iota_ready, 1)
            FRONT, BACK = range(0, 4), range(4, NTG)
            best_scores(0, first=True)
            choose(0, first=True)
            best_scores(1)
            dve.wait_ge(iota_ready, 2)
            one_hots(0, first=True)
            gate_hidden(0, FRONT)
            gate_hidden(0, BACK)
            choose(1)
            best_scores(2)
            one_hots(1)
            choose(2)

            def expert_step(t, scores=True, more=True):
                gate_hidden(t, FRONT)
                if scores:
                    best_scores(t + 2)
                gate_hidden(t, BACK)
                if scores:
                    choose(t + 2)
                if more:
                    one_hots(t + 1)

            with dve.Fori(1, NT - 2) as t:
                expert_step(t)
            expert_step(NT - 2, scores=False)
            expert_step(NT - 1, scores=False, more=False)

        @block.gpsimd
        def _(pool):
            P = nc.gpsimd
            NQK = HEADS + KV_HEADS + 1

            def inverse_roots(g, first=False):
                pool.wait_ge(rmsv_ready, g * 2 + 1)
                if not first:
                    pool.wait_ge(v_ready, g)
                    pool.wait_ge(qkn_ready, g)
                P.tensor_tensor(rinv[:, 0:HEADS], rmsv[:, 0:HEADS], half_neg[0:GT, 0:HEADS], ALU.pow).then_inc(rinv_ready, 1)
                pool.wait_ge(rmsv_ready, g * 2 + 2)
                P.tensor_tensor(rinv[:, HEADS:NQK], rmsv[:, HEADS:NQK], half_neg[0:GT, HEADS:NQK], ALU.pow).then_inc(rinv_ready, 1)

            def normalise_p(g, first=False):
                pool.wait_ge(pinv_ready, g + 1)
                if not first:
                    pool.wait_ge(pt_ready, g)
                P.tensor_tensor(pn[:], sm[:].rearrange("p a b k -> p (a b) k"), spread(pinv[:], 2, GT), ALU.mult).then_inc(pn_ready, 1)

            def current_v(g, first=False):
                pool.wait_ge(v_ready, g + 1)
                if not first:
                    pool.wait_ge(o_ready, g * 2)
                P.tensor_copy(vcur[:], vall[:, ds(g, 1), :].rearrange("p o n -> p (o n)")).then_inc(vcur_ready, 1)

            P.memset(mean_w[:], 1.0 / DIM)
            P.memset(half_neg[:], -0.5)
            for m in range(3):
                P.memset(digit_shift[:, m:m + 1], -32.0 * (m + 1))
            P.memset(eps_bn[:], LN_EPS * X_SCALE ** 2)
            P.memset(hT[:, :, TOK:PAD_TOK], 0.0).then_inc(const_ready, 1)
            pool.wait_ge(const_ready, 1)
            inverse_roots(0, first=True)
            inverse_roots(1)
            normalise_p(0, first=True)
            current_v(0, first=True)
            inverse_roots(2)
            pool.wait_ge(wmean_ready, 1)
            P.tensor_tensor(wpow[:], wmean[:], half_neg[:, 0:2], ALU.pow).then_inc(wroot_ready, 1)
            normalise_p(1)
            current_v(1)
            with pool.Fori(2, NG - 1) as i:
                inverse_roots(i + 1)
                normalise_p(i)
                current_v(i)
            normalise_p(NG - 1)
            current_v(NG - 1)

            pool.wait_ge(h2_ready, NG)
            P.iota(iota8[:], [[1, TOPK]], base=0, channel_multiplier=0, allow_small_or_imprecise_dtypes=True).then_inc(iota_ready, 1)

            for b in range(NB):
                pool.wait_ge(veps_ready, b + 1)
                P.tensor_tensor(rstd2[:, b * BT:(b + 1) * BT], var2[:, b * BT:(b + 1) * BT],
                                half_neg[:, 0:BT], ALU.pow).then_inc(rstd2_ready, 1)

            def batch_scale(c, s, first=False):
                pool.wait_ge(mv_ready, c + 1)
                P.tensor_tensor(bnv[:], mv[:, s, 1:2], eps_bn[:], ALU.add).then_inc(bnv_ready, 1)
                pool.wait_ge(bnv_ready, c + 1)
                P.tensor_tensor(rstd[:], bnv[:], half_neg[:, 0:1], ALU.pow).then_inc(rstd_ready, 1)
                pool.wait_ge(rstd_ready, c + 1)
                if not first:
                    pool.wait_ge(qb_ready, c - 1)
                P.tensor_tensor(bna[:, s:s + 1], gamma[:, ds(c, 1)], rstd[:], ALU.mult).then_inc(bna_ready, 1)
                pool.wait_ge(bna_ready, c + 1)
                P.tensor_tensor(bnm[:], mv[:, s, 0:1], bna[:, s:s + 1], ALU.mult).then_inc(bnm_ready, 1)
                pool.wait_ge(bnm_ready, c + 1)
                P.tensor_tensor(bnb[:, s:s + 1], beta[:, ds(c, 1)], bnm[:], ALU.subtract).then_inc(bnb_ready, 1)

            def keep_top(c, s):
                pool.wait_ge(topi_ready, c + 1)
                P.tensor_copy(top_s[:, :, ds(c, 1), :].rearrange("p t o k -> p t (o k)"), best_s[:, s])
                P.tensor_copy(top_i[:, :, ds(c, 1), :].rearrange("p t o k -> p t (o k)"), best_i[:, s]).then_inc(top_kept, 1)

            def weights_low(c, s):
                pool.wait_ge(wr_high, c + 1)
                P.tensor_tensor(wr[:, s, 1], wqc[:, s], wr[:, s, 0].bitcast(fp32), ALU.subtract).then_inc(wr_low, 1)

            weights_low(0, 0)
            weights_low(1, 1)
            pool.wait_ge(ld_gamma, 16)
            pool.wait_ge(ld_beta, 16)
            for c in range(2):
                batch_scale(c, c, first=True)
                weights_low(c + 2, c)
            for b in range(NB):
                pool.wait_ge(x_high, b + 1)
                P.tensor_tensor(xl[:, :, b * BLK:(b + 1) * BLK], xnT[:, :, b * BLK:(b + 1) * BLK],
                                xh[:, :, b * BLK:(b + 1) * BLK], ALU.subtract).then_inc(x_low, 1)
            batch_scale(2, 0)
            weights_low(4, 0)
            batch_scale(3, 1)
            weights_low(5, 1)
            keep_top(0, 0)
            with pool.Fori(2, NC2 // 2 - 1) as j:
                for s in range(2):
                    batch_scale(2 * j + s, s)
                    weights_low(2 * j + 2 + s, s)
                    keep_top(2 * j + s - 3, 1 - s)
            batch_scale(NC2 - 2, 0)
            keep_top(NC2 - 5, 1)
            batch_scale(NC2 - 1, 1)
            keep_top(NC2 - 4, 0)
            for c in range(NC2 - 3, NC2):
                keep_top(c, c % 2)
            P.iota(iota32[:], [[1, EC], [0, 128]], base=0, channel_multiplier=0, allow_small_or_imprecise_dtypes=True).then_inc(iota_ready, 1)

            def final_sum(t):
                pool.wait_ge(up_copied, t + 1)
                P.tensor_tensor(hT[:, :, ds(t * 128, 128)], upout[:], hT[:, :, ds(t * 128, 128)], ALU.add).then_inc(sum_ready, 1)

            def low_parts(t, half, first=False):
                pool.wait_ge(a_high, t * 2 + half + 1)
                if half == 0 and not first:
                    pool.wait_ge(up_ready, t - 1)
                tok = slice(half * 64, half * 64 + 64)
                P.tensor_tensor(al[:, ds(t % 2, 1), :, tok].rearrange("p o c t -> p (o c) t"), act_h[:, :, tok],
                                ah[:, ds(t % 2, 1), :, tok].rearrange("p o c t -> p (o c) t"), ALU.subtract).then_inc(a_low, 1)

            def gate_high_digits(t):
                pool.wait_ge(hi_hot, t + 1)
                P.tensor_tensor(gated_hi[:], gated_hi[:], spread(picksT[:, 2, :], 1, EC), ALU.mult).then_inc(gated, 1)

            gate_high_digits(0)
            low_parts(0, 0, first=True)
            low_parts(0, 1, first=True)
            gate_high_digits(1)
            low_parts(1, 0, first=True)
            low_parts(1, 1, first=True)
            gate_high_digits(2)
            final_sum(0)
            with pool.Fori(2, NT - 1) as t:
                low_parts(t, 0)
                low_parts(t, 1)
                gate_high_digits(t + 1)
                final_sum(t - 1)
            low_parts(NT - 1, 0)
            low_parts(NT - 1, 1)
            final_sum(NT - 2)
            final_sum(NT - 1)


def kernel(**inputs):
    import numpy as np
    import concourse.bacc as bacc
    from concourse import mybir
    from concourse.bass_utils import run_bass_kernel_spmd

    f = np.float32
    a = {k: np.asarray(v) for k, v in inputs.items()}
    side = 6
    x = a["x"].reshape(IMAGES, 3, side, 16, side, 16).transpose(1, 3, 5, 0, 2, 4).reshape(KC, 128, TOK)

    def rows(w, chunks):
        return w.reshape(chunks, 128, -1).transpose(1, 0, 2)

    q, k = np.arange(GT)[:, None], np.arange(GT)[None, :]
    rel = (k - q).astype(f)
    hidden = (k > q) | (k < q - 16) | (k // PATCHES != q // PATCHES)
    slopes = (2.0 ** -0.5) ** np.arange(1, HEADS + 1, dtype=f)
    table = np.where(hidden[None], f(-1e30), slopes[:, None, None].astype(f) * rel[None]).astype(f)
    table = table.reshape(REP, KV_HEADS, GT, GT).transpose(2, 1, 0, 3)

    arrays = {
        "x_t": x,
        "tok_w": rows(a["L0_tok_W"].T, KC),
        "tok_b": a["L0_tok_b"].reshape(FC, 128).T,
        "pos": rows(a["L0_tok_pos_embd"].reshape(PATCHES, DIM).T, FC),
        "ident": np.eye(128, dtype=f),
        "bias": table,
        "wq": rows(a["L0_attn_wq"].T, FC),
        "wkv": rows(np.concatenate([a["L0_attn_wk"].T, a["L0_attn_wv"].T], axis=1), FC),
        "wo": rows(a["L0_attn_wo"].T, QC),
        "qw": np.concatenate([a["L0_attn_q_norm_w"]] * 2).reshape(128, 1),
        "kw": np.concatenate([a["L0_attn_k_norm_w"]] * 2).reshape(128, 1),
        "ffn_wq": a["L0_ffn_w_q"].reshape(FC, 128, NC2, KD).transpose(2, 1, 0, 3),
        "gamma": a["L0_ffn_bn_gamma"].reshape(NC2, 128).T,
        "beta": a["L0_ffn_bn_beta"].reshape(NC2, 128).T,
        "keys": a["L0_ffn_keys"].transpose(3, 2, 0, 1).reshape(KD, NC2, KEYS),
        "down": rows(a["L0_ffn_down_embed"].T, FC).reshape(128, FC, WCH, EXPERTS // WCH).transpose(0, 2, 1, 3).reshape(128, WCH, WN),
        "up": rows(a["L0_ffn_up_embed"], EC).reshape(128, WCH, WN),
    }
    arrays = {n: np.ascontiguousarray(v) for n, v in arrays.items()}
    nc = bacc.Bacc("TRN2", target_bir_lowering=False, num_devices=1)
    args = [nc.dram_tensor("in_" + n, v.shape, mybir.dt.from_np(v.dtype), kind="ExternalInput").ap() for n, v in arrays.items()]
    out = nc.dram_tensor("out", (128, FC, TOK), mybir.dt.float32, kind="ExternalOutput").ap()
    vit_block(nc, *args, out)
    r = run_bass_kernel_spmd(nc, [{"in_" + n: v for n, v in arrays.items()}], core_ids=[0])
    return r.results[0]["out"].transpose(2, 1, 0).reshape(IMAGES, PATCHES, DIM)
```
